# Optimizing a Trainium2 kernel written in Bass

```python
import numpy as np
import jax
import jax.numpy as jnp

def _softmax(x, axis=-1):
    return jax.nn.softmax(x, axis=axis)

def _gelu(x):
    return jax.nn.gelu(x, approximate=True)

def _silu(x):
    return jax.nn.silu(x)

def _sigmoid(x):
    return jax.nn.sigmoid(x)

def _layernorm(x, axis=-1, eps=1e-05):
    m = jnp.mean(x, axis=axis, keepdims=True)
    v = jnp.var(x, axis=axis, keepdims=True)
    return (x - m) / jnp.sqrt(v + eps)

def _scatter_add(tgt, idx, src, axis=0):
    return tgt.at[idx].add(src)

def _segment_sum(src, seg, n):
    return jax.ops.segment_sum(src, seg, n)
kernel_name = 'mk_hybrid_d1_jaxref_r8_33935e'

def setup_inputs(seed: int=0):
    np.random.seed(seed)
    _w = jnp.asarray

    def _L0_attn_a_setup():
        import jax, jax.numpy as jnp
        import numpy as np
        B, S, D = (4, 256, 128)
        H = 8
        HD = D // H
        SCALE = 1.0 / np.sqrt(HD)
        key = jax.random.key(seed)
        ks = jax.random.split(key, 9)

        def lin_w(k):
            return jax.random.normal(k, (D, D), dtype=jnp.float32) * (1.0 / np.sqrt(D))
        return {'hidden_states': jax.random.normal(ks[0], (B, S, D), dtype=jnp.float32), 'Wq': lin_w(ks[1]), 'bq': jax.random.normal(ks[2], (D,), dtype=jnp.float32) * 0.02, 'Wk': lin_w(ks[3]), 'bk': jax.random.normal(ks[4], (D,), dtype=jnp.float32) * 0.02, 'Wv': lin_w(ks[5]), 'bv': jax.random.normal(ks[6], (D,), dtype=jnp.float32) * 0.02, 'Wo': lin_w(ks[7]), 'bo': jax.random.normal(ks[8], (D,), dtype=jnp.float32) * 0.02}
    _L0_attn_a_in = _L0_attn_a_setup()

    def _L0_attn_b_setup():
        import jax, jax.numpy as jnp
        import numpy as np
        D_MODEL = 128
        N_HEADS = 64
        D_HEAD = D_MODEL // N_HEADS
        B = 2
        S = 256

        def _xavier(key, fan):
            lim = np.sqrt(6.0 / (2 * fan)).astype(np.float32)
            return jax.random.uniform(key, (fan, fan), dtype=jnp.float32, minval=-lim, maxval=lim)
        key = jax.random.key(seed)
        ks = jax.random.split(key, 9)
        blim = 1.0 / np.sqrt(D_MODEL)

        def bias(k):
            return jax.random.uniform(k, (D_MODEL,), dtype=jnp.float32, minval=-blim, maxval=blim)
        return {'x': jax.random.normal(ks[0], (B, S, D_MODEL), dtype=jnp.float32), 'Wq': _xavier(ks[1], D_MODEL), 'bq': bias(ks[2]), 'Wk': _xavier(ks[3], D_MODEL), 'bk': bias(ks[4]), 'Wv': _xavier(ks[5], D_MODEL), 'bv': bias(ks[6]), 'Wo': _xavier(ks[7], D_MODEL), 'bo': jnp.zeros((D_MODEL,), dtype=jnp.float32), 'beta': jnp.zeros((1,), dtype=jnp.float32)}
    _L0_attn_b_in = _L0_attn_b_setup()

    def _L0_ffn_setup():
        import jax, jax.numpy as jnp
        import numpy as np
        TOP_K = 2
        ROUTED_SCALING = 1.0
        key = jax.random.key(seed)
        k1, k2, k3, k4 = jax.random.split(key, 4)
        S, B, H = (128, 2, 128)
        E, FFN = (8, 176)
        return {'hidden_states': jax.random.normal(k1, (S, B, H), dtype=jnp.float32), 'gate_w': jax.random.normal(k2, (E, H), dtype=jnp.float32) * 0.02, 'w1': jax.random.normal(k3, (E, H, 2 * FFN), dtype=jnp.float32) * 0.02, 'w2': jax.random.normal(k4, (E, FFN, H), dtype=jnp.float32) * 0.02}
    _L0_ffn_in = _L0_ffn_setup()
    _d = {'L0_attn_a_hidden_states': _L0_attn_a_in['hidden_states'], 'L0_attn_a_Wq': _L0_attn_a_in['Wq'], 'L0_attn_a_bq': _L0_attn_a_in['bq'], 'L0_attn_a_Wk': _L0_attn_a_in['Wk'], 'L0_attn_a_bk': _L0_attn_a_in['bk'], 'L0_attn_a_Wv': _L0_attn_a_in['Wv'], 'L0_attn_a_bv': _L0_attn_a_in['bv'], 'L0_attn_a_Wo': _L0_attn_a_in['Wo'], 'L0_attn_a_bo': _L0_attn_a_in['bo'], 'L0_attn_b_Wq': _L0_attn_b_in['Wq'], 'L0_attn_b_bq': _L0_attn_b_in['bq'], 'L0_attn_b_Wk': _L0_attn_b_in['Wk'], 'L0_attn_b_bk': _L0_attn_b_in['bk'], 'L0_attn_b_Wv': _L0_attn_b_in['Wv'], 'L0_attn_b_bv': _L0_attn_b_in['bv'], 'L0_attn_b_Wo': _L0_attn_b_in['Wo'], 'L0_attn_b_bo': _L0_attn_b_in['bo'], 'L0_attn_b_beta': _L0_attn_b_in['beta'], 'L0_ffn_gate_w': _L0_ffn_in['gate_w'], 'L0_ffn_w1': _L0_ffn_in['w1'], 'L0_ffn_w2': _L0_ffn_in['w2']}
    _x0 = _d['L0_attn_a_hidden_states']
    _d['L0_attn_a_hidden_states'] = jax.random.normal(jax.random.fold_in(jax.random.key(seed), 1), (16, 512, 128), dtype=_x0.dtype)
    del _x0
    return _d

def reference(L0_attn_a_hidden_states, L0_attn_a_Wq, L0_attn_a_bq, L0_attn_a_Wk, L0_attn_a_bk, L0_attn_a_Wv, L0_attn_a_bv, L0_attn_a_Wo, L0_attn_a_bo, L0_attn_b_Wq, L0_attn_b_bq, L0_attn_b_Wk, L0_attn_b_bk, L0_attn_b_Wv, L0_attn_b_bv, L0_attn_b_Wo, L0_attn_b_bo, L0_attn_b_beta, L0_ffn_gate_w, L0_ffn_w1, L0_ffn_w2):

    def _L0_attn_a_ref(hidden_states, Wq, bq, Wk, bk, Wv, bv, Wo, bo):
        import jax, jax.numpy as jnp
        import numpy as np
        B, S, D = (4, 256, 128)
        H = 8
        HD = D // H
        SCALE = 1.0 / np.sqrt(HD)
        b, s, _ = hidden_states.shape
        Q = hidden_states @ Wq + bq
        K = hidden_states @ Wk + bk
        V = hidden_states @ Wv + bv
        Q = Q.reshape(b, s, H, HD).transpose(0, 2, 1, 3)
        K = K.reshape(b, s, H, HD).transpose(0, 2, 1, 3)
        V = V.reshape(b, s, H, HD).transpose(0, 2, 1, 3)
        scores = jnp.einsum('bhqd,bhkd->bhqk', Q, K) * SCALE
        attn = jax.nn.softmax(scores, axis=-1)
        out = jnp.einsum('bhqk,bhkd->bhqd', attn, V)
        out = out.transpose(0, 2, 1, 3).reshape(b, s, D)
        return out @ Wo + bo

    def _L0_attn_b_ref(x, Wq, bq, Wk, bk, Wv, bv, Wo, bo, beta):
        import jax, jax.numpy as jnp
        import numpy as np
        D_MODEL = 128
        N_HEADS = 64
        D_HEAD = D_MODEL // N_HEADS
        B = 2
        S = 256

        def _xavier(key, fan):
            lim = np.sqrt(6.0 / (2 * fan)).astype(np.float32)
            return jax.random.uniform(key, (fan, fan), dtype=jnp.float32, minval=-lim, maxval=lim)
        b, s, dm = x.shape
        h, d = (N_HEADS, D_HEAD)

        def heads(y):
            return y.reshape(b, s, h, d).transpose(0, 2, 1, 3).reshape(b * h, s, d)
        q = heads(x @ Wq.T + bq)
        k = heads(x @ Wk.T + bk)
        v = heads(x @ Wv.T + bv)
        be = jnp.exp(beta)
        q = jax.nn.softmax(be * q, axis=-1)
        k = jax.nn.softmax(be * k, axis=-1)
        kv = jnp.cumsum(jnp.einsum('zsD,zsd->zsDd', k, v), axis=1)
        kn = jnp.cumsum(k, axis=1)
        num = jnp.einsum('zsD,zsDd->zsd', q, kv)
        den = jnp.sum(q * kn, axis=-1, keepdims=True)
        out = num / den
        out = out.reshape(b, h, s, d).transpose(0, 2, 1, 3).reshape(b, s, dm)
        return out @ Wo.T + bo

    def _L0_ffn_ref(hidden_states, gate_w, w1, w2):
        import jax, jax.numpy as jnp
        import numpy as np
        TOP_K = 2
        ROUTED_SCALING = 1.0
        x = jnp.transpose(hidden_states, (1, 0, 2))
        B, S, H = x.shape
        E = gate_w.shape[0]
        xt = x.reshape(-1, H)
        T = xt.shape[0]
        scores = jax.nn.softmax(xt @ gate_w.T, axis=-1)
        topk_w, topk_idx = jax.lax.top_k(scores, TOP_K)
        topk_w = topk_w / (jnp.sum(topk_w, axis=-1, keepdims=True) + 1e-20)
        topk_w = topk_w * ROUTED_SCALING
        combine = jnp.zeros((T, E), dtype=xt.dtype)
        combine = combine.at[jnp.arange(T)[:, None], topk_idx].set(topk_w)
        out = jnp.zeros_like(xt)
        for e in range(E):
            h = xt @ w1[e]
            g, u = jnp.split(h, 2, axis=-1)
            y = jax.nn.silu(g) * u @ w2[e]
            out = out + combine[:, e:e + 1] * y
        out = out.reshape(B, S, H)
        return jnp.transpose(out, (1, 0, 2))
    x = L0_attn_a_hidden_states
    x = x + _L0_attn_a_ref(_layernorm(x, axis=-1), L0_attn_a_Wq, L0_attn_a_bq, L0_attn_a_Wk, L0_attn_a_bk, L0_attn_a_Wv, L0_attn_a_bv, L0_attn_a_Wo, L0_attn_a_bo)
    x = x + _L0_ffn_ref(_layernorm(x, axis=-1), L0_ffn_gate_w, L0_ffn_w1, L0_ffn_w2)
    x = x + _L0_attn_b_ref(_layernorm(x, axis=-1), L0_attn_b_Wq, L0_attn_b_bq, L0_attn_b_Wk, L0_attn_b_bk, L0_attn_b_Wv, L0_attn_b_bv, L0_attn_b_Wo, L0_attn_b_bo, L0_attn_b_beta)
    x = x + _L0_ffn_ref(_layernorm(x, axis=-1), L0_ffn_gate_w, L0_ffn_w1, L0_ffn_w2)
    return x

_drawn_inputs = setup_inputs


def setup_inputs(seed=0):
    import zlib

    import numpy as np

    out = dict(_drawn_inputs(seed))
    spreads = {'L0_attn_b_bo': (0.0, 0.1)}
    factors = {'L0_attn_a_bq': 8.0,
     'L0_attn_a_bk': 8.0,
     'L0_attn_b_bq': 8.0,
     'L0_attn_b_bk': 8.0,
     'L0_ffn_gate_w': 7.031,
     'L0_ffn_w1': 6.061,
     'L0_ffn_w2': 6.071}
    for name, (base, spread) in spreads.items():
        noise = np.random.default_rng([zlib.crc32(name.encode()), seed]).standard_normal(out[name].shape)
        drawn = base * np.exp(spread * noise) if base else spread * noise
        out[name] = jnp.asarray(drawn.astype(out[name].dtype))
    for name, factor in factors.items():
        out[name] = (out[name] * factor).astype(out[name].dtype)
    return out
```

```python
from contextlib import ExitStack

import concourse.bass as bass
from concourse import mybir

F32 = mybir.dt.float32
F32R = mybir.dt.float32r
ACT = mybir.ActivationFunctionType
ALU = mybir.AluOpType
AX = mybir.AxisListType

P = 128
SEQS, SEQ, D = 16, 512, 128
CH = SEQ // P
EPS = 1e-5

HEADS = 8
HEAD = D // HEADS

EXPERTS, FFN = 8, 176
TAIL = FFN - P
ODD_TAIL = 64
TAIL_ROWS = ODD_TAIL + TAIL
PAIRS = EXPERTS // 2
UNITS = 3 * PAIRS


def at_least(engine, semaphore, value):
    if isinstance(value, int) and value <= 0:
        return
    engine.wait_ge(semaphore, value)


def three_products(tensor, out, stationary, moving, start=True, stop=True):
    (s_hi, s_lo), (m_hi, m_lo) = stationary, moving
    tensor.matmul(out, s_hi, m_hi, start=start, stop=False)
    tensor.matmul(out, s_hi, m_lo, start=False, stop=False)
    return tensor.matmul(out, s_lo, m_hi, start=False, stop=stop)


def halves(w):
    return w[0][:, :], w[1][:, :]


class Space:

    def __init__(self, nc, ctx, tag):
        self.nc, self.ctx, self.tag = nc, ctx, tag

    def sb(self, name, shape, dt=F32):
        return self.ctx.enter_context(self.nc.sbuf_tensor(f"{self.tag}_{name}", shape, dt))

    def ps(self, name, shape, dt=F32):
        return self.ctx.enter_context(self.nc.psum_tensor(f"{self.tag}_{name}", shape, dt))


class Norm:

    def __init__(self, nc, space, sem, x_all, ident, transposed, in_time_order=False):
        self.in_time_order = in_time_order
        self.nc, self.x_all, self.ident = nc, x_all, ident
        self.stats = space.sb("ln_stats", [P, CH, 6])
        self.moments = space.sb("ln_moments", [P, CH, 2])
        self.shifted = space.sb("ln_shifted", [P, CH])
        self.spare = space.sb("ln_spare", [P, 1])
        self.eps = space.sb("ln_eps", [P, CH])
        self.power = space.sb("ln_power", [P, CH])
        self.rstd = space.sb("ln_rstd", [P, CH])
        self.rows = space.sb("ln_rows", [P, CH, D])
        self.transposed = transposed
        self.hi = [space.sb(f"xn_hi{i}", [P, SEQ], F32R) for i in range(2)]
        self.lo = [space.sb(f"xn_lo{i}", [P, SEQ], F32R) for i in range(2)]
        t = space.tag
        self.stats_done = sem(f"{t}_ln_stats_done")
        self.moments_done = sem(f"{t}_ln_moments_done")
        self.power_set = sem(f"{t}_ln_power_set")
        self.shifted_done = sem(f"{t}_ln_shifted_done")
        self.rstd_done = sem(f"{t}_ln_rstd_done")
        self.rows_done = sem(f"{t}_ln_rows_done")
        self.transposes_done = sem(f"{t}_ln_transposes_done")
        self.hi_done = sem(f"{t}_xn_hi_done")
        self.lo_done = sem(f"{t}_xn_lo_done")

    def halves(self, b_parity):
        return self.hi[b_parity][:, :], self.lo[b_parity][:, :]

    def halves_chunk(self, b_parity, c):
        return (self.hi[b_parity][:, c * P:(c + 1) * P], self.lo[b_parity][:, c * P:(c + 1) * P])

    def gpsimd_setup(self, pool):
        pool.memset(self.eps[:, :], EPS)
        pool.memset(self.power[:, :], -0.5).then_inc(self.power_set, 1)
        pool.wait_ge(self.power_set, 1)

    def vector_statistics(self, dve, b):
        for c in range(CH):
            last = dve.bn_stats(self.stats[:, c, :], self.x_all[:, b, c, :])
        last.then_inc(self.stats_done, 1)
        dve.wait_ge(self.stats_done, b + 1)
        dve.memset(self.spare[:, :], 0.0)
        for c in range(CH):
            last = dve.bn_aggr(self.moments[:, c, :], self.stats[:, c, :])
        last.then_inc(self.moments_done, 1)

    def gpsimd_rstd(self, pool, b):
        pool.wait_ge(self.moments_done, b + 1)
        pool.tensor_tensor(self.shifted[:, :], self.moments[:, :, 1], self.eps[:, :], ALU.add)\
            .then_inc(self.shifted_done, 1)
        pool.wait_ge(self.shifted_done, b + 1)
        pool.tensor_tensor(self.rstd[:, :], self.shifted[:, :], self.power[:, :], ALU.pow)\
            .then_inc(self.rstd_done, 1)

    def vector_rows(self, dve, b):
        dve.wait_ge(self.rstd_done, b + 1)
        for c in range(CH):
            last = dve.tensor_scalar(self.rows[:, c, :], self.x_all[:, b, c, :], self.moments[:, c, 0:1],
                                     self.rstd[:, c:c + 1], ALU.subtract, ALU.mult)
        last.then_inc(self.rows_done, 1)

    def tensor_transposes(self, pe, b):
        pe.wait_ge(self.rows_done, b + 1)
        at_least(pe, self.lo_done, b)
        for c in range(CH):
            last = pe.transpose(self.transposed[:, c * P:(c + 1) * P], self.rows[:, c, :], self.ident[:, :])
        last.then_inc(self.transposes_done, 1)

    def scalar_hi(self, act, b, parity):
        act.wait_ge(self.transposes_done, b + 1)
        act.copy(self.columns(self.hi[parity]), self.read_turned()).then_inc(self.hi_done, 1)

    def vector_lo(self, dve, b, parity):
        dve.wait_ge(self.hi_done, b + 1)
        dve.tensor_tensor(self.columns(self.lo[parity]), self.read_turned(),
                          self.columns(self.hi[parity]).bitcast(F32), ALU.subtract).then_inc(self.lo_done, 1)

    def read_turned(self):
        t = self.transposed[:, :]
        return t.rearrange("d (c p) -> d c p", c=CH) if self.in_time_order else t

    def columns(self, half):
        return half[:, :].rearrange("d (p c) -> d c p", c=CH) if self.in_time_order else half[:, :]


def attention_phase(nc, sem, x_all, ident, wq, wk, wv, wo, a, tag):
    M_ROW, M_END = 3 * HEAD, 3 * HEAD + 2
    ITEMS = HEADS * CH
    FIRST_MAX, QUEUE = 8, 2
    STACK_COUNT, MAX_COUNT = 16 * 7, 16 * 2
    with ExitStack() as ctx:
        space = Space(nc, ctx, tag)
        sb, ps = space.sb, space.ps
        max_ps = [ps(f"max{i}", [P, SEQ]) for i in range(2)]
        score_ps = [ps(f"score{i}", [P, SEQ]) for i in range(2)]
        pv_ps = [ps(f"pv{i}", [P, SEQ]) for i in range(2)]
        work_ps = ps("work", [P, SEQ])
        out_ps = ps("out", [P, CH, D])
        norm = Norm(nc, space, sem, x_all, ident, work_ps)
        bq, bk = sb("bq", [P, 1]), sb("bk", [P, 1])
        bv, bo = sb("bv", [P, D]), sb("bo", [P, D])
        q_stack = [sb(f"q_stack{i}", [P, HEADS, SEQ], F32R) for i in range(2)]
        k_stack = [sb(f"k_stack{i}", [P, HEADS, SEQ], F32R) for i in range(2)]
        zeros = sb("zeros", [2, SEQ])
        q_hi, q_lo, k_hi, k_lo = (sb(n, [P, SEQ], F32R) for n in ("q_hi", "q_lo", "k_hi", "k_lo"))
        v_rows = sb("v_rows", [P, CH, HEADS, HEAD])
        v_ones = [sb(f"v_ones{i}", [P, CH, HEADS, 32]) for i in range(2)]
        neg_max = sb("neg_max", [P, HEADS, CH])
        m_hi, m_lo = sb("m_hi", [ITEMS, P], F32R), sb("m_lo", [ITEMS, P], F32R)
        probs = [sb(f"probs{i}", [P, SEQ]) for i in range(4)]
        pv = [sb(f"pv_sb{i}", [P, SEQ]) for i in range(2)]
        rsum = sb("rsum", [P, CH, 4])
        o_rows = sb("o_rows", [P, CH, D])
        o_hi, o_lo = sb("o_hi", [P, SEQ], F32R), sb("o_lo", [P, SEQ], F32R)
        spare = sb("pool_spare", [P, 1])

        names = ("consts_loaded", "consts_set", "q_proj", "k_proj", "v_proj", "q_hi_done", "q_lo_done",
                 "k_hi_done", "k_lo_done", "v_rows_done", "v_ones_done", "stack_loaded0", "stack_loaded1", "max_scores",
                 "max_done", "max_turned", "m_hi_done", "m_lo_done", "m_loaded", "scores", "exp_done",
                 "pv_done", "pv_copied", "o_turned", "rsum_done", "o_rows_done", "o_back", "o_hi_done",
                 "o_lo_done", "y_done", "bo_added", "x_done")
        (consts_loaded, consts_set, q_proj, k_proj, v_proj, q_hi_done, q_lo_done, k_hi_done, k_lo_done,
         v_rows_done, v_ones_done, stack_loaded0, stack_loaded1, max_scores, max_done, max_turned, m_hi_done, m_lo_done,
         m_loaded, scores, exp_done, pv_done, pv_copied, o_turned, rsum_done, o_rows_done, o_back,
         o_hi_done, o_lo_done, y_done, bo_added, x_done) = (sem(f"{tag}_{n}") for n in names)
        CONSTS = 4 * 16
        stack_loaded = (stack_loaded0, stack_loaded1)

        def stacked(turn, q):
            return STACK_COUNT * (turn + 1)

        def item(i):
            return i // 16 * 4 + i % 4, i % 16 // 4

        def run(body, engine):
            body(0, 0, 0, False, True, True)
            body(1, 1, 0, True, True, True)
            with engine.Fori(1, SEQS // 2 - 1) as turn:
                body(2 * turn, 0, turn, True, True, True)
                body(2 * turn + 1, 1, turn, True, True, True)
            body(SEQS - 2, 0, SEQS // 2 - 1, True, True, False)
            body(SEQS - 1, 1, SEQS // 2 - 1, True, False, False)

        block = ctx.enter_context(nc.Block())

        @block.sync
        def _(sp):
            sp.dma_start(bq[:, :], a["a_bq"]).then_inc(consts_loaded, 16)
            sp.dma_start(bk[:, :], a["a_bk"]).then_inc(consts_loaded, 16)
            sp.dma_start(bv[:, :], a["a_bv"].partition_broadcast(P)).then_inc(consts_loaded, 16)
            sp.dma_start(bo[:, :], a["a_bo"].partition_broadcast(P)).then_inc(consts_loaded, 16)

            def stack(b, q):
                at_least(sp, scores, ITEMS * (b - 1))
                sp.dma_start(q_stack[q][M_ROW:M_END, :, :].bitcast(F32),
                             zeros[:, :].unsqueeze(1).to_broadcast([2, HEADS, SEQ]))\
                    .then_inc(stack_loaded[q], 16)
                sp.wait_ge(q_lo_done, b + 1)
                for row, half in ((0, q_hi), (HEAD, q_lo), (2 * HEAD, q_hi)):
                    sp.dma_start(rows_of_stack(q_stack[q], row), half[:, :].bitcast(F32)).then_inc(stack_loaded[q], 16)
                sp.wait_ge(k_lo_done, b + 1)
                for row, half in ((0, k_hi), (HEAD, k_hi), (2 * HEAD, k_lo)):
                    sp.dma_start(rows_of_stack(k_stack[q], row), half[:, :].bitcast(F32)).then_inc(stack_loaded[q], 16)

            def rows_of_stack(t, row):
                return t[row:row + HEAD, :, :].bitcast(F32)

            def maxima(b, q):
                sp.wait_ge(m_lo_done, b + 1)
                for row, half in ((M_ROW, m_hi), (M_ROW + 1, m_lo)):
                    sp.dma_start(q_stack[q][row:row + 1, :, :].bitcast(F32).rearrange("r h (c t) -> r (h c) t", c=CH),
                                 half[:, :].bitcast(F32)).then_inc(m_loaded, 16)

            def body(b, q, turn, before, after1, after2):
                if after1:
                    maxima(b + 1, 1 - q)
                if after2:
                    stack(b + 2, q)

            sp.wait_ge(consts_set, 1)
            stack(0, 0)
            stack(1, 1)
            maxima(0, 0)
            run(body, sp)

        @block.tensor
        def _(pe):
            def project(b, q, part):
                if part == 0:
                    at_least(pe, v_rows_done, b)
                    at_least(pe, m_lo_done, b - 1)
                    norm.tensor_transposes(pe, b)
                if part == 1:
                    pe.wait_ge(norm.lo_done, b + 1)
                    three_products(pe, work_ps[:, :], halves(wq), norm.halves(q)).then_inc(q_proj, 1)
                if part == 2:
                    pe.wait_ge(q_lo_done, b + 1)
                    three_products(pe, work_ps[:, :], halves(wk), norm.halves(q)).then_inc(k_proj, 1)
                if part == 3:
                    pe.wait_ge(k_lo_done, b + 1)
                    for c in range(CH):
                        last = three_products(pe, work_ps[:, c * P:(c + 1) * P], norm.halves_chunk(q, c), halves(wv))
                    last.then_inc(v_proj, 1)

            def largest(b, q, turn, j):
                h, c = j // CH, j % CH
                if j == 0:
                    pe.wait_ge(stack_loaded[q], stacked(turn, q))
                at_least(pe, max_done, b * ITEMS + j - 1)
                pe.matmul(max_ps[j % 2][:, :], q_stack[q][:, h, c * P:(c + 1) * P], k_stack[q][:, h, :],
                          start=True, stop=True).then_inc(max_scores, 1)

            def turn_max(b, projected):
                pe.wait_ge(max_done, ITEMS * (b + 1))
                pe.wait_ge(v_rows_done, projected)
                pe.transpose(work_ps[0:ITEMS, 0:P], neg_max[:, :, :].rearrange("p h c -> p (h c)"), ident[:, :])\
                    .then_inc(max_turned, 1)

            def score(b, q, i):
                h, c = item(i)
                if i == 0:
                    pe.wait_ge(m_loaded, MAX_COUNT * (b + 1))
                at_least(pe, exp_done, b * ITEMS + i - 1)
                pe.matmul(score_ps[i % 2][:, :], k_stack[q][:, h, c * P:(c + 1) * P], q_stack[q][:, h, :],
                          start=True, stop=True).then_inc(scores, 1)

            def weigh(b, q, i):
                h, c = item(i)
                group, side = h // 4, h % 4
                if i == 0:
                    pe.wait_ge(v_ones_done, b + 1)
                if c == 0:
                    at_least(pe, pv_copied, 2 * (b - 1) + group + 1)
                pe.wait_ge(exp_done, b * ITEMS + i + 1)
                pe.matmul(pv_ps[group][32 * side:32 * side + 32, :], v_ones[q][:, c, h, :], probs[i % 4][:, :],
                          start=(c == 0), stop=(c == CH - 1)).then_inc(pv_done, 1)

            def turn_out(b, group):
                pe.wait_ge(pv_copied, 2 * b + group + 1)
                if group:
                    pe.wait_ge(o_rows_done, 2 * b + 1)
                else:
                    at_least(pe, x_done, b)
                for c in range(CH):
                    last = pe.transpose(out_ps[:, c, :], pv[group][:, c * P:(c + 1) * P], ident[:, :])
                last.then_inc(o_turned, 1)

            def turn_back(b):
                pe.wait_ge(o_rows_done, 2 * b + 2)
                for c in range(CH):
                    last = pe.transpose(out_ps[:, c, :], o_rows[:, c, :], ident[:, :])
                last.then_inc(o_back, 1)

            def project_out(b):
                pe.wait_ge(o_lo_done, b + 1)
                for c in range(CH):
                    t = slice(c * P, (c + 1) * P)
                    last = three_products(pe, out_ps[:, c, :], (o_hi[:, t], o_lo[:, t]), halves(wo))
                last.then_inc(y_done, 1)

            def body(b, q, turn, before, after1, after2):
                for i in range(ITEMS):
                    score(b, q, i)
                    if i >= QUEUE:
                        weigh(b, q, i - QUEUE)
                    if before:
                        if i == 2:
                            turn_out(b - 1, 1)
                        if i == 5:
                            turn_back(b - 1)
                        if i == 9:
                            project_out(b - 1)
                    if after1 and FIRST_MAX <= i < FIRST_MAX + ITEMS // 2:
                        largest(b + 1, 1 - q, turn + q, 2 * (i - FIRST_MAX))
                        largest(b + 1, 1 - q, turn + q, 2 * (i - FIRST_MAX) + 1)
                    if after2 and i in (12, 16, 20, 25):
                        project(b + 2, q, (12, 16, 20, 25).index(i))
                    if i == 22:
                        turn_out(b, 0)
                    if after1 and i == 29:
                        turn_max(b + 1, b + 3 if after2 else SEQS)
                for i in range(ITEMS - QUEUE, ITEMS):
                    weigh(b, q, i)

            pe.wait_ge(consts_set, 1)
            for part in range(4):
                project(0, 0, part)
            for part in range(4):
                project(1, 1, part)
            for j in range(ITEMS):
                largest(0, 0, 0, j)
            turn_max(0, 2)
            run(body, pe)
            turn_out(SEQS - 1, 1)
            turn_back(SEQS - 1)
            project_out(SEQS - 1)

        @block.scalar
        def _(act):
            def project(b, q, turn, part):
                if part == 0:
                    norm.scalar_hi(act, b, q)
                if part == 1:
                    act.wait_ge(q_proj, b + 1)
                    at_least(act, stack_loaded[1 - q], STACK_COUNT * (turn + q))
                    act.activation(q_hi[:, :], work_ps[:, :], ACT.Identity, bias=bq[:, :]).then_inc(q_hi_done, 1)
                if part == 2:
                    act.wait_ge(k_proj, b + 1)
                    act.activation(k_hi[:, :], work_ps[:, :], ACT.Identity, bias=bk[:, :]).then_inc(k_hi_done, 1)

                if part == 3:
                    act.wait_ge(v_proj, b + 1)
                    at_least(act, v_ones_done, b)
                    act.copy(v_rows[:, :, :, :].rearrange("p c h d -> p (c h d)"), work_ps[:, :])\
                        .then_inc(v_rows_done, 1)

            def round_max(b):
                act.wait_ge(max_turned, b + 1)
                at_least(act, m_loaded, MAX_COUNT * b)
                act.copy(m_hi[:, :], work_ps[0:ITEMS, 0:P]).then_inc(m_hi_done, 1)

            def exponential(b, i):
                n = b * ITEMS + i
                act.wait_ge(scores, n + 1)
                at_least(act, pv_done, n - 3)
                act.activation(probs[i % 4][:, :], score_ps[i % 2][:, :], ACT.Exp, scale=HEAD ** -0.5)\
                    .then_inc(exp_done, 1)

            def copy_pv(b, group):
                act.wait_ge(pv_done, b * ITEMS + 16 * (group + 1))
                at_least(act, o_turned, 2 * (b - 1) + group + 1)
                act.copy(pv[group][:, :], pv_ps[group][:, :]).then_inc(pv_copied, 1)

            def out_hi(b):
                act.wait_ge(o_back, b + 1)
                act.copy(o_hi[:, :], out_ps[:, :, :].rearrange("p c d -> p (c d)")).then_inc(o_hi_done, 1)

            def body(b, q, turn, before, after1, after2):
                for i in range(ITEMS):
                    exponential(b, i)
                    if before:
                        if i == 1:
                            copy_pv(b - 1, 1)
                        if i == 7:
                            out_hi(b - 1)
                    if after2 and i in (13, 17, 21, 26):
                        project(b + 2, q, turn + 1, (13, 17, 21, 26).index(i))
                    if i == 19:
                        copy_pv(b, 0)
                    if after1 and i == 30:
                        round_max(b + 1)

            act.wait_ge(consts_set, 1)
            act.wait_ge(consts_loaded, CONSTS)
            for b in range(2):
                for part in range(4):
                    project(b, b, 0, part)
            round_max(0)
            run(body, act)
            copy_pv(SEQS - 1, 1)
            out_hi(SEQS - 1)

        @block.vector
        def _(dve):
            def project(b, q, part):
                if part == 0:
                    norm.vector_statistics(dve, b)
                if part == 1:
                    norm.vector_rows(dve, b)
                if part == 2:
                    norm.vector_lo(dve, b, q)
                if part == 3:
                    dve.wait_ge(q_hi_done, b + 1)
                    dve.scalar_tensor_tensor(q_lo[:, :], work_ps[:, :], bq[:, :], q_hi[:, :].bitcast(F32),
                                             ALU.add, ALU.subtract).then_inc(q_lo_done, 1)
                if part == 4:
                    dve.wait_ge(k_hi_done, b + 1)
                    dve.scalar_tensor_tensor(k_lo[:, :], work_ps[:, :], bk[:, :], k_hi[:, :].bitcast(F32),
                                             ALU.add, ALU.subtract).then_inc(k_lo_done, 1)
            def find_max(b, j):
                h, c = j // CH, j % CH
                dve.wait_ge(max_scores, b * ITEMS + j + 1)
                dve.tensor_reduce(neg_max[:, h, c:c + 1], max_ps[j % 2][:, :], AX.X, ALU.max, negate=True)\
                    .then_inc(max_done, 1)

            def max_lo(b):
                dve.wait_ge(m_hi_done, b + 1)
                dve.tensor_tensor(m_lo[:, :], work_ps[0:ITEMS, 0:P], m_hi[:, :].bitcast(F32), ALU.subtract)\
                    .then_inc(m_lo_done, 1)

            def normalise(b, group):
                n = 2 * b + group
                dve.wait_ge(o_turned, n + 1)
                heads = out_ps[:, :, :].rearrange("p c (h r) -> p c h r", r=32)
                dve.reciprocal(rsum[:, :, :], heads[:, :, :, 0]).then_inc(rsum_done, 1)
                dve.wait_ge(rsum_done, n + 1)
                half = o_rows[:, :, group * 64:group * 64 + 64].rearrange("p c (h d) -> p c h d", d=HEAD)
                dve.tensor_tensor(half, heads[:, :, :, 1:HEAD + 1],
                                  rsum[:, :, :].unsqueeze(3).to_broadcast([P, CH, 4, HEAD]), ALU.mult)\
                    .then_inc(o_rows_done, 1)

            def out_lo(b):
                dve.wait_ge(o_hi_done, b + 1)
                dve.tensor_tensor(o_lo[:, :], out_ps[:, :, :].rearrange("p c d -> p (c d)"),
                                  o_hi[:, :].bitcast(F32), ALU.subtract).then_inc(o_lo_done, 1)

            def add_out(b):
                dve.wait_ge(bo_added, b + 1)
                dve.wait_ge(y_done, b + 1)
                dve.tensor_tensor(x_all[:, b, :, :], x_all[:, b, :, :], out_ps[:, :, :], ALU.add)\
                    .then_inc(x_done, 1)

            def body(b, q, turn, before, after1, after2):
                for i in range(ITEMS):
                    if before:
                        if i == 3:
                            normalise(b - 1, 1)
                        if i == 7:
                            out_lo(b - 1)
                        if i == 10:
                            add_out(b - 1)
                    if after2:
                        if i in (4, 8, 14, 18, 22):
                            project(b + 2, q, (4, 8, 14, 18, 22).index(i))
                    if after1 and FIRST_MAX <= i < FIRST_MAX + ITEMS // 2:
                        find_max(b + 1, 2 * (i - FIRST_MAX))
                        find_max(b + 1, 2 * (i - FIRST_MAX) + 1)
                    if i == 23:
                        normalise(b, 0)
                    if after1 and i == 31:
                        max_lo(b + 1)

            for q in range(2):
                dve.memset(k_stack[q][:, :, :].bitcast(F32), 1.0)
                dve.memset(q_stack[q][:, :, :].bitcast(F32), 0.0)
                dve.memset(v_ones[q][:, :, :, 0:1], 1.0)
                dve.memset(v_ones[q][:, :, :, 1:32], 0.0)
            dve.memset(zeros[:, :], 0.0).then_inc(consts_set, 1)
            dve.wait_ge(consts_loaded, CONSTS)
            for b in range(2):
                for part in range(5):
                    project(b, b, part)
            for j in range(ITEMS):
                find_max(0, j)
            max_lo(0)
            run(body, dve)
            normalise(SEQS - 1, 1)
            out_lo(SEQS - 1)
            add_out(SEQS - 1)

        @block.gpsimd
        def _(pool):
            def copy_v(b, q):
                pool.wait_ge(v_rows_done, b + 1)
                at_least(pool, pv_done, ITEMS * (b - 1))
                pool.tensor_tensor(v_ones[q][:, :, :, 1:HEAD + 1], v_rows[:, :, :, :],
                                   bv[:, :].rearrange("p (h d) -> p h d", d=HEAD).unsqueeze(1)
                                   .to_broadcast([P, CH, HEADS, HEAD]), ALU.add).then_inc(v_ones_done, 1)

            def add_bias(b):
                pool.wait_ge(norm.rows_done, b + 1)
                pool.tensor_tensor(spare[:, :], norm.eps[:, 0:1], norm.eps[:, 0:1], ALU.add)
                pool.tensor_tensor(x_all[:, b, :, :], x_all[:, b, :, :],
                                   bo[:, :].unsqueeze(1).to_broadcast([P, CH, D]), ALU.add).then_inc(bo_added, 1)

            def body(b, q, turn, before, after1, after2):
                if after1:
                    copy_v(b + 1, 1 - q)
                if after2:
                    norm.gpsimd_rstd(pool, b + 2)
                    add_bias(b + 2)

            norm.gpsimd_setup(pool)
            pool.wait_ge(consts_set, 1)
            pool.wait_ge(consts_loaded, CONSTS)
            norm.gpsimd_rstd(pool, 0)
            add_bias(0)
            copy_v(0, 0)
            norm.gpsimd_rstd(pool, 1)
            add_bias(1)
            run(body, pool)


def ffn_phase(nc, sem, x_all, ident, gate, up, down, tag):
    gate_hi, gate_lo = gate
    (up_hi, up_lo), (upt_hi, upt_lo) = up
    (dn_hi, dn_lo), (dnt_hi, dnt_lo) = down
    with ExitStack() as ctx:
        space = Space(nc, ctx, tag)
        hidden_ps = [space.ps(f"hidden{i}", [P, 2, SEQ]) for i in range(2)]
        y_ps = [space.ps(f"y{i}", [P, CH, D]) for i in range(2)]
        norm_ps = space.ps("norm", [P, SEQ])
        logits_ps = space.ps("logits", [P, CH, EXPERTS])
        norm = Norm(nc, space, sem, x_all, ident, norm_ps)
        pool_spare = space.sb("pool_spare", [P, 1])
        silu = [space.sb(f"silu{i}", [P, SEQ]) for i in range(2)]
        act_f = [space.sb(f"act{i}", [P, SEQ]) for i in range(2)]
        act_hi = [space.sb(f"act_hi{i}", [P, SEQ], F32R) for i in range(6)]
        act_lo = [space.sb(f"act_lo{i}", [P, SEQ], F32R) for i in range(6)]
        weighted = [space.sb(f"weighted{i}", [P, CH, D]) for i in range(2)]
        combine = [space.sb(f"combine{i}", [P, CH, EXPERTS]) for i in range(2)]
        r = {n: space.sb(f"r_{n}", [P, CH, EXPERTS]) for n in
             ("logits", "shifted", "exp", "prob", "eq1", "key1", "mask1", "rest", "eq2", "key2", "mask2",
              "both", "chosen")}
        s = {n: space.sb(f"s_{n}", [P, CH]) for n in
             ("max", "sum", "rsum", "top1", "first1", "top2", "first2", "den", "rden")}
        rank = space.sb("rank", [P, EXPERTS])

        up_done = sem(f"{tag}_up_done")
        silu_done = sem(f"{tag}_silu_done")
        act_done = sem(f"{tag}_act_done")
        act_hi_done = sem(f"{tag}_act_hi_done")
        act_lo_done = sem(f"{tag}_act_lo_done")
        y_done = sem(f"{tag}_y_done")
        weighted_done = sem(f"{tag}_weighted_done")
        added = sem(f"{tag}_added")
        logits_done = sem(f"{tag}_logits_done")
        shifted_done = sem(f"{tag}_shifted_done")
        exp_done = sem(f"{tag}_exp_done")
        combine_done = sem(f"{tag}_combine_done")
        route = sem(f"{tag}_route_step")
        rank_set = sem(f"{tag}_rank_set")
        ROUTE_STEPS = 17

        def rows_of(u):
            return TAIL_ROWS if u % 3 == 2 else P

        block = ctx.enter_context(nc.Block())

        @block.tensor
        def _(pe):
            def logits(b, q):
                pe.wait_ge(norm.lo_done, b + 1)
                at_least(pe, shifted_done, b)
                for c in range(CH):
                    last = three_products(pe, logits_ps[:, c, :], norm.halves_chunk(q, c),
                                          (gate_hi[:, :], gate_lo[:, :]))
                last.then_inc(logits_done, 1)

            def up_unit(b, q, u):
                pair, kind = u // 3, u % 3
                at_least(pe, act_done, b * UNITS + u - 1)
                if u == 0:
                    pe.wait_ge(norm.lo_done, b + 1)
                for half in range(2):
                    if kind < 2:
                        w = (up_hi[:, 2 * pair + kind, half, :], up_lo[:, 2 * pair + kind, half, :])
                    else:
                        w = (upt_hi[:, pair, half, :], upt_lo[:, pair, half, :])
                    last = three_products(pe, hidden_ps[u % 2][0:rows_of(u), half, :], w, norm.halves(q))
                last.then_inc(up_done, 1)

            def down_expert(b, e):
                pair = e // 2
                pe.wait_ge(act_lo_done, b * UNITS + 3 * pair + 3)
                at_least(pe, weighted_done, b * EXPERTS + e - 1)
                main, tail = (pair % 2) * 3 + e % 2, (pair % 2) * 3 + 2
                for c in range(CH):
                    t = slice(c * P, (c + 1) * P)
                    three_products(pe, y_ps[e % 2][:, c, :], (act_hi[main][:, t], act_lo[main][:, t]),
                                   (dn_hi[:, e, :], dn_lo[:, e, :]), stop=False)
                    last = three_products(pe, y_ps[e % 2][:, c, :],
                                          (act_hi[tail][0:TAIL_ROWS, t], act_lo[tail][0:TAIL_ROWS, t]),
                                          (dnt_hi[:, e, :], dnt_lo[:, e, :]), start=False)
                last.then_inc(y_done, 1)

            def sequence(b, q, first, final):
                for pair in range(PAIRS):
                    up_unit(b, q, 3 * pair)
                    if pair:
                        down_expert(b, 2 * pair - 2)
                    elif not first:
                        down_expert(b - 1, EXPERTS - 2)
                    up_unit(b, q, 3 * pair + 1)
                    if pair:
                        down_expert(b, 2 * pair - 1)
                    elif not first:
                        down_expert(b - 1, EXPERTS - 1)
                    up_unit(b, q, 3 * pair + 2)
                    if pair == 2 and not final:
                        norm.tensor_transposes(pe, b + 1)
                    if pair == 3 and not final:
                        logits(b + 1, 1 - q)

            norm.tensor_transposes(pe, 0)
            logits(0, 0)
            sequence(0, 0, True, False)
            sequence(1, 1, False, False)
            with pe.Fori(1, SEQS // 2 - 1) as i:
                sequence(2 * i, 0, False, False)
                sequence(2 * i + 1, 1, False, False)
            sequence(SEQS - 2, 0, False, False)
            sequence(SEQS - 1, 1, False, True)
            down_expert(SEQS - 1, EXPERTS - 2)
            down_expert(SEQS - 1, EXPERTS - 1)

        @block.scalar
        def _(act):
            def silu_unit(b, u):
                n = b * UNITS + u
                act.wait_ge(up_done, n + 1)
                at_least(act, act_done, n - 1)
                rows = rows_of(u)
                act.activation(silu[u % 2][0:rows, :], hidden_ps[u % 2][0:rows, 0, :], ACT.Silu)\
                    .then_inc(silu_done, 1)

            def round_unit(b, u):
                n = b * UNITS + u
                pair = u // 3
                act.wait_ge(act_done, n + 1)
                at_least(act, y_done, b * EXPERTS + 2 * (pair - 2) + 2)
                rows = rows_of(u)
                slot = (pair % 2) * 3 + u % 3
                act.copy(act_hi[slot][0:rows, :], act_f[u % 2][0:rows, :]).then_inc(act_hi_done, 1)

            def exponentials(b):
                act.wait_ge(shifted_done, b + 1)
                at_least(act, combine_done, b)
                act.activation(r["exp"][:, :, :], r["shifted"][:, :, :], ACT.Exp).then_inc(exp_done, 1)

            def sequence(b, q, first, final):
                for u in range(UNITS):
                    silu_unit(b, u)
                    if u:
                        round_unit(b, u - 1)
                    elif not first:
                        round_unit(b - 1, UNITS - 1)
                    if u == 8 and not final:
                        norm.scalar_hi(act, b + 1, 1 - q)
                    if u == 11 and not final:
                        exponentials(b + 1)

            norm.scalar_hi(act, 0, 0)
            exponentials(0)
            sequence(0, 0, True, False)
            sequence(1, 1, False, False)
            with act.Fori(1, SEQS // 2 - 1) as i:
                sequence(2 * i, 0, False, False)
                sequence(2 * i + 1, 1, False, False)
            sequence(SEQS - 2, 0, False, False)
            sequence(SEQS - 1, 1, False, True)
            round_unit(SEQS - 1, UNITS - 1)

        @block.vector
        def _(dve):
            def route_a(b):
                dve.wait_ge(logits_done, b + 1)
                dve.tensor_copy(r["logits"][:, :, :], logits_ps[:, :, :]).then_inc(route, 1)
                dve.wait_ge(route, b * ROUTE_STEPS + 1)
                dve.tensor_reduce(s["max"][:, :], r["logits"][:, :, :], AX.X, ALU.max).then_inc(route, 1)
                dve.wait_ge(route, b * ROUTE_STEPS + 2)
                dve.tensor_tensor(r["shifted"][:, :, :], r["logits"][:, :, :], per_expert(s["max"]),
                                  ALU.subtract).then_inc(shifted_done, 1)

            def per_expert(t):
                return t[:, :].unsqueeze(2).to_broadcast([P, CH, EXPERTS])

            def route_b(b, q):
                step = [2]

                def then(instruction):
                    instruction.then_inc(route, 1)
                    step[0] += 1
                    dve.wait_ge(route, b * ROUTE_STEPS + step[0])

                dve.wait_ge(exp_done, b + 1)
                then(dve.tensor_reduce(s["sum"][:, :], r["exp"][:, :, :], AX.X, ALU.add))
                then(dve.reciprocal(s["rsum"][:, :], s["sum"][:, :]))
                then(dve.tensor_tensor(r["prob"][:, :, :], r["exp"][:, :, :], per_expert(s["rsum"]), ALU.mult))
                ranks = rank[:, :].unsqueeze(1).to_broadcast([P, CH, EXPERTS])
                for of, top, eq, key, first, mask in ((r["prob"], s["top1"], r["eq1"], r["key1"], s["first1"], r["mask1"]),
                                                      (r["rest"], s["top2"], r["eq2"], r["key2"], s["first2"], r["mask2"])):
                    then(dve.tensor_reduce(top[:, :], of[:, :, :], AX.X, ALU.max))
                    then(dve.tensor_tensor(eq[:, :, :], of[:, :, :], per_expert(top), ALU.is_equal))
                    then(dve.tensor_tensor(key[:, :, :], eq[:, :, :], ranks, ALU.mult))
                    then(dve.tensor_reduce(first[:, :], key[:, :, :], AX.X, ALU.max))
                    then(dve.tensor_tensor(mask[:, :, :], key[:, :, :], per_expert(first), ALU.is_equal))
                    if mask is r["mask1"]:
                        then(dve.scalar_tensor_tensor(r["rest"][:, :, :], mask[:, :, :], -2.0, of[:, :, :],
                                                      ALU.mult, ALU.add))
                dve.tensor_tensor(r["both"][:, :, :], r["mask1"][:, :, :], r["mask2"][:, :, :], ALU.add)
                dve.scalar_tensor_tensor(s["den"][:, :], s["top1"][:, :], 1e-20, s["top2"][:, :],
                                         ALU.add, ALU.add).then_inc(route, 1)
                dve.wait_ge(route, b * ROUTE_STEPS + 17)
                dve.reciprocal(s["rden"][:, :], s["den"][:, :])
                dve.tensor_tensor(r["chosen"][:, :, :], r["both"][:, :, :], r["prob"][:, :, :], ALU.mult)\
                    .then_inc(combine_done, 1)
                dve.wait_ge(combine_done, 2 * b + 1)
                dve.tensor_tensor(combine[q][:, :, :], r["chosen"][:, :, :], per_expert(s["rden"]), ALU.mult)\
                    .then_inc(combine_done, 1)

            def product_unit(b, u):
                n = b * UNITS + u
                dve.wait_ge(silu_done, n + 1)
                at_least(dve, act_lo_done, n - 1)
                rows = rows_of(u)
                dve.tensor_tensor(act_f[u % 2][0:rows, :], silu[u % 2][0:rows, :],
                                  hidden_ps[u % 2][0:rows, 1, :], ALU.mult).then_inc(act_done, 1)

            def lo_unit(b, u):
                n = b * UNITS + u
                dve.wait_ge(act_hi_done, n + 1)
                rows = rows_of(u)
                slot = (u // 3 % 2) * 3 + u % 3
                dve.tensor_tensor(act_lo[slot][0:rows, :], act_f[u % 2][0:rows, :],
                                  act_hi[slot][0:rows, :].bitcast(F32), ALU.subtract).then_inc(act_lo_done, 1)

            def weigh(b, q, e):
                n = b * EXPERTS + e
                dve.wait_ge(y_done, n + 1)
                at_least(dve, added, n - 1)
                if e == 0:
                    dve.wait_ge(combine_done, 2 * b + 2)
                dve.tensor_tensor(weighted[e % 2][:, :, :], y_ps[e % 2][:, :, :],
                                  combine[q][:, :, e].unsqueeze(2).to_broadcast([P, CH, D]), ALU.mult)\
                    .then_inc(weighted_done, 1)

            def sequence(b, q, first, final):
                for u in range(UNITS):
                    product_unit(b, u)
                    if u:
                        lo_unit(b, u - 1)
                    elif not first:
                        lo_unit(b - 1, UNITS - 1)
                    pair, kind = u // 3, u % 3
                    if kind > 0:
                        e = 2 * pair + kind - 3
                        if pair:
                            weigh(b, q, e)
                        elif not first:
                            weigh(b - 1, 1 - q, EXPERTS + e)
                    if final:
                        continue
                    if u == 3:
                        norm.vector_statistics(dve, b + 1)
                    if u == 5:
                        norm.vector_rows(dve, b + 1)
                    if u == 8:
                        norm.vector_lo(dve, b + 1, 1 - q)
                    if u == 11:
                        route_a(b + 1)
                        route_b(b + 1, 1 - q)

            for e in range(EXPERTS):
                last = dve.memset(rank[:, e:e + 1], float(EXPERTS - e))
            last.then_inc(rank_set, 1)
            dve.wait_ge(rank_set, 1)
            norm.vector_statistics(dve, 0)
            norm.vector_rows(dve, 0)
            norm.vector_lo(dve, 0, 0)
            route_a(0)
            route_b(0, 0)
            sequence(0, 0, True, False)
            sequence(1, 1, False, False)
            with dve.Fori(1, SEQS // 2 - 1) as i:
                sequence(2 * i, 0, False, False)
                sequence(2 * i + 1, 1, False, False)
            sequence(SEQS - 2, 0, False, False)
            sequence(SEQS - 1, 1, False, True)
            lo_unit(SEQS - 1, UNITS - 1)
            weigh(SEQS - 1, 1, EXPERTS - 2)
            weigh(SEQS - 1, 1, EXPERTS - 1)

        @block.gpsimd
        def _(pool):
            def add_expert(b, e):
                n = b * EXPERTS + e
                at_least(pool, added, n)
                pool.wait_ge(weighted_done, n + 1)
                pool.tensor_tensor(pool_spare[:, :], norm.eps[:, 0:1], norm.eps[:, 0:1], ALU.add)
                pool.tensor_tensor(x_all[:, b, :, :], x_all[:, b, :, :], weighted[e % 2][:, :, :], ALU.add)\
                    .then_inc(added, 1)

            norm.gpsimd_setup(pool)
            norm.gpsimd_rstd(pool, 0)

            def sequence(b, final):
                for e in range(2):
                    add_expert(b, e)
                if not final:
                    norm.gpsimd_rstd(pool, b + 1)
                for e in range(2, EXPERTS):
                    add_expert(b, e)

            sequence(0, False)
            with pool.Fori(1, SEQS - 1) as b:
                sequence(b, False)
            sequence(SEQS - 1, True)


def linear_phase(nc, sem, x_all, ident, wq, wk, wv, wo, a, scalars, tag):
    with ExitStack() as ctx:
        space = Space(nc, ctx, tag)
        sb, ps = space.sb, space.ps
        work_ps = ps("work", [P, SEQ])
        q_ps = [ps(f"q{i}", [P, SEQ]) for i in range(2)]
        k_ps = [ps(f"k{i}", [P, SEQ]) for i in range(2)]
        v_ps = [ps(f"v{i}", [P, SEQ]) for i in range(2)]
        out_ps = ps("out", [P, CH, D])
        norm = Norm(nc, space, sem, x_all, ident, work_ps, in_time_order=True)
        bv, bo = sb("bv", [P, 1]), sb("bo", [P, D])
        q = [[sb(f"q{f}_{i}", [P, SEQ]) for i in range(2)] for f in range(2)]
        k = [[sb(f"k{f}_{i}", [P, SEQ]) for i in range(2)] for f in range(2)]
        kv = [sb(f"kv{f}", [P, SEQ]) for f in range(2)]
        kv_sum = [sb(f"kv_sum{f}", [P, SEQ]) for f in range(2)]
        k_sum = [sb(f"k_sum{f}", [P, SEQ]) for f in range(2)]
        num = [sb(f"num{f}", [P, SEQ]) for f in range(2)]
        den = [sb(f"den{f}", [P, SEQ]) for f in range(2)]
        num_all, den_all, rden, o = (sb(n, [P, SEQ]) for n in ("num", "den", "rden", "o"))
        ones = sb("ones", [P, SEQ])
        o_hi, o_lo = sb("o_hi", [P, SEQ], F32R), sb("o_lo", [P, SEQ], F32R)
        spare = sb("pool_spare", [P, 1])

        names = ("consts_loaded", "ones_set", "projected", "k_done", "q_done", "kv_done", "k_sum_done",
                 "kv_sum_done", "num_parts", "num_done", "den_parts", "den_done", "rden_done", "o_done",
                 "o_hi_done", "o_lo_done", "y_done", "bo_added", "x_done")
        (consts_loaded, ones_set, projected, k_done, q_done, kv_done, k_sum_done, kv_sum_done, num_parts,
         num_done, den_parts, den_done, rden_done, o_done, o_hi_done, o_lo_done, y_done, bo_added, x_done) = (
            sem(f"{tag}_{n}") for n in names)

        def run(body, engine):
            body(0, 0, False)
            body(1, 1, False)
            with engine.Fori(1, SEQS // 2 - 1) as i:
                body(2 * i, 0, False)
                body(2 * i + 1, 1, False)
            body(SEQS - 2, 0, False)
            body(SEQS - 1, 1, True)

        block = ctx.enter_context(nc.Block())

        @block.sync
        def _(sp):
            sp.dma_start(bv[:, :], a["b_bv"]).then_inc(consts_loaded, 16)
            sp.dma_start(bo[:, :], a["b_bo"].partition_broadcast(P)).then_inc(consts_loaded, 16)

        @block.tensor
        def _(pe):
            def project(b, i):
                norm.tensor_transposes(pe, b)
                at_least(pe, kv_done, b - 1)
                at_least(pe, q_done, b - 1)
                pe.wait_ge(norm.lo_done, b + 1)
                three_products(pe, k_ps[i][:, :], halves(wk), norm.halves(i))
                three_products(pe, v_ps[i][:, :], halves(wv), norm.halves(i))
                three_products(pe, q_ps[i][:, :], halves(wq), norm.halves(i)).then_inc(projected, 1)

            def body(b, i, final):
                if not final:
                    project(b + 1, 1 - i)
                at_least(pe, x_done, b)
                pe.wait_ge(o_lo_done, b + 1)
                for c in range(CH):
                    o_c = tuple(t[:, :].rearrange("r (p c) -> r c p", c=CH)[:, c, :] for t in (o_hi, o_lo))
                    last = three_products(pe, out_ps[:, c, :], o_c, halves(wo))
                last.then_inc(y_done, 1)

            project(0, 0)
            run(body, pe)

        @block.scalar
        def _(act):
            def features(b, i):
                norm.scalar_hi(act, b, i)
                act.wait_ge(projected, b + 1)
                at_least(act, o_done, b - 1)
                act.activation(k[0][i][:, :], k_ps[i][:, :], ACT.Sigmoid, bias=scalars[:, 4:5], scale=scalars[:, 0:1])
                act.activation(k[1][i][:, :], k_ps[i][:, :], ACT.Sigmoid, bias=scalars[:, 5:6], scale=scalars[:, 1:2])\
                    .then_inc(k_done, 1)
                act.activation(q[0][i][:, :], q_ps[i][:, :], ACT.Sigmoid, bias=scalars[:, 2:3], scale=scalars[:, 0:1])
                act.activation(q[1][i][:, :], q_ps[i][:, :], ACT.Sigmoid, bias=scalars[:, 3:4], scale=scalars[:, 1:2])\
                    .then_inc(q_done, 1)

            def body(b, i, final):
                if not final:
                    features(b + 1, 1 - i)
                act.wait_ge(o_done, b + 1)
                at_least(act, y_done, b)
                act.copy(o_hi[:, :], o[:, :]).then_inc(o_hi_done, 1)

            features(0, 0)
            run(body, act)

        @block.vector
        def _(dve):
            def body(b, i, final):
                dve.wait_ge(k_done, b + 1)
                for f in range(2):
                    last = dve.scalar_tensor_tensor(kv[f][:, :], v_ps[i][:, :], bv[:, :], k[f][i][:, :],
                                                    ALU.add, ALU.mult)
                last.then_inc(kv_done, 1)
                for f in range(2):
                    last = dve.tensor_tensor_scan(k_sum[f][:, :], ones[:, :], k[f][i][:, :], 0.0, ALU.mult, ALU.add)
                last.then_inc(k_sum_done, 1)
                dve.wait_ge(kv_done, b + 1)
                for f in range(2):
                    last = dve.tensor_tensor_scan(kv_sum[f][:, :], ones[:, :], kv[f][:, :], 0.0, ALU.mult, ALU.add)
                last.then_inc(kv_sum_done, 1)
                if not final:
                    norm.vector_statistics(dve, b + 1)
                dve.wait_ge(q_done, b + 1)
                dve.wait_ge(kv_sum_done, b + 1)
                for f in range(2):
                    last = dve.tensor_tensor(num[f][:, :], q[f][i][:, :], kv_sum[f][:, :], ALU.mult)
                last.then_inc(num_parts, 1)
                if not final:
                    norm.vector_rows(dve, b + 1)
                dve.wait_ge(num_parts, b + 1)
                dve.tensor_tensor(num_all[:, :], num[0][:, :], num[1][:, :], ALU.add).then_inc(num_done, 1)
                if not final:
                    norm.vector_lo(dve, b + 1, 1 - i)
                dve.wait_ge(den_done, b + 1)
                dve.reciprocal(rden[:, :], den_all[:, :]).then_inc(rden_done, 1)
                dve.wait_ge(rden_done, b + 1)
                dve.tensor_tensor(o[:, :], num_all[:, :], rden[:, :], ALU.mult).then_inc(o_done, 1)
                dve.wait_ge(o_hi_done, b + 1)
                dve.tensor_tensor(o_lo[:, :], o[:, :], o_hi[:, :].bitcast(F32), ALU.subtract).then_inc(o_lo_done, 1)
                dve.wait_ge(bo_added, b + 1)
                dve.wait_ge(y_done, b + 1)
                dve.tensor_tensor(x_all[:, b, :, :], x_all[:, b, :, :], out_ps[:, :, :], ALU.add)\
                    .then_inc(x_done, 1)

            dve.memset(ones[:, :], 1.0).then_inc(ones_set, 1)
            dve.wait_ge(ones_set, 1)
            dve.wait_ge(consts_loaded, 32)
            norm.vector_statistics(dve, 0)
            norm.vector_rows(dve, 0)
            norm.vector_lo(dve, 0, 0)
            run(body, dve)

        @block.gpsimd
        def _(pool):
            def body(b, i, final):
                pool.wait_ge(norm.rows_done, b + 1)
                pool.tensor_tensor(spare[:, :], norm.eps[:, 0:1], norm.eps[:, 0:1], ALU.add)
                pool.tensor_tensor(x_all[:, b, :, :], x_all[:, b, :, :],
                                   bo[:, :].unsqueeze(1).to_broadcast([P, CH, D]), ALU.add).then_inc(bo_added, 1)
                if not final:
                    norm.gpsimd_rstd(pool, b + 1)
                pool.wait_ge(q_done, b + 1)
                pool.wait_ge(k_sum_done, b + 1)
                for f in range(2):
                    last = pool.tensor_tensor(den[f][:, :], q[f][i][:, :], k_sum[f][:, :], ALU.mult)
                last.then_inc(den_parts, 1)
                pool.wait_ge(den_parts, b + 1)
                pool.tensor_tensor(den_all[:, :], den[0][:, :], den[1][:, :], ALU.add).then_inc(den_done, 1)

            norm.gpsimd_setup(pool)
            pool.wait_ge(consts_loaded, 32)
            norm.gpsimd_rstd(pool, 0)
            run(body, pool)


def linear_weights(nc, sem, ctx, a):
    names = ("wq", "wk", "wv", "wo")
    out = {n: tuple(ctx.enter_context(nc.sbuf_tensor(f"b_{n}_{h}", [P, D], F32R)) for h in ("hi", "lo")) for n in names}
    scalars = ctx.enter_context(nc.sbuf_tensor("b_scalars", [P, 8], F32))
    with ExitStack() as local:
        def sb(name, shape):
            return local.enter_context(nc.sbuf_tensor(f"b_{name}", shape, F32))

        raw = {n: sb(f"{n}_raw", [P, D]) for n in ("wq0", "wq1", "wk0", "wk1", "wv", "wo")}
        diff = {n: sb(f"{n}_diff", [P, D]) for n in ("wq", "wk")}
        bias = {n: sb(f"{n}_raw", [P, 2]) for n in ("bq", "bk")}
        bias_diff = sb("bias_diff", [P, 2])
        beta = sb("beta", [P, 1])
        loaded, diff_done, hi_done, beta_done = (sem(f"b_weights_{n}") for n in ("loaded", "diff", "hi", "beta"))
        minus_done = sem("b_weights_minus")
        block = local.enter_context(nc.Block())

        @block.sync
        def _(sp):
            for n, t in raw.items():
                sp.dma_start(t[:, :], a[f"b_{n}"]).then_inc(loaded, 16)
            for n, t in bias.items():
                sp.dma_start(t[:, :], a[f"b_{n}"]).then_inc(loaded, 16)
            sp.dma_start(beta[:, :], a["b_beta"].partition_broadcast(P)).then_inc(loaded, 16)

        @block.scalar
        def _(act):
            act.wait_ge(loaded, 9 * 16)
            act.activation(scalars[:, 0:1], beta[:, :], ACT.Exp).then_inc(beta_done, 1)
            act.wait_ge(diff_done, 1)
            for n in names:
                last = act.copy(out[n][0][:, :], (diff[n] if n in diff else raw[n])[:, :])
            last.then_inc(hi_done, 1)

        @block.vector
        def _(dve):
            dve.wait_ge(loaded, 9 * 16)
            for n in diff:
                dve.tensor_tensor(diff[n][:, :], raw[f"{n}0"][:, :], raw[f"{n}1"][:, :], ALU.subtract)
            for j, n in enumerate(bias):
                last = dve.tensor_tensor(bias_diff[:, j:j + 1], bias[n][:, 0:1], bias[n][:, 1:2], ALU.subtract)
            last.then_inc(diff_done, 1)
            dve.wait_ge(diff_done, 1)
            dve.wait_ge(beta_done, 1)
            dve.tensor_scalar(scalars[:, 1:2], scalars[:, 0:1], -1.0, None, ALU.mult).then_inc(minus_done, 1)
            dve.wait_ge(minus_done, 1)
            for j in range(2):
                for sign in range(2):
                    dve.tensor_tensor(scalars[:, 2 + 2 * j + sign:3 + 2 * j + sign], bias_diff[:, j:j + 1],
                                      scalars[:, sign:sign + 1], ALU.mult)
            dve.wait_ge(hi_done, 1)
            for n in names:
                dve.tensor_tensor(out[n][1][:, :], (diff[n] if n in diff else raw[n])[:, :],
                                  out[n][0][:, :].bitcast(F32), ALU.subtract)
    return out, scalars


def run_phases(nc, sem, ctx, x_all, ident, a):
    b, scalars = linear_weights(nc, sem, ctx, a)
    f = split_weights(nc, sem, ctx, "ffn", [(n, a[n]) for n in ("gate", "up_main", "up_tail", "down_main", "down_tail")])
    s = split_weights(nc, sem, ctx, "a", [(n, a[n]) for n in ("a_wq", "a_wk", "a_wv", "a_wo")])
    attention_phase(nc, sem, x_all, ident, s["a_wq"], s["a_wk"], s["a_wv"], s["a_wo"], a, "a")
    experts = (f["gate"], (f["up_main"], f["up_tail"]), (f["down_main"], f["down_tail"]))
    ffn_phase(nc, sem, x_all, ident, *experts, "f1")
    linear_phase(nc, sem, x_all, ident, b["wq"], b["wk"], b["wv"], b["wo"], a, scalars, "b")
    ffn_phase(nc, sem, x_all, ident, *experts, "f2")


def split_weights(nc, sem, ctx, tag, loads):
    out = {}
    with ExitStack() as local:
        raws = {}
        for name, ap in loads:
            shape = [int(n) for n in ap.shape]
            out[name] = tuple(ctx.enter_context(nc.sbuf_tensor(f"{tag}_{name}_{h}", shape, F32R))
                              for h in ("hi", "lo"))
        for name, ap in loads:
            raws[name] = local.enter_context(nc.sbuf_tensor(f"{tag}_{name}_raw", [int(n) for n in ap.shape], F32))
        loaded = [sem(f"{tag}_{name}_loaded") for name, _ in loads]
        hi_done = sem(f"{tag}_weights_hi_done")
        lo_done = sem(f"{tag}_weights_lo_done")
        block = local.enter_context(nc.Block())

        def whole(t):
            return t[tuple(slice(None) for _ in t.shape)]

        @block.sync
        def _(sp):
            for (name, ap), done in zip(loads, loaded):
                sp.dma_start(whole(raws[name]), ap).then_inc(done, 16)

        @block.scalar
        def _(act):
            for (name, _), done in zip(loads, loaded):
                act.wait_ge(done, 16)
                act.copy(whole(out[name][0]), whole(raws[name])).then_inc(hi_done, 1)

        @block.vector
        def _(dve):
            for n, (name, _) in enumerate(loads):
                dve.wait_ge(hi_done, n + 1)
                dve.tensor_tensor(whole(out[name][1]), whole(raws[name]), whole(out[name][0]).bitcast(F32),
                                  ALU.subtract).then_inc(lo_done, 1)
    return out


def identity(nc, sem, ident):
    ready = sem("identity_ready")
    with nc.Block() as block:
        @block.gpsimd
        def _(pool):
            pool.memset(ident[:, :], 0.0).then_inc(ready, 1)
            pool.wait_ge(ready, 1)
            pool.affine_select(out=ident[:, :], in_=ident[:, :], compare_op=ALU.not_equal, fill=1.0, base=0,
                               pattern=[[-1, P]], channel_multiplier=1).then_inc(ready, 1)


def load_all(nc, sem, x_all, x):
    loaded = sem("x_loaded")
    with nc.Block() as block:
        @block.sync
        def _(sp):
            for b in range(SEQS):
                sp.dma_start(x_all[:, b, :, :], x[b].rearrange("(p c) d -> p c d", c=CH)).then_inc(loaded, 16)
            sp.wait_ge(loaded, 16 * SEQS)


def store_all(nc, sem, x_all, out):
    stored = sem("x_stored")
    with nc.Block() as block:
        @block.sync
        def _(sp):
            for b in range(SEQS):
                sp.dma_start(out[b].rearrange("(p c) d -> p c d", c=CH), x_all[:, b, :, :]).then_inc(stored, 16)
            sp.wait_ge(stored, 16 * SEQS)


def program(nc, a, out):
    with ExitStack() as ctx:
        def sem(name):
            return ctx.enter_context(nc.semaphore(name))

        x_all = ctx.enter_context(nc.sbuf_tensor("x_all", [P, SEQS, CH, D], F32))
        ident = ctx.enter_context(nc.sbuf_tensor("ident", [P, P], F32))
        identity(nc, sem, ident)
        load_all(nc, sem, x_all, a["x"])
        run_phases(nc, sem, ctx, x_all, ident, a)
        store_all(nc, sem, x_all, out)


def kernel(**inputs):
    import numpy as np
    import concourse.bacc as bacc
    from concourse.bass_utils import run_bass_kernel_spmd

    i = {name: np.asarray(value) for name, value in inputs.items()}
    heads, width = HEADS, D // HEADS

    def depth_major(w):
        return w.reshape(w.shape[:-1] + (heads, width)).swapaxes(-1, -2).reshape(w.shape)

    w1 = i["L0_ffn_w1"].reshape(EXPERTS, D, 2, FFN).transpose(1, 0, 2, 3)
    up_tail = np.zeros((D, PAIRS, 2, TAIL_ROWS), w1.dtype)
    up_tail[..., :TAIL] = w1[:, 0::2, :, P:]
    up_tail[..., ODD_TAIL:] = w1[:, 1::2, :, P:]
    w2 = i["L0_ffn_w2"].transpose(1, 0, 2)
    down_tail = np.zeros((TAIL_ROWS, EXPERTS, D), w2.dtype)
    down_tail[:TAIL, 0::2] = w2[P:, 0::2]
    down_tail[ODD_TAIL:, 1::2] = w2[P:, 1::2]
    pair_first, pair_second = np.arange(D) // 2 * 2, np.arange(D) // 2 * 2 + 1
    laid_out = {
        "x": i["L0_attn_a_hidden_states"],
        "a_wq": depth_major(i["L0_attn_a_Wq"]), "a_bq": depth_major(i["L0_attn_a_bq"])[:, None],
        "a_wk": depth_major(i["L0_attn_a_Wk"]), "a_bk": depth_major(i["L0_attn_a_bk"])[:, None],
        "a_wv": i["L0_attn_a_Wv"], "a_bv": i["L0_attn_a_bv"][None],
        "a_wo": i["L0_attn_a_Wo"], "a_bo": i["L0_attn_a_bo"][None],
        "b_wq0": i["L0_attn_b_Wq"].T[:, pair_first], "b_wq1": i["L0_attn_b_Wq"].T[:, pair_second],
        "b_wk0": i["L0_attn_b_Wk"].T[:, pair_first], "b_wk1": i["L0_attn_b_Wk"].T[:, pair_second],
        "b_bq": np.stack([i["L0_attn_b_bq"][pair_first], i["L0_attn_b_bq"][pair_second]], 1),
        "b_bk": np.stack([i["L0_attn_b_bk"][pair_first], i["L0_attn_b_bk"][pair_second]], 1),
        "b_wv": i["L0_attn_b_Wv"].T, "b_bv": i["L0_attn_b_bv"][:, None],
        "b_wo": i["L0_attn_b_Wo"].T, "b_bo": i["L0_attn_b_bo"][None],
        "b_beta": i["L0_attn_b_beta"][None],
        "gate": i["L0_ffn_gate_w"].T,
        "up_main": w1[..., :P], "up_tail": up_tail,
        "down_main": w2[:P], "down_tail": down_tail,
    }
    nc = bacc.Bacc("TRN2", target_bir_lowering=False, num_devices=1)
    arrays, args = {}, {}
    for name, value in laid_out.items():
        value = np.ascontiguousarray(value)
        arrays[f"in_{name}"] = value
        args[name] = nc.dram_tensor(f"in_{name}", value.shape, F32, kind="ExternalInput").ap()
    out = nc.dram_tensor("out", (SEQS, SEQ, D), F32, kind="ExternalOutput").ap()
    program(nc, args, out)
    result = run_bass_kernel_spmd(nc, [arrays], core_ids=[0])
    return result.results[0]["out"]
```

```python
import math
from contextlib import ExitStack

import concourse.bass as bass
from concourse import mybir

F32 = mybir.dt.float32
F32R = mybir.dt.float32r
ACT = mybir.ActivationFunctionType
ALU = mybir.AluOpType
AX = mybir.AxisListType

P = 128
SEQS, SEQ, D = 16, 512, 128
CH = SEQ // P
EPS = 1e-5

HEADS = 8
HEAD = D // HEADS

EXPERTS, FFN = 8, 176
TAIL = FFN - P
ODD_TAIL = 64
TAIL_ROWS = ODD_TAIL + TAIL
PAIRS = EXPERTS // 2
UNITS = 3 * PAIRS


def at_least(engine, semaphore, value):
    if isinstance(value, int) and value <= 0:
        return
    engine.wait_ge(semaphore, value)


def three_products(tensor, out, stationary, moving, start=True, stop=True):
    (s_hi, s_lo), (m_hi, m_lo) = stationary, moving
    tensor.matmul(out, s_hi, m_hi, start=start, stop=False)
    tensor.matmul(out, s_hi, m_lo, start=False, stop=False)
    return tensor.matmul(out, s_lo, m_hi, start=False, stop=stop)


def halves(w):
    return w[0][:, :], w[1][:, :]


class Space:

    def __init__(self, nc, ctx, tag):
        self.nc, self.ctx, self.tag = nc, ctx, tag

    def sb(self, name, shape, dt=F32):
        return self.ctx.enter_context(self.nc.sbuf_tensor(f"{self.tag}_{name}", shape, dt))

    def ps(self, name, shape, dt=F32):
        return self.ctx.enter_context(self.nc.psum_tensor(f"{self.tag}_{name}", shape, dt))


class Norm:

    def __init__(self, nc, space, sem, x_all, ident, transposed, in_time_order=False):
        self.in_time_order = in_time_order
        self.nc, self.x_all, self.ident = nc, x_all, ident
        self.stats = space.sb("ln_stats", [P, CH, 6])
        self.moments = space.sb("ln_moments", [P, CH, 2])
        self.shifted = space.sb("ln_shifted", [P, CH])
        self.spare = space.sb("ln_spare", [P, 1])
        self.eps = space.sb("ln_eps", [P, CH])
        self.power = space.sb("ln_power", [P, CH])
        self.rstd = space.sb("ln_rstd", [P, CH])
        self.rows = space.sb("ln_rows", [P, CH, D])
        self.transposed = transposed
        self.hi = [space.sb(f"xn_hi{i}", [P, SEQ], F32R) for i in range(2)]
        self.lo = [space.sb(f"xn_lo{i}", [P, SEQ], F32R) for i in range(2)]
        t = space.tag
        self.stats_done = sem(f"{t}_ln_stats_done")
        self.moments_done = sem(f"{t}_ln_moments_done")
        self.power_set = sem(f"{t}_ln_power_set")
        self.shifted_done = sem(f"{t}_ln_shifted_done")
        self.rstd_done = sem(f"{t}_ln_rstd_done")
        self.rows_done = sem(f"{t}_ln_rows_done")
        self.transposes_done = sem(f"{t}_ln_transposes_done")
        self.hi_done = sem(f"{t}_xn_hi_done")
        self.lo_done = sem(f"{t}_xn_lo_done")

    def halves(self, b_parity):
        return self.hi[b_parity][:, :], self.lo[b_parity][:, :]

    def halves_chunk(self, b_parity, c):
        return (self.hi[b_parity][:, c * P:(c + 1) * P], self.lo[b_parity][:, c * P:(c + 1) * P])

    def gpsimd_setup(self, pool):
        pool.memset(self.eps[:, :], EPS)
        pool.memset(self.power[:, :], -0.5).then_inc(self.power_set, 1)
        pool.wait_ge(self.power_set, 1)

    def vector_statistics(self, dve, b, chunks=range(CH)):
        for c in chunks:
            last = dve.bn_stats(self.stats[:, c, :], self.x_all[:, b, c, :])
        if c == CH - 1:
            last.then_inc(self.stats_done, 1)

    def vector_moments(self, dve, b):
        dve.wait_ge(self.stats_done, b + 1)
        dve.memset(self.spare[:, :], 0.0)
        for c in range(CH):
            last = dve.bn_aggr(self.moments[:, c, :], self.stats[:, c, :])
        last.then_inc(self.moments_done, 1)

    def gpsimd_rstd(self, pool, b):
        pool.wait_ge(self.moments_done, b + 1)
        pool.tensor_tensor(self.shifted[:, :], self.moments[:, :, 1], self.eps[:, :], ALU.add)\
            .then_inc(self.shifted_done, 1)
        pool.wait_ge(self.shifted_done, b + 1)
        pool.tensor_tensor(self.rstd[:, :], self.shifted[:, :], self.power[:, :], ALU.pow)\
            .then_inc(self.rstd_done, 1)

    def vector_rows(self, dve, b, chunks=range(CH)):
        if 0 in chunks:
            dve.wait_ge(self.rstd_done, b + 1)
        for c in chunks:
            last = dve.tensor_scalar(self.rows[:, c, :], self.x_all[:, b, c, :], self.moments[:, c, 0:1],
                                     self.rstd[:, c:c + 1], ALU.subtract, ALU.mult)
        if c == CH - 1:
            last.then_inc(self.rows_done, 1)

    def tensor_transposes(self, pe, b):
        pe.wait_ge(self.rows_done, b + 1)
        at_least(pe, self.lo_done, b)
        for c in range(CH):
            last = pe.transpose(self.transposed[:, c * P:(c + 1) * P], self.rows[:, c, :], self.ident[:, :])
        last.then_inc(self.transposes_done, 1)

    def scalar_hi(self, act, b, parity):
        act.wait_ge(self.transposes_done, b + 1)
        act.copy(self.columns(self.hi[parity]), self.read_turned()).then_inc(self.hi_done, 1)

    def vector_lo(self, dve, b, parity):
        dve.wait_ge(self.hi_done, b + 1)
        dve.tensor_tensor(self.columns(self.lo[parity]), self.read_turned(),
                          self.columns(self.hi[parity]).bitcast(F32), ALU.subtract).then_inc(self.lo_done, 1)

    def read_turned(self):
        t = self.transposed[:, :]
        return t.rearrange("d (c p) -> d c p", c=CH) if self.in_time_order else t

    def columns(self, half):
        return half[:, :].rearrange("d (p c) -> d c p", c=CH) if self.in_time_order else half[:, :]


def attention_phase(nc, sem, x_all, ident, wq, wk, wv, wo, a, tag):
    M_ROW, M_END = 3 * HEAD, 3 * HEAD + 2
    ITEMS = HEADS * CH
    BURST, AT_BURST = 4, 1
    HALF = ITEMS // 2
    STACK_COUNT, MAX_COUNT = 16 * 7, 16 * 2
    AT_MAX, AT_PROJECT, AT_OUT0, AT_OUT1, AT_BACK, AT_Y = (2, 23), (9, 12, 16, 20), 25, 6, 10, 14
    with ExitStack() as ctx:
        space = Space(nc, ctx, tag)
        sb, ps = space.sb, space.ps
        max_ps = [ps(f"max{i}", [P, SEQ]) for i in range(2)]
        score_ps = [ps(f"score{i}", [P, SEQ]) for i in range(2)]
        pv_ps = [ps(f"pv{i}", [P, SEQ]) for i in range(2)]
        work_ps = ps("work", [P, SEQ])
        out_ps = ps("out", [P, CH, D])
        norm = Norm(nc, space, sem, x_all, ident, work_ps)
        bq, bk = sb("bq", [P, 1]), sb("bk", [P, 1])
        bv, bo = sb("bv", [P, D]), sb("bo", [P, D])
        q_stack = [sb(f"q_stack{i}", [P, HEADS, SEQ], F32R) for i in range(2)]
        k_stack = [sb(f"k_stack{i}", [P, HEADS, SEQ], F32R) for i in range(2)]
        zeros = sb("zeros", [2, SEQ])
        q_hi, q_lo, k_hi, k_lo = (sb(n, [P, SEQ], F32R) for n in ("q_hi", "q_lo", "k_hi", "k_lo"))
        v_rows = sb("v_rows", [P, CH, HEADS, HEAD])
        v_ones = [sb(f"v_ones{i}", [P, CH, HEADS, 32]) for i in range(2)]
        neg_max = sb("neg_max", [P, HEADS, CH])
        m_hi = [sb(f"m_hi{g}", [HALF, P], F32R) for g in range(2)]
        m_lo = [sb(f"m_lo{g}", [HALF, P], F32R) for g in range(2)]
        probs = [sb(f"probs{i}", [P, SEQ]) for i in range(2 * BURST)]
        pv = [sb(f"pv_sb{i}", [P, SEQ]) for i in range(2)]
        rsum = sb("rsum", [P, CH, 4])
        o_rows = sb("o_rows", [P, CH, D])
        o_hi, o_lo = sb("o_hi", [P, SEQ], F32R), sb("o_lo", [P, SEQ], F32R)
        spare = sb("pool_spare", [P, 1])

        names = ("consts_loaded", "consts_set", "q_proj", "k_proj", "v_proj", "q_hi_done", "q_lo_done",
                 "k_hi_done", "k_lo_done", "v_rows_done", "v_ones_done", "stack_loaded00", "stack_loaded01", "stack_loaded10",
                 "stack_loaded11", "max_scores",
                 "max_done", "max_turned", "m_hi_done", "m_lo_done", "m_loaded0", "m_loaded1", "scores", "exp_done",
                 "pv_done", "pv_copied", "o_turned", "rsum_done", "o_rows_done", "o_back", "o_hi_done",
                 "o_lo_done", "y_done", "bo_added", "x_done")
        (consts_loaded, consts_set, q_proj, k_proj, v_proj, q_hi_done, q_lo_done, k_hi_done, k_lo_done,
         v_rows_done, v_ones_done, stack_loaded00, stack_loaded01,
         stack_loaded10, stack_loaded11, max_scores, max_done, max_turned, m_hi_done, m_lo_done,
         m_loaded0, m_loaded1, scores, exp_done, pv_done, pv_copied, o_turned, rsum_done, o_rows_done, o_back,
         o_hi_done, o_lo_done, y_done, bo_added, x_done) = (sem(f"{tag}_{n}") for n in names)
        CONSTS = 4 * 16
        stack_loaded = ((stack_loaded00, stack_loaded01), (stack_loaded10, stack_loaded11))
        m_loaded = (m_loaded0, m_loaded1)

        def stacked(turn, q):
            return STACK_COUNT * (turn + 1)

        def item(i):
            return i // 16 * 4 + i % 4, i % 16 // 4

        def run(body, engine):
            body(0, 0, 0, False, True, True)
            body(1, 1, 0, True, True, True)
            with engine.Fori(1, SEQS // 2 - 1) as turn:
                body(2 * turn, 0, turn, True, True, True)
                body(2 * turn + 1, 1, turn, True, True, True)
            body(SEQS - 2, 0, SEQS // 2 - 1, True, True, False)
            body(SEQS - 1, 1, SEQS // 2 - 1, True, False, False)

        block = ctx.enter_context(nc.Block())

        @block.sync
        def _(sp):
            sp.dma_start(bq[:, :], a["a_bq"]).then_inc(consts_loaded, 16)
            sp.dma_start(bk[:, :], a["a_bk"]).then_inc(consts_loaded, 16)
            sp.dma_start(bv[:, :], a["a_bv"].partition_broadcast(P)).then_inc(consts_loaded, 16)
            sp.dma_start(bo[:, :], a["a_bo"].partition_broadcast(P)).then_inc(consts_loaded, 16)

            def stack(b, q, group):
                heads = slice(4 * group, 4 * group + 4)
                done = stack_loaded[q][group]

                def restack(stacked_rows, row, half):
                    sp.dma_start(stacked_rows[row:row + HEAD, heads, :].bitcast(F32),
                                 half[group * 64:group * 64 + 64, :].bitcast(F32)).then_inc(done, 16)

                at_least(sp, scores, ITEMS * (b - 2) + HALF * (group + 1))
                sp.dma_start(q_stack[q][M_ROW:M_END, heads, :].bitcast(F32),
                             zeros[:, :].unsqueeze(1).to_broadcast([2, 4, SEQ])).then_inc(done, 16)
                sp.wait_ge(q_lo_done, b + 1)
                for row, half in ((0, q_hi), (HEAD, q_lo), (2 * HEAD, q_hi)):
                    restack(q_stack[q], row, half)
                sp.wait_ge(k_lo_done, b + 1)
                for row, half in ((0, k_hi), (HEAD, k_hi), (2 * HEAD, k_lo)):
                    restack(k_stack[q], row, half)

            def maxima(b, q, group):
                sp.wait_ge(m_lo_done, 2 * b + group + 1)
                for row, half in ((M_ROW, m_hi[group]), (M_ROW + 1, m_lo[group])):
                    sp.dma_start(q_stack[q][row:row + 1, 4 * group:4 * group + 4, :].bitcast(F32)
                                 .rearrange("r h (c t) -> r (h c) t", c=CH),
                                 half[:, :].bitcast(F32)).then_inc(m_loaded[group], 16)

            def body(b, q, turn, before, after1, after2):
                maxima(b, q, 1)
                if after1:
                    stack(b + 1, 1 - q, 1)
                if after2:
                    stack(b + 2, q, 0)
                if after1:
                    maxima(b + 1, 1 - q, 0)

            sp.wait_ge(consts_set, 1)
            stack(0, 0, 0)
            stack(0, 0, 1)
            stack(1, 1, 0)
            maxima(0, 0, 0)
            run(body, sp)

        @block.tensor
        def _(pe):
            def project(b, q, part):
                if part == 0:
                    at_least(pe, v_rows_done, b)
                    at_least(pe, m_lo_done, 2 * b - 2)
                    norm.tensor_transposes(pe, b)
                if part == 1:
                    pe.wait_ge(norm.lo_done, b + 1)
                    three_products(pe, work_ps[:, :], halves(wq), norm.halves(q)).then_inc(q_proj, 1)
                if part == 2:
                    pe.wait_ge(q_lo_done, b + 1)
                    three_products(pe, work_ps[:, :], halves(wk), norm.halves(q)).then_inc(k_proj, 1)
                if part == 3:
                    pe.wait_ge(k_lo_done, b + 1)
                    for c in range(CH):
                        last = three_products(pe, work_ps[:, c * P:(c + 1) * P], norm.halves_chunk(q, c), halves(wv))
                    last.then_inc(v_proj, 1)

            def largest(b, q, turn, j):
                h, c = j // CH, j % CH
                if j % HALF == 0:
                    pe.wait_ge(stack_loaded[q][j // HALF], stacked(turn, q))
                at_least(pe, max_done, b * ITEMS + j - 1)
                pe.matmul(max_ps[j % 2][:, :], q_stack[q][:, h, c * P:(c + 1) * P], k_stack[q][:, h, :],
                          start=True, stop=True).then_inc(max_scores, 1)

            def turn_max(b, group, projected=None):
                pe.wait_ge(max_done, ITEMS * b + HALF * (group + 1))
                if group:
                    pe.wait_ge(m_lo_done, 2 * b + 1)
                else:
                    pe.wait_ge(v_rows_done, projected)
                pe.transpose(work_ps[0:HALF, 0:P],
                             neg_max[:, 4 * group:4 * group + 4, :].rearrange("p h c -> p (h c)"), ident[:, :])\
                    .then_inc(max_turned, 1)

            def score(b, q, i):
                h, c = item(i)
                if i % HALF == 0:
                    pe.wait_ge(m_loaded[i // HALF], MAX_COUNT * (b + 1))
                at_least(pe, exp_done, b * ITEMS + i - 1)
                pe.matmul(score_ps[i % 2][:, :], k_stack[q][:, h, c * P:(c + 1) * P], q_stack[q][:, h, :],
                          start=True, stop=True).then_inc(scores, 1)

            def weigh(b, q, burst):
                for i in range(burst * BURST, (burst + 1) * BURST):
                    h, c = item(i)
                    group, side = h // 4, h % 4
                    if i == 0:
                        pe.wait_ge(v_ones_done, b + 1)
                    if i % HALF == 0:
                        at_least(pe, pv_copied, 2 * (b - 1) + group + 1)
                    pe.wait_ge(exp_done, b * ITEMS + i + 1)
                    pe.matmul(pv_ps[group][32 * side:32 * side + 32, :], v_ones[q][:, c, h, :],
                              probs[i % (2 * BURST)][:, :], start=(c == 0), stop=(c == CH - 1)).then_inc(pv_done, 1)

            def turn_out(b, group):
                pe.wait_ge(pv_copied, 2 * b + group + 1)
                if group:
                    pe.wait_ge(o_rows_done, 2 * b + 1)
                else:
                    at_least(pe, x_done, b)
                for c in range(CH):
                    last = pe.transpose(out_ps[:, c, :], pv[group][:, c * P:(c + 1) * P], ident[:, :])
                last.then_inc(o_turned, 1)

            def turn_back(b):
                pe.wait_ge(o_rows_done, 2 * b + 2)
                for c in range(CH):
                    last = pe.transpose(out_ps[:, c, :], o_rows[:, c, :], ident[:, :])
                last.then_inc(o_back, 1)

            def project_out(b):
                pe.wait_ge(o_lo_done, b + 1)
                for c in range(CH):
                    t = slice(c * P, (c + 1) * P)
                    last = three_products(pe, out_ps[:, c, :], (o_hi[:, t], o_lo[:, t]), halves(wo))
                last.then_inc(y_done, 1)

            def body(b, q, turn, before, after1, after2):
                for i in range(ITEMS):
                    score(b, q, i)
                    if after1:
                        largest(b + 1, 1 - q, turn + q, i)
                    if i % BURST == AT_BURST:
                        if i >= BURST:
                            weigh(b, q, i // BURST - 1)
                        elif before:
                            weigh(b - 1, 1 - q, ITEMS // BURST - 1)
                    if i == AT_MAX[0]:
                        turn_max(b, 1)
                    if after1 and i == AT_MAX[1]:
                        turn_max(b + 1, 0, b + 3 if after2 else SEQS)
                    if after2 and i in AT_PROJECT:
                        project(b + 2, q, AT_PROJECT.index(i))
                    if i == AT_OUT0:
                        turn_out(b, 0)
                    if before:
                        if i == AT_OUT1:
                            turn_out(b - 1, 1)
                        if i == AT_BACK:
                            turn_back(b - 1)
                        if i == AT_Y:
                            project_out(b - 1)

            pe.wait_ge(consts_set, 1)
            for part in range(4):
                project(0, 0, part)
            for part in range(4):
                project(1, 1, part)
            for j in range(ITEMS):
                largest(0, 0, 0, j)
            turn_max(0, 0, 2)
            run(body, pe)
            weigh(SEQS - 1, 1, ITEMS // BURST - 1)
            turn_out(SEQS - 1, 1)
            turn_back(SEQS - 1)
            project_out(SEQS - 1)

        @block.scalar
        def _(act):
            def project(b, q, turn, part):
                if part == 0:
                    norm.scalar_hi(act, b, q)
                if part == 1:
                    act.wait_ge(q_proj, b + 1)
                    at_least(act, stack_loaded[1 - q][1], STACK_COUNT * (turn + q))
                    act.activation(q_hi[:, :], work_ps[:, :], ACT.Identity, bias=bq[:, :]).then_inc(q_hi_done, 1)
                if part == 2:
                    act.wait_ge(k_proj, b + 1)
                    act.activation(k_hi[:, :], work_ps[:, :], ACT.Identity, bias=bk[:, :]).then_inc(k_hi_done, 1)

                if part == 3:
                    act.wait_ge(v_proj, b + 1)
                    at_least(act, v_ones_done, b)
                    act.copy(v_rows[:, :, :, :].rearrange("p c h d -> p (c h d)"), work_ps[:, :])\
                        .then_inc(v_rows_done, 1)

            def round_max(b, group):
                act.wait_ge(max_turned, 2 * b + group + 1)
                at_least(act, m_loaded[group], MAX_COUNT * b)
                act.copy(m_hi[group][:, :], work_ps[0:HALF, 0:P]).then_inc(m_hi_done, 1)

            def exponential(b, i):
                n = b * ITEMS + i
                act.wait_ge(scores, n + 1)
                at_least(act, pv_done, n - 2 * BURST + 1)
                act.activation(probs[i % (2 * BURST)][:, :], score_ps[i % 2][:, :], ACT.Exp, scale=HEAD ** -0.5)\
                    .then_inc(exp_done, 1)

            def copy_pv(b, group):
                act.wait_ge(pv_done, b * ITEMS + 16 * (group + 1))
                at_least(act, o_turned, 2 * (b - 1) + group + 1)
                act.copy(pv[group][:, :], pv_ps[group][:, :]).then_inc(pv_copied, 1)

            def out_hi(b):
                act.wait_ge(o_back, b + 1)
                act.copy(o_hi[:, :], out_ps[:, :, :].rearrange("p c d -> p (c d)")).then_inc(o_hi_done, 1)

            def body(b, q, turn, before, after1, after2):
                for i in range(ITEMS):
                    exponential(b, i)
                    if i == AT_MAX[0]:
                        round_max(b, 1)
                    if before:
                        if i == 3:
                            copy_pv(b - 1, 1)
                        if i == AT_BACK + 1:
                            out_hi(b - 1)
                    if after2 and i - 1 in AT_PROJECT:
                        project(b + 2, q, turn + 1, AT_PROJECT.index(i - 1))
                    if i == HALF + 3:
                        copy_pv(b, 0)
                    if after1 and i == AT_MAX[1]:
                        round_max(b + 1, 0)

            act.wait_ge(consts_set, 1)
            act.wait_ge(consts_loaded, CONSTS)
            for b in range(2):
                for part in range(4):
                    project(b, b, 0, part)
            round_max(0, 0)
            run(body, act)
            copy_pv(SEQS - 1, 1)
            out_hi(SEQS - 1)

        @block.vector
        def _(dve):
            def project(b, q, part):
                if part == 0:
                    norm.vector_statistics(dve, b, (0, 1))
                if part == 1:
                    norm.vector_statistics(dve, b, (2, 3))
                if part == 2:
                    norm.vector_moments(dve, b)
                if 3 <= part < 7:
                    norm.vector_rows(dve, b, (part - 3,))
                if part == 7:
                    norm.vector_lo(dve, b, q)
                if part == 8:
                    dve.wait_ge(q_hi_done, b + 1)
                    dve.scalar_tensor_tensor(q_lo[:, :], work_ps[:, :], bq[:, :], q_hi[:, :].bitcast(F32),
                                             ALU.add, ALU.subtract).then_inc(q_lo_done, 1)
                if part == 9:
                    dve.wait_ge(k_hi_done, b + 1)
                    dve.scalar_tensor_tensor(k_lo[:, :], work_ps[:, :], bk[:, :], k_hi[:, :].bitcast(F32),
                                             ALU.add, ALU.subtract).then_inc(k_lo_done, 1)

            def find_max(b, j):
                h, c = j // CH, j % CH
                if j % HALF == 0:
                    at_least(dve, max_turned, 2 * b + j // HALF - 1)
                dve.wait_ge(max_scores, b * ITEMS + j + 1)
                dve.tensor_reduce(neg_max[:, h, c:c + 1], max_ps[j % 2][:, :], AX.X, ALU.max, negate=True)\
                    .then_inc(max_done, 1)

            def max_lo(b, group):
                dve.wait_ge(m_hi_done, 2 * b + group + 1)
                dve.tensor_tensor(m_lo[group][:, :], work_ps[0:HALF, 0:P], m_hi[group][:, :].bitcast(F32),
                                  ALU.subtract).then_inc(m_lo_done, 1)

            def normalise(b, group):
                n = 2 * b + group
                dve.wait_ge(o_turned, n + 1)
                heads = out_ps[:, :, :].rearrange("p c (h r) -> p c h r", r=32)
                dve.reciprocal(rsum[:, :, :], heads[:, :, :, 0]).then_inc(rsum_done, 1)
                dve.wait_ge(rsum_done, n + 1)
                half = o_rows[:, :, group * 64:group * 64 + 64].rearrange("p c (h d) -> p c h d", d=HEAD)
                dve.tensor_tensor(half, heads[:, :, :, 1:HEAD + 1],
                                  rsum[:, :, :].unsqueeze(3).to_broadcast([P, CH, 4, HEAD]), ALU.mult)\
                    .then_inc(o_rows_done, 1)

            def out_lo(b):
                dve.wait_ge(o_hi_done, b + 1)
                dve.tensor_tensor(o_lo[:, :], out_ps[:, :, :].rearrange("p c d -> p (c d)"),
                                  o_hi[:, :].bitcast(F32), ALU.subtract).then_inc(o_lo_done, 1)

            def add_out(b):
                dve.wait_ge(bo_added, b + 1)
                dve.wait_ge(y_done, b + 1)
                dve.tensor_tensor(x_all[:, b, :, :], x_all[:, b, :, :], out_ps[:, :, :], ALU.add)\
                    .then_inc(x_done, 1)

            def body(b, q, turn, before, after1, after2):
                for i in range(ITEMS):
                    if after1:
                        find_max(b + 1, i)
                    if before:
                        if i == AT_OUT1 + 1:
                            normalise(b - 1, 1)
                        if i == AT_BACK + 1:
                            out_lo(b - 1)
                        if i == AT_Y + 1:
                            add_out(b - 1)
                    if after2 and i in AT_SPLIT:
                        project(b + 2, q, AT_SPLIT.index(i))
                    if i == AT_OUT0 + 1:
                        normalise(b, 0)
                    if i == AT_MAX[0] + 1:
                        max_lo(b, 1)
                    if after1 and i == AT_MAX[1] + 1:
                        max_lo(b + 1, 0)

            AT_SPLIT = (0, 1, 2, 5, 6, 7, 8, AT_PROJECT[0] + 1, AT_PROJECT[1] + 1, AT_PROJECT[2] + 1)
            for q in range(2):
                dve.memset(k_stack[q][:, :, :].bitcast(F32), 1.0)
                dve.memset(q_stack[q][:, :, :].bitcast(F32), 0.0)
                dve.memset(v_ones[q][:, :, :, 0:1], 1.0)
                dve.memset(v_ones[q][:, :, :, 1:32], 0.0)
            dve.memset(zeros[:, :], 0.0).then_inc(consts_set, 1)
            dve.wait_ge(consts_loaded, CONSTS)
            for b in range(2):
                for part in range(len(AT_SPLIT)):
                    project(b, b, part)
            for j in range(ITEMS):
                find_max(0, j)
            max_lo(0, 0)
            run(body, dve)
            normalise(SEQS - 1, 1)
            out_lo(SEQS - 1)
            add_out(SEQS - 1)

        @block.gpsimd
        def _(pool):
            def copy_v(b, q):
                pool.wait_ge(v_rows_done, b + 1)
                at_least(pool, pv_done, ITEMS * (b - 1))
                pool.tensor_tensor(v_ones[q][:, :, :, 1:HEAD + 1], v_rows[:, :, :, :],
                                   bv[:, :].rearrange("p (h d) -> p h d", d=HEAD).unsqueeze(1)
                                   .to_broadcast([P, CH, HEADS, HEAD]), ALU.add).then_inc(v_ones_done, 1)

            def add_bias(b):
                pool.wait_ge(norm.rows_done, b + 1)
                pool.tensor_tensor(spare[:, :], norm.eps[:, 0:1], norm.eps[:, 0:1], ALU.add)
                pool.tensor_tensor(x_all[:, b, :, :], x_all[:, b, :, :],
                                   bo[:, :].unsqueeze(1).to_broadcast([P, CH, D]), ALU.add).then_inc(bo_added, 1)

            def body(b, q, turn, before, after1, after2):
                if after1:
                    copy_v(b + 1, 1 - q)
                if after2:
                    norm.gpsimd_rstd(pool, b + 2)
                    add_bias(b + 2)

            norm.gpsimd_setup(pool)
            pool.wait_ge(consts_set, 1)
            pool.wait_ge(consts_loaded, CONSTS)
            norm.gpsimd_rstd(pool, 0)
            add_bias(0)
            copy_v(0, 0)
            norm.gpsimd_rstd(pool, 1)
            add_bias(1)
            run(body, pool)


def ffn_phase(nc, sem, x_all, ident, gate, up, down, selector_dram, tag):
    gate_hi, gate_lo = gate
    (up_hi, up_lo), (upt_hi, upt_lo) = up
    (dn_hi, dn_lo), (dnt_hi, dnt_lo) = down
    ROUTE_STEPS, SHIFT_STEP = 20, 2
    SPLIT_LAG = 2
    DOWN_LAG = 3
    SLOTS = 6
    with ExitStack() as ctx:
        space = Space(nc, ctx, tag)
        gate_ps = [space.ps(f"gate{i}", [P, SEQ]) for i in range(2)]
        up_ps = [space.ps(f"up{i}", [P, SEQ]) for i in range(3)]
        y_ps = space.ps("y", [P, SEQ])
        spread_ps = space.ps("spread", [P, SEQ])
        work_ps = space.ps("work", [P, SEQ])
        logits_ps = work_ps[:, 0:CH * EXPERTS].rearrange("p (c e) -> p c e", c=CH)
        norm = Norm(nc, space, sem, x_all, ident, work_ps)
        silu = [space.sb(f"silu{i}", [P, SEQ]) for i in range(2)]
        spread = [space.sb(f"spread_sb{i}", [P, SEQ]) for i in range(2)]
        weighted = [space.sb(f"weighted{i}", [P, SEQ]) for i in range(2)]
        act_f = [space.sb(f"act{i}", [P, SEQ]) for i in range(3)]
        act_hi = [space.sb(f"act_hi{i}", [P, SEQ], F32R) for i in range(SLOTS)]
        act_lo = [space.sb(f"act_lo{i}", [P, SEQ], F32R) for i in range(SLOTS)]
        y_sb = space.sb("y_sb", [P, SEQ])
        r = {n: space.sb(f"r_{n}", [P, CH, EXPERTS]) for n in
             ("logits", "shifted", "exp", "prob", "eq1", "key1", "mask1", "rest", "eq2", "key2", "mask2",
              "both", "chosen", "combine")}
        s = {n: space.sb(f"s_{n}", [P, CH]) for n in
             ("max", "sum", "rsum", "top1", "first1", "top2", "first2", "den", "rden")}
        rank = space.sb("rank", [P, EXPERTS])
        halves_sb = space.sb("weight_halves", [P, CH, 2 * EXPERTS], F32R)
        weight_rows = [space.sb(f"weight_rows{i}", [P, SEQ], F32R) for i in range(2)]
        selector = space.sb("selector", [P, UNITS, P], F32R)
        selector_raw = space.sb("selector_raw", [2 * EXPERTS, UNITS, P])

        names = ("gate_done", "up_done", "silu_done", "spread_turned", "spread_done", "weighted_done", "act_done",
                 "act_hi_done", "act_lo_done", "down_done", "y_copied", "y_turned", "added",
                 "logits_done", "exp_done", "route", "weights_turned", "weights_copied", "consts_set",
                 "selector_loaded", "selector_set")
        (gate_done, up_done, silu_done, spread_turned, spread_done, weighted_done, act_done, act_hi_done,
         act_lo_done, down_done, y_copied, y_turned, added, logits_done, exp_done, route,
         weights_turned, weights_copied, consts_set, selector_loaded, selector_set) = (sem(f"{tag}_{n}") for n in names)

        AT_TURN, AT_LOGITS, AT_BACK, AT_STATISTICS, AT_ROWS, AT_WEIGHTS = 0, 3, 6, 8, 11, 11
        AT_EXP = AT_LOGITS + 1
        ROUTE_AT = {4: range(0, 2), 6: range(2, 6), 7: range(6, 9), 8: range(9, 12),
                    9: range(12, 16), 10: range(16, 19), 11: range(19, 20)}

        def rows_of(u):
            return TAIL_ROWS if u % 3 == 2 else P

        def back(b, u, first):
            if u >= 0:
                return b, u
            return None if first else (b - 1, UNITS + u)

        def run(sequence, engine):
            sequence(0, 0, True, True, True)
            sequence(1, 1, False, True, True)
            with engine.Fori(1, SEQS // 2 - 1) as i:
                sequence(2 * i, 0, False, True, True)
                sequence(2 * i + 1, 1, False, True, True)
            sequence(SEQS - 2, 0, False, True, False)
            sequence(SEQS - 1, 1, False, False, False)

        block = ctx.enter_context(nc.Block())

        @block.sync
        def _(sp):
            sp.dma_start(selector_raw[:, :, :], selector_dram).then_inc(selector_loaded, 16)

        @block.tensor
        def _(pe):
            def logits(b, q):
                pe.wait_ge(norm.lo_done, b + 1)
                for c in range(CH):
                    last = three_products(pe, logits_ps[:, c, :], norm.halves_chunk(q, c),
                                          (gate_hi[:, :], gate_lo[:, :]))
                last.then_inc(logits_done, 1)

            def turn_weights(b):
                pe.wait_ge(route, (b + 1) * ROUTE_STEPS)
                at_least(pe, added, b - 1)
                for c in range(CH):
                    last = pe.transpose(work_ps[0:2 * EXPERTS, c * P:(c + 1) * P], halves_sb[:, c, :].bitcast(F32),
                                        ident[:, :])
                last.then_inc(weights_turned, 1)

            def spread_unit(b, q, u):
                n = b * UNITS + u
                if u == 0:
                    pe.wait_ge(weights_copied, b + 1)
                at_least(pe, spread_done, n)
                pe.matmul(spread_ps[0:rows_of(u), :], selector[:, u, 0:rows_of(u)], weight_rows[q][:, :],
                          start=True, stop=True).then_inc(spread_turned, 1)

            def gate_unit(b, q, u):
                if u == 0:
                    pe.wait_ge(norm.lo_done, b + 1)
                at_least(pe, silu_done, b * UNITS + u - 1)
                three_products(pe, gate_ps[u % 2][0:rows_of(u), :], up_weights(u, 0), norm.halves(q))\
                    .then_inc(gate_done, 1)

            def up_unit(b, q, u):
                at_least(pe, act_done, b * UNITS + u - 2)
                three_products(pe, up_ps[u % 3][0:rows_of(u), :], up_weights(u, 1), norm.halves(q))\
                    .then_inc(up_done, 1)

            def up_weights(u, half):
                pair, kind = u // 3, u % 3
                if kind < 2:
                    return up_hi[:, 2 * pair + kind, half, :], up_lo[:, 2 * pair + kind, half, :]
                return upt_hi[:, pair, half, :], upt_lo[:, pair, half, :]

            def down_unit(b, u):
                pair, kind = u // 3, u % 3
                pe.wait_ge(act_lo_done, b * UNITS + u + 1)
                if kind < 2:
                    w = dn_hi[:, 2 * pair + kind, :], dn_lo[:, 2 * pair + kind, :]
                else:
                    w = dnt_hi[:, pair, :], dnt_lo[:, pair, :]
                if u == 0:
                    at_least(pe, y_copied, b)
                rows = rows_of(u)
                three_products(pe, y_ps[:, :], w, (act_hi[u % SLOTS][0:rows, :], act_lo[u % SLOTS][0:rows, :]),
                               start=(u == 0), stop=(u == UNITS - 1)).then_inc(down_done, 1)

            def turn_back(b, next1):
                pe.wait_ge(y_copied, b + 1)
                if next1:
                    pe.wait_ge(route, (b + 2) * ROUTE_STEPS + 2)
                for c in range(CH):
                    last = pe.transpose(work_ps[:, c * P:(c + 1) * P], y_sb[:, c * P:(c + 1) * P], ident[:, :])
                last.then_inc(y_turned, 1)

            def sequence(b, q, first, next1, next2):
                for u in range(UNITS):
                    gate_unit(b, q, u)
                    up_unit(b, q, u)
                    if u < UNITS - 1:
                        spread_unit(b, q, u + 1)
                    if next1 and u == AT_WEIGHTS:
                        turn_weights(b + 1)
                    down = back(b, u - DOWN_LAG, first)
                    if down:
                        down_unit(*down)
                    if next1 and u == UNITS - 1:
                        spread_unit(b + 1, 1 - q, 0)
                    if next1 and u == AT_TURN:
                        pe.wait_ge(weights_copied, b + 1)
                        norm.tensor_transposes(pe, b + 1)
                    if next1 and u == AT_LOGITS:
                        logits(b + 1, 1 - q)
                    if not first and u == AT_BACK:
                        turn_back(b - 1, next1)

            norm.tensor_transposes(pe, 0)
            logits(0, 0)
            turn_weights(0)
            pe.wait_ge(selector_set, 1)
            spread_unit(0, 0, 0)
            run(sequence, pe)
            for u in range(UNITS - DOWN_LAG, UNITS):
                down_unit(SEQS - 1, u)
            pe.wait_ge(added, SEQS - 1)
            turn_back(SEQS - 1, False)

        @block.scalar
        def _(act):
            def silu_unit(b, u):
                n = b * UNITS + u
                act.wait_ge(gate_done, n + 1)
                at_least(act, weighted_done, n - 1)
                rows = rows_of(u)
                act.activation(silu[u % 2][0:rows, :], gate_ps[u % 2][0:rows, :], ACT.Silu).then_inc(silu_done, 1)

            def round_unit(b, u):
                n = b * UNITS + u
                act.wait_ge(act_done, n + 1)
                at_least(act, down_done, n - SLOTS + 1)
                rows = rows_of(u)
                act.copy(act_hi[u % SLOTS][0:rows, :], act_f[u % 3][0:rows, :]).then_inc(act_hi_done, 1)

            def copy_spread(b, u):
                n = b * UNITS + u
                act.wait_ge(spread_turned, n + 1)
                at_least(act, weighted_done, n - 1)
                rows = rows_of(u)
                act.copy(spread[u % 2][0:rows, :], spread_ps[0:rows, :]).then_inc(spread_done, 1)

            def exponentials(b):
                act.wait_ge(route, b * ROUTE_STEPS + SHIFT_STEP)
                act.activation(r["exp"][:, :, :], r["shifted"][:, :, :], ACT.Exp).then_inc(exp_done, 1)

            def copy_weights(b, q):
                act.wait_ge(weights_turned, b + 1)
                act.copy(weight_rows[q][0:2 * EXPERTS, :], work_ps[0:2 * EXPERTS, :]).then_inc(weights_copied, 1)

            def copy_y(b):
                act.wait_ge(down_done, (b + 1) * UNITS)
                at_least(act, y_turned, b)
                act.copy(y_sb[:, :], y_ps[:, :]).then_inc(y_copied, 1)

            def sequence(b, q, first, next1, next2):
                for u in range(UNITS):
                    if not first and u == DOWN_LAG:
                        copy_y(b - 1)
                    silu_unit(b, u)
                    rounded = back(b, u - SPLIT_LAG, first)
                    if rounded:
                        round_unit(*rounded)
                    if next1 and u == AT_WEIGHTS:
                        copy_weights(b + 1, 1 - q)
                    if u < UNITS - 1 and u != AT_EXP + 1:
                        copy_spread(b, u + 1)
                    if next1 and u == UNITS - 1:
                        copy_spread(b + 1, 0)
                    if next1 and u == AT_TURN + 1:
                        norm.scalar_hi(act, b + 1, 1 - q)
                    if next1 and u == AT_EXP:
                        exponentials(b + 1)

            act.wait_ge(consts_set, 1)
            act.wait_ge(selector_loaded, 16)
            act.copy(selector[0:2 * EXPERTS, :, :], selector_raw[:, :, :]).then_inc(selector_set, 1)
            norm.scalar_hi(act, 0, 0)
            exponentials(0)
            copy_weights(0, 0)
            copy_spread(0, 0)
            run(sequence, act)
            for u in range(UNITS - SPLIT_LAG, UNITS):
                round_unit(SEQS - 1, u)
            copy_y(SEQS - 1)

        @block.vector
        def _(dve):
            def per_expert(t):
                return t[:, :].unsqueeze(2).to_broadcast([P, CH, EXPERTS])

            ranks = rank[:, :].unsqueeze(1).to_broadcast([P, CH, EXPERTS])

            def largest(of, top):
                return lambda: dve.tensor_reduce(s[top][:, :], r[of][:, :, :], AX.X, ALU.max)

            def compare(of, top, to):
                return lambda: dve.tensor_tensor(r[to][:, :, :], r[of][:, :, :], per_expert(s[top]), ALU.is_equal)

            def ranked(of, to):
                return lambda: dve.tensor_tensor(r[to][:, :, :], r[of][:, :, :], ranks, ALU.mult)

            def both_of(*parts):
                def step():
                    for part in parts:
                        last = part()
                    return last
                return step

            route_steps = [
                lambda: dve.tensor_reduce(s["max"][:, :], logits_ps, AX.X, ALU.max),
                lambda: dve.tensor_tensor(r["shifted"][:, :, :], logits_ps, per_expert(s["max"]), ALU.subtract),
                lambda: dve.tensor_reduce(s["sum"][:, :], r["exp"][:, :, :], AX.X, ALU.add),
                lambda: dve.reciprocal(s["rsum"][:, :], s["sum"][:, :]),
                lambda: dve.tensor_tensor(r["prob"][:, :, :], r["exp"][:, :, :], per_expert(s["rsum"]), ALU.mult),
                largest("prob", "top1"), compare("prob", "top1", "eq1"), ranked("eq1", "key1"),
                largest("key1", "first1"), compare("key1", "first1", "mask1"),
                lambda: dve.scalar_tensor_tensor(r["rest"][:, :, :], r["mask1"][:, :, :], -2.0, r["prob"][:, :, :],
                                                 ALU.mult, ALU.add),
                largest("rest", "top2"),
                both_of(compare("rest", "top2", "eq2"),
                        lambda: dve.scalar_tensor_tensor(s["den"][:, :], s["top1"][:, :], 1e-20, s["top2"][:, :],
                                                         ALU.add, ALU.add)),
                both_of(ranked("eq2", "key2"), lambda: dve.reciprocal(s["rden"][:, :], s["den"][:, :])),
                largest("key2", "first2"), compare("key2", "first2", "mask2"),
                lambda: dve.tensor_tensor(r["both"][:, :, :], r["mask1"][:, :, :], r["mask2"][:, :, :], ALU.add),
                lambda: dve.tensor_tensor(r["chosen"][:, :, :], r["both"][:, :, :], r["prob"][:, :, :], ALU.mult),
                both_of(*(lambda to=to: dve.tensor_tensor(to, r["chosen"][:, :, :], per_expert(s["rden"]), ALU.mult)
                          for to in (r["combine"][:, :, :], halves_sb[:, :, 0:EXPERTS]))),
                lambda: dve.tensor_tensor(halves_sb[:, :, EXPERTS:], r["combine"][:, :, :],
                                          halves_sb[:, :, 0:EXPERTS].bitcast(F32), ALU.subtract),
            ]
            assert len(route_steps) == ROUTE_STEPS

            def routing(b, steps):
                for n in steps:
                    if n == 0:
                        dve.wait_ge(logits_done, b + 1)
                    elif n == SHIFT_STEP:
                        dve.wait_ge(exp_done, b + 1)
                    else:
                        dve.wait_ge(route, b * ROUTE_STEPS + n)
                    if n == ROUTE_STEPS - 2:
                        at_least(dve, weights_turned, b)
                    route_steps[n]().then_inc(route, 1)

            def product_unit(b, u):
                n = b * UNITS + u
                dve.wait_ge(up_done, n + 1)
                dve.wait_ge(weighted_done, n + 1)
                at_least(dve, act_lo_done, n - 2)
                rows = rows_of(u)
                dve.tensor_tensor(act_f[u % 3][0:rows, :], weighted[u % 2][0:rows, :],
                                  up_ps[u % 3][0:rows, :], ALU.mult).then_inc(act_done, 1)

            def lo_unit(b, u):
                dve.wait_ge(act_hi_done, b * UNITS + u + 1)
                rows = rows_of(u)
                dve.tensor_tensor(act_lo[u % SLOTS][0:rows, :], act_f[u % 3][0:rows, :],
                                  act_hi[u % SLOTS][0:rows, :].bitcast(F32), ALU.subtract).then_inc(act_lo_done, 1)

            def copy_spread(b, u):
                n = b * UNITS + u
                dve.wait_ge(spread_turned, n + 1)
                at_least(dve, weighted_done, n - 1)
                dve.tensor_copy(spread[u % 2][0:rows_of(u), :], spread_ps[0:rows_of(u), :]).then_inc(spread_done, 1)

            def add_back(b):
                dve.wait_ge(y_turned, b + 1)
                dve.tensor_tensor(x_all[:, b, :, :], x_all[:, b, :, :],
                                  work_ps[:, :].rearrange("p (c d) -> p c d", c=CH), ALU.add).then_inc(added, 1)

            def sequence(b, q, first, next1, next2):
                for u in range(UNITS):
                    if u == AT_EXP + 1:
                        copy_spread(b, u + 1)
                    if next1:
                        if u == AT_TURN + 2:
                            norm.vector_lo(dve, b + 1, 1 - q)
                        if u in ROUTE_AT:
                            routing(b + 1, ROUTE_AT[u])
                    if not first and u == AT_BACK + 1:
                        add_back(b - 1)
                    if next2 and u == AT_STATISTICS:
                        norm.vector_statistics(dve, b + 2)
                        norm.vector_moments(dve, b + 2)
                    if next2 and u == AT_ROWS:
                        norm.vector_rows(dve, b + 2)
                    split = back(b, u - SPLIT_LAG, first)
                    if split:
                        lo_unit(*split)
                    product_unit(b, u)

            for e in range(EXPERTS):
                dve.memset(rank[:, e:e + 1], float(EXPERTS - e))
            dve.memset(selector[:, :, :].bitcast(F32), 0.0)
            for i in range(2):
                last = dve.memset(weight_rows[i][:, :].bitcast(F32), 0.0)
            last.then_inc(consts_set, 1)
            dve.wait_ge(consts_set, 1)
            norm.vector_statistics(dve, 0)
            norm.vector_moments(dve, 0)
            norm.vector_rows(dve, 0)
            norm.vector_lo(dve, 0, 0)
            routing(0, range(ROUTE_STEPS))
            norm.vector_statistics(dve, 1)
            norm.vector_moments(dve, 1)
            norm.vector_rows(dve, 1)
            run(sequence, dve)
            for u in range(UNITS - SPLIT_LAG, UNITS):
                lo_unit(SEQS - 1, u)
            add_back(SEQS - 1)

        @block.gpsimd
        def _(pool):
            def weigh_unit(b, u):
                n = b * UNITS + u
                pool.wait_ge(silu_done, n + 1)
                pool.wait_ge(spread_done, n + 1)
                at_least(pool, act_done, n - 1)
                rows = rows_of(u)
                pool.tensor_tensor(weighted[u % 2][0:rows, :], silu[u % 2][0:rows, :], spread[u % 2][0:rows, :],
                                   ALU.mult).then_inc(weighted_done, 1)

            norm.gpsimd_setup(pool)
            norm.gpsimd_rstd(pool, 0)
            norm.gpsimd_rstd(pool, 1)

            def sequence(b, q, first, next1, next2):
                for u in range(UNITS):
                    weigh_unit(b, u)
                    if next2 and u == AT_STATISTICS + 1:
                        norm.gpsimd_rstd(pool, b + 2)

            run(sequence, pool)


def linear_phase(nc, sem, x_all, ident, wq, wk, wv, wo, a, scalars, tag):
    with ExitStack() as ctx:
        space = Space(nc, ctx, tag)
        sb, ps = space.sb, space.ps
        work_ps = ps("work", [P, SEQ])
        q_ps = [ps(f"q{i}", [P, SEQ]) for i in range(2)]
        k_ps = [ps(f"k{i}", [P, SEQ]) for i in range(2)]
        v_ps = [ps(f"v{i}", [P, SEQ]) for i in range(2)]
        out_ps = ps("out", [P, CH, D])
        norm = Norm(nc, space, sem, x_all, ident, work_ps, in_time_order=True)
        bv, bo = sb("bv", [P, 1]), sb("bo", [P, D])
        q = [[sb(f"q{f}_{i}", [P, SEQ]) for i in range(2)] for f in range(2)]
        k = [[sb(f"k{f}_{i}", [P, SEQ]) for i in range(2)] for f in range(2)]
        v = [sb(f"v_sb{i}", [P, SEQ]) for i in range(2)]
        kv = [sb(f"kv{f}", [P, SEQ]) for f in range(2)]
        kv_sum = [sb(f"kv_sum{f}", [P, SEQ]) for f in range(2)]
        k_sum = [sb(f"k_sum{f}", [P, SEQ]) for f in range(2)]
        num = [sb(f"num{f}", [P, SEQ]) for f in range(2)]
        den = [sb(f"den{f}", [P, SEQ]) for f in range(2)]
        num_all, den_all, rden, o = (sb(n, [P, SEQ]) for n in ("num", "den", "rden", "o"))
        ones = sb("ones", [P, SEQ])
        o_hi, o_lo = sb("o_hi", [P, SEQ], F32R), sb("o_lo", [P, SEQ], F32R)
        spare = sb("pool_spare", [P, 1])

        names = ("consts_loaded", "ones_set", "k_projected", "v_projected", "q_projected", "k_done", "v_done", "q_done", "kv0_done", "kv1_done", "k_sum_done",
                 "kv_sum_done", "num_parts", "num_done", "den_parts", "den_done", "rden_done", "o_done",
                 "o_hi_done", "o_lo_done", "y_done", "bo_added", "x_done")
        (consts_loaded, ones_set, k_projected, v_projected, q_projected, k_done, v_done, q_done, kv0_done, kv1_done, k_sum_done, kv_sum_done, num_parts,
         num_done, den_parts, den_done, rden_done, o_done, o_hi_done, o_lo_done, y_done, bo_added, x_done) = (
            sem(f"{tag}_{n}") for n in names)

        def run(body, engine):
            body(0, 0, True, True, True)
            body(1, 1, False, True, True)
            with engine.Fori(1, SEQS // 2 - 1) as i:
                body(2 * i, 0, False, True, True)
                body(2 * i + 1, 1, False, True, True)
            body(SEQS - 2, 0, False, True, False)
            body(SEQS - 1, 1, False, False, False)

        block = ctx.enter_context(nc.Block())

        @block.sync
        def _(sp):
            sp.dma_start(bv[:, :], a["b_bv"]).then_inc(consts_loaded, 16)
            sp.dma_start(bo[:, :], a["b_bo"].partition_broadcast(P)).then_inc(consts_loaded, 16)

        @block.tensor
        def _(pe):
            def project(b, i):
                at_least(pe, v_done, b - 1)
                at_least(pe, q_done, b - 1)
                pe.wait_ge(norm.lo_done, b + 1)
                three_products(pe, k_ps[i][:, :], halves(wk), norm.halves(i)).then_inc(k_projected, 1)
                three_products(pe, v_ps[i][:, :], halves(wv), norm.halves(i)).then_inc(v_projected, 1)
                three_products(pe, q_ps[i][:, :], halves(wq), norm.halves(i)).then_inc(q_projected, 1)

            def project_out(b):
                at_least(pe, x_done, b)
                pe.wait_ge(o_lo_done, b + 1)
                for c in range(CH):
                    o_c = tuple(t[:, :].rearrange("r (p c) -> r c p", c=CH)[:, c, :] for t in (o_hi, o_lo))
                    last = three_products(pe, out_ps[:, c, :], o_c, halves(wo))
                last.then_inc(y_done, 1)

            def body(b, i, first, next1, next2):
                if next1:
                    project(b + 1, 1 - i)
                if not first:
                    project_out(b - 1)
                if next2:
                    norm.tensor_transposes(pe, b + 2)

            norm.tensor_transposes(pe, 0)
            project(0, 0)
            norm.tensor_transposes(pe, 1)
            run(body, pe)
            project_out(SEQS - 1)

        @block.scalar
        def _(act):
            def features(b, i):
                at_least(act, o_done, b - 1)
                act.wait_ge(k_projected, b + 1)
                act.activation(k[0][i][:, :], k_ps[i][:, :], ACT.Sigmoid, bias=scalars[:, 4:5], scale=scalars[:, 0:1])
                act.activation(k[1][i][:, :], k_ps[i][:, :], ACT.Sigmoid, bias=scalars[:, 5:6], scale=scalars[:, 1:2])\
                    .then_inc(k_done, 1)
                act.wait_ge(v_projected, b + 1)
                act.activation(v[i][:, :], v_ps[i][:, :], ACT.Identity, bias=bv[:, :]).then_inc(v_done, 1)
                act.wait_ge(q_projected, b + 1)
                act.activation(q[0][i][:, :], q_ps[i][:, :], ACT.Sigmoid, bias=scalars[:, 2:3], scale=scalars[:, 0:1])
                act.activation(q[1][i][:, :], q_ps[i][:, :], ACT.Sigmoid, bias=scalars[:, 3:4], scale=scalars[:, 1:2])\
                    .then_inc(q_done, 1)

            def body(b, i, first, next1, next2):
                if next1:
                    features(b + 1, 1 - i)
                if next2:
                    norm.scalar_hi(act, b + 2, i)
                act.wait_ge(o_done, b + 1)
                at_least(act, y_done, b)
                act.copy(o_hi[:, :], o[:, :]).then_inc(o_hi_done, 1)

            act.wait_ge(consts_loaded, 32)
            norm.scalar_hi(act, 0, 0)
            features(0, 0)
            norm.scalar_hi(act, 1, 1)
            run(body, act)

        @block.vector
        def _(dve):
            def split_o(b):
                dve.wait_ge(o_hi_done, b + 1)
                dve.tensor_tensor(o_lo[:, :], o[:, :], o_hi[:, :].bitcast(F32), ALU.subtract).then_inc(o_lo_done, 1)

            def add_out(b):
                dve.wait_ge(bo_added, b + 1)
                dve.wait_ge(y_done, b + 1)
                dve.tensor_tensor(x_all[:, b, :, :], x_all[:, b, :, :], out_ps[:, :, :], ALU.add)\
                    .then_inc(x_done, 1)

            def body(b, i, first, next1, next2):
                dve.wait_ge(k_done, b + 1)
                at_least(dve, den_done, b)
                for f in range(2):
                    last = dve.tensor_tensor_scan(k_sum[f][:, :], ones[:, :], k[f][i][:, :], 0.0, ALU.mult, ALU.add)
                last.then_inc(k_sum_done, 1)
                dve.wait_ge(v_done, b + 1)
                dve.tensor_tensor(kv[1][:, :], v[i][:, :], k[1][i][:, :], ALU.mult).then_inc(kv1_done, 1)
                if not first:
                    split_o(b - 1)
                dve.wait_ge(kv1_done, b + 1)
                dve.wait_ge(kv0_done, b + 1)
                for f in range(2):
                    last = dve.tensor_tensor_scan(kv_sum[f][:, :], ones[:, :], kv[f][:, :], 0.0, ALU.mult, ALU.add)
                last.then_inc(kv_sum_done, 1)
                if next2:
                    norm.vector_statistics(dve, b + 2)
                    norm.vector_moments(dve, b + 2)
                dve.wait_ge(q_done, b + 1)
                at_least(dve, num_done, b)
                dve.wait_ge(kv_sum_done, b + 1)
                for f in range(2):
                    last = dve.tensor_tensor(num[f][:, :], q[f][i][:, :], kv_sum[f][:, :], ALU.mult)
                last.then_inc(num_parts, 1)
                if not first:
                    add_out(b - 1)
                if next2:
                    norm.vector_rows(dve, b + 2)
                dve.wait_ge(den_done, b + 1)
                at_least(dve, o_done, b)
                dve.reciprocal(rden[:, :], den_all[:, :]).then_inc(rden_done, 1)
                if next2:
                    norm.vector_lo(dve, b + 2, i)

            dve.memset(ones[:, :], 1.0).then_inc(ones_set, 1)
            dve.wait_ge(ones_set, 1)
            dve.wait_ge(consts_loaded, 32)
            for b in range(2):
                norm.vector_statistics(dve, b)
                norm.vector_moments(dve, b)
                norm.vector_rows(dve, b)
                norm.vector_lo(dve, b, b)
            run(body, dve)
            split_o(SEQS - 1)
            add_out(SEQS - 1)

        @block.gpsimd
        def _(pool):
            def add_bias(b):
                pool.wait_ge(norm.rows_done, b + 1)
                pool.tensor_tensor(spare[:, :], norm.eps[:, 0:1], norm.eps[:, 0:1], ALU.add)
                pool.tensor_tensor(x_all[:, b, :, :], x_all[:, b, :, :],
                                   bo[:, :].unsqueeze(1).to_broadcast([P, CH, D]), ALU.add).then_inc(bo_added, 1)

            def first_product(b, i):
                pool.wait_ge(v_done, b + 1)
                at_least(pool, kv_sum_done, b)
                pool.tensor_tensor(kv[0][:, :], v[i][:, :], k[0][i][:, :], ALU.mult).then_inc(kv0_done, 1)

            def body(b, i, first, next1, next2):
                pool.wait_ge(q_done, b + 1)
                pool.wait_ge(k_sum_done, b + 1)
                for f in range(2):
                    last = pool.tensor_tensor(den[f][:, :], q[f][i][:, :], k_sum[f][:, :], ALU.mult)
                last.then_inc(den_parts, 1)
                if next2:
                    norm.gpsimd_rstd(pool, b + 2)
                pool.wait_ge(den_parts, b + 1)
                at_least(pool, rden_done, b)
                pool.tensor_tensor(den_all[:, :], den[0][:, :], den[1][:, :], ALU.add).then_inc(den_done, 1)
                pool.wait_ge(num_parts, b + 1)
                pool.tensor_tensor(num_all[:, :], num[0][:, :], num[1][:, :], ALU.add).then_inc(num_done, 1)
                if next1:
                    first_product(b + 1, 1 - i)
                pool.wait_ge(num_done, b + 1)
                pool.wait_ge(rden_done, b + 1)
                at_least(pool, o_lo_done, b)
                pool.tensor_tensor(o[:, :], num_all[:, :], rden[:, :], ALU.mult).then_inc(o_done, 1)
                add_bias(b)

            norm.gpsimd_setup(pool)
            pool.wait_ge(consts_loaded, 32)
            norm.gpsimd_rstd(pool, 0)
            norm.gpsimd_rstd(pool, 1)
            first_product(0, 0)
            run(body, pool)


def linear_weights(nc, sem, ctx, a):
    names = ("wq", "wk", "wv", "wo")
    out = {n: tuple(ctx.enter_context(nc.sbuf_tensor(f"b_{n}_{h}", [P, D], F32R)) for h in ("hi", "lo")) for n in names}
    scalars = ctx.enter_context(nc.sbuf_tensor("b_scalars", [P, 8], F32))
    with ExitStack() as local:
        def sb(name, shape):
            return local.enter_context(nc.sbuf_tensor(f"b_{name}", shape, F32))

        raw = {n: sb(f"{n}_raw", [P, D]) for n in ("wq0", "wq1", "wk0", "wk1", "wv", "wo")}
        diff = {n: sb(f"{n}_diff", [P, D]) for n in ("wq", "wk")}
        bias = {n: sb(f"{n}_raw", [P, 2]) for n in ("bq", "bk")}
        bias_diff = sb("bias_diff", [P, 2])
        beta = sb("beta", [P, 1])
        loaded, diff_done, hi_done, beta_done = (sem(f"b_weights_{n}") for n in ("loaded", "diff", "hi", "beta"))
        minus_done = sem("b_weights_minus")
        block = local.enter_context(nc.Block())

        @block.sync
        def _(sp):
            for n, t in raw.items():
                sp.dma_start(t[:, :], a[f"b_{n}"]).then_inc(loaded, 16)
            for n, t in bias.items():
                sp.dma_start(t[:, :], a[f"b_{n}"]).then_inc(loaded, 16)
            sp.dma_start(beta[:, :], a["b_beta"].partition_broadcast(P)).then_inc(loaded, 16)

        @block.scalar
        def _(act):
            act.wait_ge(loaded, 9 * 16)
            act.activation(scalars[:, 0:1], beta[:, :], ACT.Exp).then_inc(beta_done, 1)
            act.wait_ge(diff_done, 1)
            for n in names:
                last = act.copy(out[n][0][:, :], (diff[n] if n in diff else raw[n])[:, :])
            last.then_inc(hi_done, 1)

        @block.vector
        def _(dve):
            dve.wait_ge(loaded, 9 * 16)
            for n in diff:
                dve.tensor_tensor(diff[n][:, :], raw[f"{n}0"][:, :], raw[f"{n}1"][:, :], ALU.subtract)
            for j, n in enumerate(bias):
                last = dve.tensor_tensor(bias_diff[:, j:j + 1], bias[n][:, 0:1], bias[n][:, 1:2], ALU.subtract)
            last.then_inc(diff_done, 1)
            dve.wait_ge(diff_done, 1)
            dve.wait_ge(beta_done, 1)
            dve.tensor_scalar(scalars[:, 1:2], scalars[:, 0:1], -1.0, None, ALU.mult).then_inc(minus_done, 1)
            dve.wait_ge(minus_done, 1)
            for j in range(2):
                for sign in range(2):
                    dve.tensor_tensor(scalars[:, 2 + 2 * j + sign:3 + 2 * j + sign], bias_diff[:, j:j + 1],
                                      scalars[:, sign:sign + 1], ALU.mult)
            dve.wait_ge(hi_done, 1)
            for n in names:
                dve.tensor_tensor(out[n][1][:, :], (diff[n] if n in diff else raw[n])[:, :],
                                  out[n][0][:, :].bitcast(F32), ALU.subtract)
    return out, scalars


def run_phases(nc, sem, ctx, x_all, ident, a):
    b, scalars = linear_weights(nc, sem, ctx, a)
    f = split_weights(nc, sem, ctx, "ffn", [(n, a[n]) for n in ("gate", "up_main", "up_tail", "down_main", "down_tail")])
    s = split_weights(nc, sem, ctx, "a", [(n, a[n]) for n in ("a_wq", "a_wk", "a_wv", "a_wo")])
    attention_phase(nc, sem, x_all, ident, s["a_wq"], s["a_wk"], s["a_wv"], s["a_wo"], a, "a")
    experts = (f["gate"], (f["up_main"], f["up_tail"]), (f["down_main"], f["down_tail"]))
    ffn_phase(nc, sem, x_all, ident, *experts, a["selector"], "f1")
    linear_phase(nc, sem, x_all, ident, b["wq"], b["wk"], b["wv"], b["wo"], a, scalars, "b")
    ffn_phase(nc, sem, x_all, ident, *experts, a["selector"], "f2")


def split_weights(nc, sem, ctx, tag, loads):
    out = {}
    with ExitStack() as local:
        raws = {}
        for name, ap in loads:
            shape = [int(n) for n in ap.shape]
            out[name] = tuple(ctx.enter_context(nc.sbuf_tensor(f"{tag}_{name}_{h}", shape, F32R))
                              for h in ("hi", "lo"))
        for name, ap in loads:
            raws[name] = local.enter_context(nc.sbuf_tensor(f"{tag}_{name}_raw", [int(n) for n in ap.shape], F32))
        loaded = [sem(f"{tag}_{name}_loaded") for name, _ in loads]
        hi_done = sem(f"{tag}_weights_hi_done")
        lo_done = sem(f"{tag}_weights_lo_done")
        block = local.enter_context(nc.Block())

        def whole(t):
            return t[tuple(slice(None) for _ in t.shape)]

        @block.sync
        def _(sp):
            for (name, ap), done in zip(loads, loaded):
                sp.dma_start(whole(raws[name]), ap).then_inc(done, 16)

        @block.scalar
        def _(act):
            for (name, _), done in zip(loads, loaded):
                act.wait_ge(done, 16)
                act.copy(whole(out[name][0]), whole(raws[name])).then_inc(hi_done, 1)

        @block.vector
        def _(dve):
            for n, (name, _) in enumerate(loads):
                dve.wait_ge(hi_done, n + 1)
                dve.tensor_tensor(whole(out[name][1]), whole(raws[name]), whole(out[name][0]).bitcast(F32),
                                  ALU.subtract).then_inc(lo_done, 1)
    return out


def identity(nc, sem, ident):
    ready = sem("identity_ready")
    with nc.Block() as block:
        @block.gpsimd
        def _(pool):
            pool.memset(ident[:, :], 0.0).then_inc(ready, 1)
            pool.wait_ge(ready, 1)
            pool.affine_select(out=ident[:, :], in_=ident[:, :], compare_op=ALU.not_equal, fill=1.0, base=0,
                               pattern=[[-1, P]], channel_multiplier=1).then_inc(ready, 1)


def load_all(nc, sem, x_all, x):
    loaded = sem("x_loaded")
    with nc.Block() as block:
        @block.sync
        def _(sp):
            for b in range(SEQS):
                sp.dma_start(x_all[:, b, :, :], x[b].rearrange("(p c) d -> p c d", c=CH)).then_inc(loaded, 16)
            sp.wait_ge(loaded, 16 * SEQS)


def store_all(nc, sem, x_all, out):
    stored = sem("x_stored")
    with nc.Block() as block:
        @block.sync
        def _(sp):
            for b in range(SEQS):
                sp.dma_start(out[b].rearrange("(p c) d -> p c d", c=CH), x_all[:, b, :, :]).then_inc(stored, 16)
            sp.wait_ge(stored, 16 * SEQS)


def program(nc, a, out):
    with ExitStack() as ctx:
        def sem(name):
            return ctx.enter_context(nc.semaphore(name))

        x_all = ctx.enter_context(nc.sbuf_tensor("x_all", [P, SEQS, CH, D], F32))
        ident = ctx.enter_context(nc.sbuf_tensor("ident", [P, P], F32))
        identity(nc, sem, ident)
        load_all(nc, sem, x_all, a["x"])
        run_phases(nc, sem, ctx, x_all, ident, a)
        store_all(nc, sem, x_all, out)


def kernel(**inputs):
    import numpy as np
    import concourse.bacc as bacc
    from concourse.bass_utils import run_bass_kernel_spmd

    i = {name: np.asarray(value) for name, value in inputs.items()}
    heads, width = HEADS, D // HEADS

    def depth_major(w):
        return w.reshape(w.shape[:-1] + (2, heads // 2, width)).swapaxes(-1, -2).reshape(w.shape)

    w1 = i["L0_ffn_w1"].reshape(EXPERTS, D, 2, FFN).transpose(1, 0, 2, 3)
    up_tail = np.zeros((D, PAIRS, 2, TAIL_ROWS), w1.dtype)
    up_tail[..., :TAIL] = w1[:, 0::2, :, P:]
    up_tail[..., ODD_TAIL:] = w1[:, 1::2, :, P:]
    w2 = i["L0_ffn_w2"].transpose(1, 0, 2)
    down_tail = np.zeros((TAIL_ROWS, PAIRS, D), w2.dtype)
    down_tail[:TAIL] = w2[P:, 0::2]
    down_tail[ODD_TAIL:] = w2[P:, 1::2]
    selector = np.zeros((2, EXPERTS, PAIRS, 3, P), np.float32)
    for pair in range(PAIRS):
        for odd in range(2):
            selector[:, 2 * pair + odd, pair, odd] = 1
            selector[:, 2 * pair + odd, pair, 2, odd * ODD_TAIL:(odd + 1) * ODD_TAIL] = 1
    pair_first, pair_second = np.arange(D) // 2 * 2, np.arange(D) // 2 * 2 + 1
    laid_out = {
        "x": i["L0_attn_a_hidden_states"],
        "a_wq": depth_major(i["L0_attn_a_Wq"]), "a_bq": depth_major(i["L0_attn_a_bq"])[:, None],
        "a_wk": depth_major(i["L0_attn_a_Wk"]), "a_bk": depth_major(i["L0_attn_a_bk"])[:, None],
        "a_wv": i["L0_attn_a_Wv"], "a_bv": i["L0_attn_a_bv"][None],
        "a_wo": i["L0_attn_a_Wo"], "a_bo": i["L0_attn_a_bo"][None],
        "b_wq0": i["L0_attn_b_Wq"].T[:, pair_first], "b_wq1": i["L0_attn_b_Wq"].T[:, pair_second],
        "b_wk0": i["L0_attn_b_Wk"].T[:, pair_first], "b_wk1": i["L0_attn_b_Wk"].T[:, pair_second],
        "b_bq": np.stack([i["L0_attn_b_bq"][pair_first], i["L0_attn_b_bq"][pair_second]], 1),
        "b_bk": np.stack([i["L0_attn_b_bk"][pair_first], i["L0_attn_b_bk"][pair_second]], 1),
        "b_wv": i["L0_attn_b_Wv"].T, "b_bv": i["L0_attn_b_bv"][:, None],
        "b_wo": i["L0_attn_b_Wo"].T, "b_bo": i["L0_attn_b_bo"][None],
        "b_beta": i["L0_attn_b_beta"][None],
        "gate": i["L0_ffn_gate_w"].T,
        "up_main": w1[..., :P], "up_tail": up_tail,
        "down_main": w2[:P], "down_tail": down_tail,
        "selector": selector.reshape(2 * EXPERTS, UNITS, P),
    }
    nc = bacc.Bacc("TRN2", target_bir_lowering=False, num_devices=1)
    arrays, args = {}, {}
    for name, value in laid_out.items():
        value = np.ascontiguousarray(value)
        arrays[f"in_{name}"] = value
        args[name] = nc.dram_tensor(f"in_{name}", value.shape, F32, kind="ExternalInput").ap()
    out = nc.dram_tensor("out", (SEQS, SEQ, D), F32, kind="ExternalOutput").ap()
    program(nc, args, out)
    result = run_bass_kernel_spmd(nc, [arrays], core_ids=[0])
    return result.results[0]["out"]
```

```python
from contextlib import ExitStack

import concourse.bass as bass
from concourse import mybir

F32 = mybir.dt.float32
F32R = mybir.dt.float32r
ACT = mybir.ActivationFunctionType
ALU = mybir.AluOpType
AX = mybir.AxisListType

P = 128
SEQS, SEQ, D = 16, 512, 128
CH = SEQ // P
EPS = 1e-5

HEADS = 8
HEAD = D // HEADS

EXPERTS, FFN = 8, 176
UNITS = EXPERTS * FFN // P


def at_least(engine, semaphore, value):
    if isinstance(value, int) and value <= 0:
        return
    engine.wait_ge(semaphore, value)


def three_products(tensor, out, stationary, moving, start=True, stop=True):
    (s_hi, s_lo), (m_hi, m_lo) = stationary, moving
    tensor.matmul(out, s_hi, m_hi, start=start, stop=False)
    tensor.matmul(out, s_hi, m_lo, start=False, stop=False)
    return tensor.matmul(out, s_lo, m_hi, start=False, stop=stop)


def halves(w):
    return w[0][:, :], w[1][:, :]


class Space:

    def __init__(self, nc, ctx, tag):
        self.nc, self.ctx, self.tag = nc, ctx, tag

    def sb(self, name, shape, dt=F32):
        return self.ctx.enter_context(self.nc.sbuf_tensor(f"{self.tag}_{name}", shape, dt))

    def ps(self, name, shape, dt=F32):
        return self.ctx.enter_context(self.nc.psum_tensor(f"{self.tag}_{name}", shape, dt))


class Norm:

    def __init__(self, nc, space, sem, x_all, ident, transposed, in_time_order=False,
                 scalar_rows=False):
        self.in_time_order = in_time_order
        self.nc, self.x_all, self.ident = nc, x_all, ident
        self.stats = space.sb("ln_stats", [P, CH, 6])
        self.moments = space.sb("ln_moments", [P, CH, 2])
        self.shifted = space.sb("ln_shifted", [P, CH])
        self.spare = space.sb("ln_spare", [P, 1])
        self.eps = space.sb("ln_eps", [P, CH])
        self.power = space.sb("ln_power", [P, CH])
        self.rstd = space.sb("ln_rstd", [P, CH])
        self.rows = space.sb("ln_rows", [P, CH, D])
        self.transposed = transposed
        if scalar_rows:
            self.scaled_mean = space.sb("ln_scaled_mean", [P, CH])
            self.shift = space.sb("ln_shift", [P, CH])
            self.zero = space.sb("ln_zero", [P, CH])
            self.scaled_done = sem(f"{space.tag}_ln_scaled_done")
            self.shift_done = sem(f"{space.tag}_ln_shift_done")
        self.hi = [space.sb(f"xn_hi{i}", [P, SEQ], F32R) for i in range(2)]
        self.lo = [space.sb(f"xn_lo{i}", [P, SEQ], F32R) for i in range(2)]
        t = space.tag
        self.stats_done = sem(f"{t}_ln_stats_done")
        self.moments_done = sem(f"{t}_ln_moments_done")
        self.power_set = sem(f"{t}_ln_power_set")
        self.shifted_done = sem(f"{t}_ln_shifted_done")
        self.rstd_done = sem(f"{t}_ln_rstd_done")
        self.rows_done = sem(f"{t}_ln_rows_done")
        self.transposes_done = sem(f"{t}_ln_transposes_done")
        self.hi_done = sem(f"{t}_xn_hi_done")
        self.lo_done = sem(f"{t}_xn_lo_done")

    def halves(self, b_parity):
        return self.hi[b_parity][:, :], self.lo[b_parity][:, :]

    def halves_chunk(self, b_parity, c):
        return (self.hi[b_parity][:, c * P:(c + 1) * P], self.lo[b_parity][:, c * P:(c + 1) * P])

    def gpsimd_setup(self, pool):
        pool.memset(self.eps[:, :], EPS)
        pool.memset(self.power[:, :], -0.5).then_inc(self.power_set, 1)
        pool.wait_ge(self.power_set, 1)

    def vector_statistics(self, dve, b, chunks=range(CH)):
        for c in chunks:
            last = dve.bn_stats(self.stats[:, c, :], self.x_all[:, b, c, :])
        if c == CH - 1:
            last.then_inc(self.stats_done, 1)

    def vector_moments(self, dve, b):
        dve.wait_ge(self.stats_done, b + 1)
        dve.memset(self.spare[:, :], 0.0)
        for c in range(CH):
            last = dve.bn_aggr(self.moments[:, c, :], self.stats[:, c, :])
        last.then_inc(self.moments_done, 1)

    def gpsimd_rstd(self, pool, b):
        pool.wait_ge(self.moments_done, b + 1)
        pool.tensor_tensor(self.shifted[:, :], self.moments[:, :, 1], self.eps[:, :], ALU.add)\
            .then_inc(self.shifted_done, 1)
        pool.wait_ge(self.shifted_done, b + 1)
        pool.tensor_tensor(self.rstd[:, :], self.shifted[:, :], self.power[:, :], ALU.pow)\
            .then_inc(self.rstd_done, 1)

    def gpsimd_shift(self, pool, b):
        pool.wait_ge(self.rstd_done, b + 1)
        pool.tensor_tensor(self.scaled_mean[:, :], self.moments[:, :, 0], self.rstd[:, :], ALU.mult)\
            .then_inc(self.scaled_done, 1)
        pool.wait_ge(self.scaled_done, b + 1)
        pool.tensor_tensor(self.shift[:, :], self.zero[:, :], self.scaled_mean[:, :], ALU.subtract)\
            .then_inc(self.shift_done, 1)

    def scalar_rows(self, act, b):
        act.wait_ge(self.shift_done, b + 1)
        for c in range(CH):
            last = act.activation(self.rows[:, c, :], self.x_all[:, b, c, :], ACT.Identity,
                                  bias=self.shift[:, c:c + 1], scale=self.rstd[:, c:c + 1])
        last.then_inc(self.rows_done, 1)

    def vector_rows(self, dve, b, chunks=range(CH)):
        if 0 in chunks:
            dve.wait_ge(self.rstd_done, b + 1)
        for c in chunks:
            last = dve.tensor_scalar(self.rows[:, c, :], self.x_all[:, b, c, :], self.moments[:, c, 0:1],
                                     self.rstd[:, c:c + 1], ALU.subtract, ALU.mult)
        if c == CH - 1:
            last.then_inc(self.rows_done, 1)

    def tensor_transposes(self, pe, b):
        pe.wait_ge(self.rows_done, b + 1)
        at_least(pe, self.lo_done, b)
        for c in range(CH):
            last = pe.transpose(self.transposed[:, c * P:(c + 1) * P], self.rows[:, c, :], self.ident[:, :])
        last.then_inc(self.transposes_done, 1)

    def scalar_hi(self, act, b, parity):
        act.wait_ge(self.transposes_done, b + 1)
        act.copy(self.columns(self.hi[parity]), self.read_turned()).then_inc(self.hi_done, 1)

    def vector_lo(self, dve, b, parity):
        dve.wait_ge(self.hi_done, b + 1)
        dve.tensor_tensor(self.columns(self.lo[parity]), self.read_turned(),
                          self.columns(self.hi[parity]).bitcast(F32), ALU.subtract).then_inc(self.lo_done, 1)

    def read_turned(self):
        t = self.transposed[:, :]
        return t.rearrange("d (c p) -> d c p", c=CH) if self.in_time_order else t

    def columns(self, half):
        return half[:, :].rearrange("d (p c) -> d c p", c=CH) if self.in_time_order else half[:, :]


def attention_stacks(nc, ctx):
    return tuple([ctx.enter_context(nc.sbuf_tensor(f"{n}_stack{i}", [P, HEADS, SEQ], F32R)) for i in range(2)]
                 for n in ("q", "k"))


def attention_phase(nc, sem, x_all, ident, wq, wk, wv, wo, a, stacks, x_loaded, tag):
    M_ROW, M_END = 3 * HEAD, 3 * HEAD + 2
    ITEMS = HEADS * CH
    BURST, AT_BURST = 4, 1
    HALF = ITEMS // 2
    STACK_COUNT, MAX_COUNT = 16 * 7, 16 * 2
    AT_MAX, AT_PROJECT, AT_OUT0, AT_OUT1, AT_BACK, AT_Y = (1, 23), (10, 13, 16, 19), 27, 7, 11, 15
    FIRST_PROJECT, FIRST_TURN = (5, 8, 11, 14), 19
    with ExitStack() as ctx:
        space = Space(nc, ctx, tag)
        sb, ps = space.sb, space.ps
        max_ps = [ps(f"max{i}", [P, SEQ]) for i in range(3)]
        score_ps = [ps(f"score{i}", [P, SEQ]) for i in range(2)]
        pv_ps = ps("pv", [P, SEQ])
        work_ps = ps("work", [P, SEQ])
        out_ps = ps("out", [P, CH, D])
        norm = Norm(nc, space, sem, x_all, ident, work_ps)
        bq, bk = sb("bq", [P, 1]), sb("bk", [P, 1])
        bv, bo = sb("bv", [P, D]), sb("bo", [P, D])
        q_stack, k_stack = stacks
        zeros = sb("zeros", [2, SEQ])
        q_hi, q_lo, k_hi, k_lo = (sb(n, [P, SEQ], F32R) for n in ("q_hi", "q_lo", "k_hi", "k_lo"))
        v_rows = sb("v_rows", [P, CH, HEADS, HEAD])
        v_ones = [sb(f"v_ones{i}", [P, CH, HEADS, 32]) for i in range(2)]
        neg_max = sb("neg_max", [P, HEADS, CH])
        m_hi = [sb(f"m_hi{g}", [HALF, P], F32R) for g in range(2)]
        m_lo = [sb(f"m_lo{g}", [HALF, P], F32R) for g in range(2)]
        probs = [sb(f"probs{i}", [P, SEQ]) for i in range(2 * BURST)]
        pv = [sb(f"pv_sb{i}", [P, SEQ]) for i in range(2)]
        rsum = sb("rsum", [P, CH, 4])
        o_rows = sb("o_rows", [P, CH, D])
        o_hi, o_lo = sb("o_hi", [P, SEQ], F32R), sb("o_lo", [P, SEQ], F32R)
        spare = sb("pool_spare", [P, 1])

        names = ("consts_loaded", "consts_set", "v_ones_set", "q_proj", "k_proj", "v_proj", "q_hi_done", "q_lo_done",
                 "k_hi_done", "k_lo_done", "v_rows_done", "v_ones_done", "stack_loaded00", "stack_loaded01", "stack_loaded10",
                 "stack_loaded11", "max_scores",
                 "max_done", "max_turned", "m_hi_done", "m_lo_done", "m_loaded0", "m_loaded1", "scores", "exp_done",
                 "pv_done", "pv_copied", "o_turned", "rsum_done", "o_rows_done", "o_back", "o_hi_done",
                 "o_lo_done", "y_done", "bo_added", "x_done")
        (consts_loaded, consts_set, v_ones_set, q_proj, k_proj, v_proj, q_hi_done, q_lo_done, k_hi_done, k_lo_done,
         v_rows_done, v_ones_done, stack_loaded00, stack_loaded01,
         stack_loaded10, stack_loaded11, max_scores, max_done, max_turned, m_hi_done, m_lo_done,
         m_loaded0, m_loaded1, scores, exp_done, pv_done, pv_copied, o_turned, rsum_done, o_rows_done, o_back,
         o_hi_done, o_lo_done, y_done, bo_added, x_done) = (sem(f"{tag}_{n}") for n in names)
        CONSTS = 4 * 16
        stack_loaded = ((stack_loaded00, stack_loaded01), (stack_loaded10, stack_loaded11))
        m_loaded = (m_loaded0, m_loaded1)

        def stacked(turn, q):
            return STACK_COUNT * (turn + 1)

        def item(i):
            return i // 16 * 4 + i % 4, i % 16 // 4

        def run(body, engine):
            body(0, 0, 0, False, True, True)
            body(1, 1, 0, True, True, True)
            with engine.Fori(1, SEQS // 2 - 1) as turn:
                body(2 * turn, 0, turn, True, True, True)
                body(2 * turn + 1, 1, turn, True, True, True)
            body(SEQS - 2, 0, SEQS // 2 - 1, True, True, False)
            body(SEQS - 1, 1, SEQS // 2 - 1, True, False, False)

        block = ctx.enter_context(nc.Block())

        @block.sync
        def _(sp):
            sp.dma_start(bq[:, :], a["a_bq"]).then_inc(consts_loaded, 16)
            sp.dma_start(bk[:, :], a["a_bk"]).then_inc(consts_loaded, 16)
            sp.dma_start(bv[:, :], a["a_bv"].partition_broadcast(P)).then_inc(consts_loaded, 16)
            sp.dma_start(bo[:, :], a["a_bo"].partition_broadcast(P)).then_inc(consts_loaded, 16)

            def stack(b, q, group):
                heads = slice(4 * group, 4 * group + 4)
                done = stack_loaded[q][group]

                def restack(stacked_rows, row, half):
                    sp.dma_start(stacked_rows[row:row + HEAD, heads, :].bitcast(F32),
                                 half[group * 64:group * 64 + 64, :].bitcast(F32)).then_inc(done, 16)

                at_least(sp, scores, ITEMS * (b - 2) + HALF * (group + 1))
                sp.dma_start(q_stack[q][M_ROW:M_END, heads, :].bitcast(F32),
                             zeros[:, :].unsqueeze(1).to_broadcast([2, 4, SEQ])).then_inc(done, 16)
                sp.wait_ge(q_lo_done, b + 1)
                for row, half in ((0, q_hi), (HEAD, q_lo), (2 * HEAD, q_hi)):
                    restack(q_stack[q], row, half)
                sp.wait_ge(k_lo_done, b + 1)
                for row, half in ((0, k_hi), (HEAD, k_hi), (2 * HEAD, k_lo)):
                    restack(k_stack[q], row, half)

            def maxima(b, q, group):
                sp.wait_ge(m_lo_done, 2 * b + group + 1)
                for row, half in ((M_ROW, m_hi[group]), (M_ROW + 1, m_lo[group])):
                    sp.dma_start(q_stack[q][row:row + 1, 4 * group:4 * group + 4, :].bitcast(F32)
                                 .rearrange("r h (c t) -> r (h c) t", c=CH),
                                 half[:, :].bitcast(F32)).then_inc(m_loaded[group], 16)

            def body(b, q, turn, before, after1, after2):
                maxima(b, q, 1)
                if after1:
                    stack(b + 1, 1 - q, 1)
                if after2:
                    stack(b + 2, q, 0)
                if after1:
                    maxima(b + 1, 1 - q, 0)

            sp.wait_ge(consts_set, 1)
            stack(0, 0, 0)
            stack(0, 0, 1)
            stack(1, 1, 0)
            maxima(0, 0, 0)
            run(body, sp)

        @block.tensor
        def _(pe):
            def project(b, q, part):
                if part == 0:
                    at_least(pe, v_rows_done, b)
                    at_least(pe, m_lo_done, 2 * b - 2)
                    norm.tensor_transposes(pe, b)
                if part == 1:
                    pe.wait_ge(norm.lo_done, b + 1)
                    three_products(pe, work_ps[:, :], halves(wq), norm.halves(q)).then_inc(q_proj, 1)
                if part == 2:
                    pe.wait_ge(q_lo_done, b + 1)
                    three_products(pe, work_ps[:, :], halves(wk), norm.halves(q)).then_inc(k_proj, 1)
                if part == 3:
                    pe.wait_ge(k_lo_done, b + 1)
                    for c in range(CH):
                        last = three_products(pe, work_ps[:, c * P:(c + 1) * P], norm.halves_chunk(q, c), halves(wv))
                    last.then_inc(v_proj, 1)

            def largest(b, q, turn, j):
                h, c = j // CH, j % CH
                if j % HALF == 0:
                    pe.wait_ge(stack_loaded[q][j // HALF], stacked(turn, q))
                at_least(pe, max_done, b * ITEMS + j - (1 if j < 2 else 2))
                pe.matmul(max_ps[j % 3][:, :], q_stack[q][:, h, c * P:(c + 1) * P], k_stack[q][:, h, :],
                          start=True, stop=True).then_inc(max_scores, 1)

            def turn_max(b, group, projected=None):
                pe.wait_ge(max_done, ITEMS * b + HALF * (group + 1))
                if group:
                    pe.wait_ge(m_lo_done, 2 * b + 1)
                else:
                    pe.wait_ge(v_rows_done, projected)
                pe.transpose(work_ps[0:HALF, 0:P],
                             neg_max[:, 4 * group:4 * group + 4, :].rearrange("p h c -> p (h c)"), ident[:, :])\
                    .then_inc(max_turned, 1)

            def score(b, q, i):
                h, c = item(i)
                if i % HALF == 0:
                    pe.wait_ge(m_loaded[i // HALF], MAX_COUNT * (b + 1))
                at_least(pe, exp_done, b * ITEMS + i - 1)
                pe.matmul(score_ps[i % 2][:, :], k_stack[q][:, h, c * P:(c + 1) * P], q_stack[q][:, h, :],
                          start=True, stop=True).then_inc(scores, 1)

            def weigh(b, q, burst):
                for i in range(burst * BURST, (burst + 1) * BURST):
                    h, c = item(i)
                    group, side = h // 4, h % 4
                    if i == 0:
                        pe.wait_ge(v_ones_done, b + 1)
                    if i % HALF == 0:
                        at_least(pe, pv_copied, 2 * b + group)
                    pe.wait_ge(exp_done, b * ITEMS + i + 1)
                    pe.matmul(pv_ps[32 * side:32 * side + 32, :], v_ones[q][:, c, h, :],
                              probs[i % (2 * BURST)][:, :], start=(c == 0), stop=(c == CH - 1)).then_inc(pv_done, 1)

            def turn_out(b, group):
                pe.wait_ge(pv_copied, 2 * b + group + 1)
                if group:
                    pe.wait_ge(o_rows_done, 2 * b + 1)
                else:
                    at_least(pe, x_done, b)
                for c in range(CH):
                    last = pe.transpose(out_ps[:, c, :], pv[group][:, c * P:(c + 1) * P], ident[:, :])
                last.then_inc(o_turned, 1)

            def turn_back(b):
                pe.wait_ge(o_rows_done, 2 * b + 2)
                for c in range(CH):
                    last = pe.transpose(out_ps[:, c, :], o_rows[:, c, :], ident[:, :])
                last.then_inc(o_back, 1)

            def project_out(b):
                pe.wait_ge(o_lo_done, b + 1)
                for c in range(CH):
                    t = slice(c * P, (c + 1) * P)
                    last = three_products(pe, out_ps[:, c, :], (o_hi[:, t], o_lo[:, t]), halves(wo))
                last.then_inc(y_done, 1)

            def body(b, q, turn, before, after1, after2):
                for i in range(ITEMS):
                    score(b, q, i)
                    if after1:
                        largest(b + 1, 1 - q, turn + q, i)
                    if i % BURST == AT_BURST:
                        if i >= BURST:
                            weigh(b, q, i // BURST - 1)
                        elif before:
                            weigh(b - 1, 1 - q, ITEMS // BURST - 1)
                    if i == AT_MAX[0]:
                        turn_max(b, 1)
                    if after1 and i == AT_MAX[1]:
                        turn_max(b + 1, 0, b + 3 if after2 else SEQS)
                    if after2 and i in AT_PROJECT:
                        project(b + 2, q, AT_PROJECT.index(i))
                    if i == AT_OUT0:
                        turn_out(b, 0)
                    if before:
                        if i == AT_OUT1:
                            turn_out(b - 1, 1)
                        if i == AT_BACK:
                            turn_back(b - 1)
                        if i == AT_Y:
                            project_out(b - 1)

            for part in range(4):
                project(0, 0, part)
            for j in range(ITEMS):
                largest(0, 0, 0, j)
                if j in FIRST_PROJECT:
                    project(1, 1, FIRST_PROJECT.index(j))
                if j == FIRST_TURN:
                    turn_max(0, 0, 2)
            run(body, pe)
            weigh(SEQS - 1, 1, ITEMS // BURST - 1)
            turn_out(SEQS - 1, 1)
            turn_back(SEQS - 1)
            project_out(SEQS - 1)

        @block.scalar
        def _(act):
            def project(b, q, turn, part):
                if part == 0:
                    norm.scalar_hi(act, b, q)
                if part == 1:
                    act.wait_ge(q_proj, b + 1)
                    at_least(act, stack_loaded[1 - q][1], STACK_COUNT * (turn + q))
                    act.activation(q_hi[:, :], work_ps[:, :], ACT.Identity, bias=bq[:, :]).then_inc(q_hi_done, 1)
                if part == 2:
                    act.wait_ge(k_proj, b + 1)
                    act.activation(k_hi[:, :], work_ps[:, :], ACT.Identity, bias=bk[:, :]).then_inc(k_hi_done, 1)

                if part == 3:
                    act.wait_ge(v_proj, b + 1)
                    at_least(act, v_ones_done, b)
                    act.copy(v_rows[:, :, :, :].rearrange("p c h d -> p (c h d)"), work_ps[:, :])\
                        .then_inc(v_rows_done, 1)

            def round_max(b, group):
                act.wait_ge(max_turned, 2 * b + group + 1)
                at_least(act, m_loaded[group], MAX_COUNT * b)
                act.copy(m_hi[group][:, :], work_ps[0:HALF, 0:P]).then_inc(m_hi_done, 1)

            def exponential(b, i):
                n = b * ITEMS + i
                act.wait_ge(scores, n + 1)
                at_least(act, pv_done, n - 2 * BURST + 1)
                act.activation(probs[i % (2 * BURST)][:, :], score_ps[i % 2][:, :], ACT.Exp, scale=HEAD ** -0.5)\
                    .then_inc(exp_done, 1)

            def copy_pv(b, group):
                act.wait_ge(pv_done, b * ITEMS + 16 * (group + 1))
                at_least(act, o_turned, 2 * (b - 1) + group + 1)
                act.copy(pv[group][:, :], pv_ps[:, :]).then_inc(pv_copied, 1)

            def out_hi(b):
                act.wait_ge(o_back, b + 1)
                act.copy(o_hi[:, :], out_ps[:, :, :].rearrange("p c d -> p (c d)")).then_inc(o_hi_done, 1)

            def body(b, q, turn, before, after1, after2):
                for i in range(ITEMS):
                    exponential(b, i)
                    if i == AT_MAX[0]:
                        round_max(b, 1)
                    if before:
                        if i == 3:
                            copy_pv(b - 1, 1)
                        if i == AT_BACK + 1:
                            out_hi(b - 1)
                    if after2 and i - 1 in AT_PROJECT:
                        project(b + 2, q, turn + 1, AT_PROJECT.index(i - 1))
                    if i == HALF + 3:
                        copy_pv(b, 0)
                    if after1 and i == AT_MAX[1]:
                        round_max(b + 1, 0)

            act.wait_ge(consts_loaded, CONSTS)
            for b in range(2):
                for part in range(4):
                    project(b, b, 0, part)
            round_max(0, 0)
            run(body, act)
            copy_pv(SEQS - 1, 1)
            out_hi(SEQS - 1)

        @block.vector
        def _(dve):
            def project(b, q, part):
                if part == 0:
                    norm.vector_statistics(dve, b, (0, 1))
                if part == 1:
                    norm.vector_statistics(dve, b, (2, 3))
                if part == 2:
                    norm.vector_moments(dve, b)
                if 3 <= part < 7:
                    norm.vector_rows(dve, b, (part - 3,))
                if part == 7:
                    norm.vector_lo(dve, b, q)
                if part == 8:
                    dve.wait_ge(q_hi_done, b + 1)
                    dve.scalar_tensor_tensor(q_lo[:, :], work_ps[:, :], bq[:, :], q_hi[:, :].bitcast(F32),
                                             ALU.add, ALU.subtract).then_inc(q_lo_done, 1)
                if part == 9:
                    dve.wait_ge(k_hi_done, b + 1)
                    dve.scalar_tensor_tensor(k_lo[:, :], work_ps[:, :], bk[:, :], k_hi[:, :].bitcast(F32),
                                             ALU.add, ALU.subtract).then_inc(k_lo_done, 1)

            def find_max(b, j):
                h, c = j // CH, j % CH
                if j % HALF == 0:
                    at_least(dve, max_turned, 2 * b + j // HALF - 1)
                dve.wait_ge(max_scores, b * ITEMS + j + 1)
                dve.tensor_reduce(neg_max[:, h, c:c + 1], max_ps[j % 3][:, :], AX.X, ALU.max, negate=True)\
                    .then_inc(max_done, 1)

            def max_lo(b, group):
                dve.wait_ge(m_hi_done, 2 * b + group + 1)
                dve.tensor_tensor(m_lo[group][:, :], work_ps[0:HALF, 0:P], m_hi[group][:, :].bitcast(F32),
                                  ALU.subtract).then_inc(m_lo_done, 1)

            def normalise(b, group):
                n = 2 * b + group
                dve.wait_ge(o_turned, n + 1)
                heads = out_ps[:, :, :].rearrange("p c (h r) -> p c h r", r=32)
                dve.reciprocal(rsum[:, :, :], heads[:, :, :, 0]).then_inc(rsum_done, 1)
                dve.wait_ge(rsum_done, n + 1)
                half = o_rows[:, :, group * 64:group * 64 + 64].rearrange("p c (h d) -> p c h d", d=HEAD)
                dve.tensor_tensor(half, heads[:, :, :, 1:HEAD + 1],
                                  rsum[:, :, :].unsqueeze(3).to_broadcast([P, CH, 4, HEAD]), ALU.mult)\
                    .then_inc(o_rows_done, 1)

            def out_lo(b):
                dve.wait_ge(o_hi_done, b + 1)
                dve.tensor_tensor(o_lo[:, :], out_ps[:, :, :].rearrange("p c d -> p (c d)"),
                                  o_hi[:, :].bitcast(F32), ALU.subtract).then_inc(o_lo_done, 1)

            def add_out(b):
                dve.wait_ge(bo_added, b + 1)
                dve.wait_ge(y_done, b + 1)
                dve.tensor_tensor(x_all[:, b, :, :], x_all[:, b, :, :], out_ps[:, :, :], ALU.add)\
                    .then_inc(x_done, 1)

            def body(b, q, turn, before, after1, after2):
                for i in range(ITEMS):
                    if after1:
                        find_max(b + 1, i)
                    if before:
                        if i == AT_OUT1 + 1:
                            normalise(b - 1, 1)
                        if i == AT_BACK + 1:
                            out_lo(b - 1)
                        if i == AT_Y + 1:
                            add_out(b - 1)
                    if after2 and i in AT_SPLIT:
                        project(b + 2, q, AT_SPLIT.index(i))
                    if i == AT_OUT0 + 1:
                        normalise(b, 0)
                    if i == AT_MAX[0] + 1:
                        max_lo(b, 1)
                    if after1 and i == AT_MAX[1] + 1:
                        max_lo(b + 1, 0)

            FIRST_SPLIT = (0, 1, 2, 3, FIRST_PROJECT[0] + 1, FIRST_PROJECT[1] + 1, FIRST_PROJECT[2] + 1)
            AT_SPLIT = (0, 1, 2, 5, 6, 7, 8, AT_PROJECT[0] + 1, AT_PROJECT[1] + 1, AT_PROJECT[2] + 1)
            dve.memset(zeros[:, :], 0.0).then_inc(consts_set, 1)
            dve.wait_ge(x_loaded[0], 2 * 16)
            for part in range(len(AT_SPLIT)):
                if part == 8:
                    dve.wait_ge(consts_loaded, CONSTS)
                project(0, 0, part)
            for part in range(3):
                project(1, 1, part)
            for j in range(ITEMS):
                find_max(0, j)
                if j in FIRST_SPLIT:
                    project(1, 1, 3 + FIRST_SPLIT.index(j))
                if j == FIRST_TURN + 1:
                    max_lo(0, 0)
            dve.wait_ge(x_loaded[1], (SEQS - 2) * 16)
            run(body, dve)
            normalise(SEQS - 1, 1)
            out_lo(SEQS - 1)
            add_out(SEQS - 1)

        @block.gpsimd
        def _(pool):
            def copy_v(b, q):
                pool.wait_ge(v_rows_done, b + 1)
                at_least(pool, pv_done, ITEMS * (b - 1))
                pool.tensor_tensor(v_ones[q][:, :, :, 1:HEAD + 1], v_rows[:, :, :, :],
                                   bv[:, :].rearrange("p (h d) -> p h d", d=HEAD).unsqueeze(1)
                                   .to_broadcast([P, CH, HEADS, HEAD]), ALU.add).then_inc(v_ones_done, 1)

            def add_bias(b):
                pool.wait_ge(norm.rows_done, b + 1)
                at_least(pool, bo_added, b)
                pool.tensor_tensor(spare[:, :], norm.eps[:, 0:1], norm.eps[:, 0:1], ALU.add)
                pool.tensor_tensor(x_all[:, b, :, :], x_all[:, b, :, :],
                                   bo[:, :].unsqueeze(1).to_broadcast([P, CH, D]), ALU.add).then_inc(bo_added, 1)

            def body(b, q, turn, before, after1, after2):
                if after1:
                    copy_v(b + 1, 1 - q)
                if after2:
                    norm.gpsimd_rstd(pool, b + 2)
                    add_bias(b + 2)

            norm.gpsimd_setup(pool)
            norm.gpsimd_rstd(pool, 0)
            norm.gpsimd_rstd(pool, 1)
            for q in range(2):
                pool.memset(v_ones[q][:, :, :, 0:1], 1.0)
                last = pool.memset(v_ones[q][:, :, :, 1:32], 0.0)
            last.then_inc(v_ones_set, 1)
            pool.wait_ge(v_ones_set, 1)
            pool.wait_ge(consts_loaded, CONSTS)
            copy_v(0, 0)
            add_bias(0)
            add_bias(1)
            pool.wait_ge(x_loaded[1], (SEQS - 2) * 16)
            run(body, pool)


def ffn_phase(nc, sem, x_all, ident, gate, up, down, selector_dram, tag, out=None):
    gate_hi, gate_lo = gate
    up_hi, up_lo = up
    down_hi, down_lo = down
    ROUTE_STEPS, SHIFT_STEP = 20, 2
    SPLIT_LAG = 2
    DOWN_LAG = 4
    SLOTS = 6
    with ExitStack() as ctx:
        space = Space(nc, ctx, tag)
        gate_ps = [space.ps(f"gate{i}", [P, SEQ]) for i in range(2)]
        up_ps = [space.ps(f"up{i}", [P, SEQ]) for i in range(3)]
        y_ps = space.ps("y", [P, SEQ])
        spread_ps = space.ps("spread", [P, SEQ])
        work_ps = space.ps("work", [P, SEQ])
        logits_ps = work_ps[:, 0:CH * EXPERTS].rearrange("p (c e) -> p c e", c=CH)
        norm = Norm(nc, space, sem, x_all, ident, work_ps)
        silu = [space.sb(f"silu{i}", [P, SEQ]) for i in range(2)]
        spread = [space.sb(f"spread_sb{i}", [P, SEQ]) for i in range(2)]
        weighted = [space.sb(f"weighted{i}", [P, SEQ]) for i in range(2)]
        act_f = [space.sb(f"act{i}", [P, SEQ]) for i in range(3)]
        act_hi = [space.sb(f"act_hi{i}", [P, SEQ], F32R) for i in range(SLOTS)]
        act_lo = [space.sb(f"act_lo{i}", [P, SEQ], F32R) for i in range(SLOTS)]
        y_sb = space.sb("y_sb", [P, SEQ])
        r = {n: space.sb(f"r_{n}", [P, CH, EXPERTS]) for n in
             ("shifted", "exp", "prob", "eq1", "key1", "mask1", "rest", "eq2", "key2", "mask2",
              "both", "chosen", "combine")}
        s = {n: space.sb(f"s_{n}", [P, CH]) for n in
             ("max", "sum", "rsum", "top1", "first1", "top2", "first2", "den", "rden")}
        rank = space.sb("rank", [P, EXPERTS])
        halves_sb = space.sb("weight_halves", [P, CH, 2 * EXPERTS], F32R)
        weight_rows = [space.sb(f"weight_rows{i}", [P, SEQ], F32R) for i in range(2)]
        selector = space.sb("selector", [P, UNITS, P], F32R)
        selector_raw = space.sb("selector_raw", [2 * EXPERTS, UNITS, P])

        names = ("gate_done", "up_done", "silu_done", "spread_turned", "spread_done", "weighted_done", "act_done",
                 "act_hi_done", "act_lo_done", "down_done", "y_copied", "y_turned", "added",
                 "logits_done", "exp_done", "route", "weights_turned", "weights_copied", "consts_set",
                 "selector_loaded", "selector_set")
        (gate_done, up_done, silu_done, spread_turned, spread_done, weighted_done, act_done, act_hi_done,
         act_lo_done, down_done, y_copied, y_turned, added, logits_done, exp_done, route,
         weights_turned, weights_copied, consts_set, selector_loaded, selector_set) = (sem(f"{tag}_{n}") for n in names)

        AT_TURN, AT_LOGITS, AT_BACK, AT_STATISTICS, AT_ROWS, AT_WEIGHTS = 0, 3, 6, 7, 10, 10
        AT_EXP = AT_LOGITS + 1
        ROUTE_AT = {AT_EXP: range(0, 2), 5: range(2, 10), 6: range(10, 16), 7: range(16, 18), 8: range(18, 20)}

        stored = sem(f"{tag}_stored") if out is not None else None

        def last_use(u):
            return 2 if u < 2 else 3

        def back(b, u, first):
            if u >= 0:
                return b, u
            return None if first else (b - 1, UNITS + u)

        def run(sequence, engine):
            sequence(0, 0, True, True, True)
            sequence(1, 1, False, True, True)
            with engine.Fori(1, SEQS // 2 - 1) as i:
                sequence(2 * i, 0, False, True, True)
                sequence(2 * i + 1, 1, False, True, True)
            sequence(SEQS - 2, 0, False, True, False)
            sequence(SEQS - 1, 1, False, False, False)

        block = ctx.enter_context(nc.Block())

        @block.sync
        def _(sp):
            sp.dma_start(selector_raw[:, :, :], selector_dram).then_inc(selector_loaded, 16)
            if out is not None:
                for b in range(SEQS):
                    sp.wait_ge(added, b + 1)
                    sp.dma_start(out[b].rearrange("(p c) d -> p c d", c=CH), x_all[:, b, :, :]).then_inc(stored, 16)
                sp.wait_ge(stored, 16 * SEQS)

        @block.tensor
        def _(pe):
            def logits(b, q):
                pe.wait_ge(norm.lo_done, b + 1)
                for c in range(CH):
                    last = three_products(pe, logits_ps[:, c, :], norm.halves_chunk(q, c),
                                          (gate_hi[:, :], gate_lo[:, :]))
                last.then_inc(logits_done, 1)

            def turn_weights(b):
                pe.wait_ge(route, (b + 1) * ROUTE_STEPS)
                at_least(pe, added, b - 1)
                for c in range(CH):
                    last = pe.transpose(work_ps[0:2 * EXPERTS, c * P:(c + 1) * P], halves_sb[:, c, :].bitcast(F32),
                                        ident[:, :])
                last.then_inc(weights_turned, 1)

            def spread_unit(b, q, u):
                n = b * UNITS + u
                if u == 0:
                    pe.wait_ge(weights_copied, b + 1)
                at_least(pe, spread_done, n)
                pe.matmul(spread_ps[:, :], selector[:, u, :], weight_rows[q][:, :],
                          start=True, stop=True).then_inc(spread_turned, 1)

            def gate_unit(b, q, u):
                if u == 0:
                    pe.wait_ge(norm.lo_done, b + 1)
                at_least(pe, silu_done, b * UNITS + u - 1)
                three_products(pe, gate_ps[(q + u) % 2][:, :], up_weights(u, 0), norm.halves(q))\
                    .then_inc(gate_done, 1)

            def up_unit(b, q, u):
                at_least(pe, act_done, b * UNITS + u + 1 - last_use(u))
                three_products(pe, up_ps[u % 3][:, :], up_weights(u, 1), norm.halves(q))\
                    .then_inc(up_done, 1)

            def up_weights(u, half):
                return up_hi[:, u, half, :], up_lo[:, u, half, :]

            def down_unit(b, u):
                pe.wait_ge(act_lo_done, b * UNITS + u + 1)
                if u == 0:
                    at_least(pe, y_copied, b)
                three_products(pe, y_ps[:, :], (down_hi[:, u, :], down_lo[:, u, :]),
                               (act_hi[u % SLOTS][:, :], act_lo[u % SLOTS][:, :]),
                               start=(u == 0), stop=(u == UNITS - 1)).then_inc(down_done, 1)

            def turn_back(b, next1):
                pe.wait_ge(y_copied, b + 1)
                if next1:
                    pe.wait_ge(route, (b + 2) * ROUTE_STEPS + 2)
                for c in range(CH):
                    last = pe.transpose(work_ps[:, c * P:(c + 1) * P], y_sb[:, c * P:(c + 1) * P], ident[:, :])
                last.then_inc(y_turned, 1)

            def sequence(b, q, first, next1, next2):
                for u in range(UNITS):
                    if not first or u:
                        gate_unit(b, q, u)
                        up_unit(b, q, u)
                    if u < UNITS - 1:
                        spread_unit(b, q, u + 1)
                    if next1 and u == AT_WEIGHTS:
                        turn_weights(b + 1)
                    down = back(b, u - DOWN_LAG, first)
                    if down:
                        down_unit(*down)
                    if next1 and u == UNITS - 1:
                        spread_unit(b + 1, 1 - q, 0)
                    if next1 and u == AT_TURN:
                        pe.wait_ge(weights_copied, b + 1)
                        norm.tensor_transposes(pe, b + 1)
                    if next1 and u == AT_LOGITS:
                        logits(b + 1, 1 - q)
                    if not first and u == AT_BACK:
                        turn_back(b - 1, next1)

            norm.tensor_transposes(pe, 0)
            logits(0, 0)
            gate_unit(0, 0, 0)
            up_unit(0, 0, 0)
            turn_weights(0)
            pe.wait_ge(selector_set, 1)
            spread_unit(0, 0, 0)
            run(sequence, pe)
            for u in range(UNITS - DOWN_LAG, UNITS):
                down_unit(SEQS - 1, u)
            pe.wait_ge(added, SEQS - 1)
            turn_back(SEQS - 1, False)

        @block.scalar
        def _(act):
            def silu_unit(b, q, u):
                n = b * UNITS + u
                act.wait_ge(gate_done, n + 1)
                at_least(act, weighted_done, n - 1)
                act.activation(silu[(q + u) % 2][:, :], gate_ps[(q + u) % 2][:, :], ACT.Silu).then_inc(silu_done, 1)

            def round_unit(b, u):
                n = b * UNITS + u
                act.wait_ge(act_done, n + 1)
                at_least(act, down_done, n - SLOTS + 2)
                act.copy(act_hi[u % SLOTS][:, :], act_f[u % 3][:, :]).then_inc(act_hi_done, 1)

            def copy_spread(b, q, u):
                n = b * UNITS + u
                act.wait_ge(spread_turned, n + 1)
                at_least(act, weighted_done, n - 1)
                act.copy(spread[(q + u) % 2][:, :], spread_ps[:, :]).then_inc(spread_done, 1)

            def exponentials(b):
                act.wait_ge(route, b * ROUTE_STEPS + SHIFT_STEP)
                act.activation(r["exp"][:, :, :], r["shifted"][:, :, :], ACT.Exp).then_inc(exp_done, 1)

            def copy_weights(b, q):
                act.wait_ge(weights_turned, b + 1)
                act.copy(weight_rows[q][0:2 * EXPERTS, :], work_ps[0:2 * EXPERTS, :]).then_inc(weights_copied, 1)

            def copy_y(b):
                act.wait_ge(down_done, (b + 1) * UNITS)
                at_least(act, y_turned, b)
                act.copy(y_sb[:, :], y_ps[:, :]).then_inc(y_copied, 1)

            def sequence(b, q, first, next1, next2):
                for u in range(UNITS):
                    if not first and u == DOWN_LAG:
                        copy_y(b - 1)
                    rounded = back(b, u - SPLIT_LAG, first)
                    if rounded and u not in (AT_EXP + 1, AT_WEIGHTS):
                        round_unit(*rounded)
                    if not first or u:
                        silu_unit(b, q, u)
                    if next1 and u == AT_WEIGHTS:
                        copy_weights(b + 1, 1 - q)
                    if u == AT_WEIGHTS:
                        round_unit(*rounded)
                    if u < UNITS - 1 and u != AT_EXP + 1:
                        copy_spread(b, q, u + 1)
                    if next1 and u == UNITS - 1:
                        copy_spread(b + 1, 1 - q, 0)
                    if next1 and u == AT_TURN + 1:
                        norm.scalar_hi(act, b + 1, 1 - q)
                    if next1 and u == AT_EXP:
                        exponentials(b + 1)
                    if u == AT_EXP:
                        round_unit(b, u + 1 - SPLIT_LAG)

            norm.scalar_hi(act, 0, 0)
            act.wait_ge(consts_set, 1)
            act.wait_ge(selector_loaded, 16)
            act.copy(selector[0:2 * EXPERTS, :, :], selector_raw[:, :, :]).then_inc(selector_set, 1)
            exponentials(0)
            silu_unit(0, 0, 0)
            copy_weights(0, 0)
            copy_spread(0, 0, 0)
            run(sequence, act)
            for u in range(UNITS - SPLIT_LAG, UNITS):
                round_unit(SEQS - 1, u)
            copy_y(SEQS - 1)

        @block.vector
        def _(dve):
            def per_expert(t):
                return t[:, :].unsqueeze(2).to_broadcast([P, CH, EXPERTS])

            ranks = rank[:, :].unsqueeze(1).to_broadcast([P, CH, EXPERTS])

            def largest(of, top):
                return lambda: dve.tensor_reduce(s[top][:, :], r[of][:, :, :], AX.X, ALU.max)

            def compare(of, top, to):
                return lambda: dve.tensor_tensor(r[to][:, :, :], r[of][:, :, :], per_expert(s[top]), ALU.is_equal)

            def ranked(of, to):
                return lambda: dve.tensor_tensor(r[to][:, :, :], r[of][:, :, :], ranks, ALU.mult)

            def both_of(*parts):
                def step():
                    for part in parts:
                        last = part()
                    return last
                return step

            route_steps = [
                lambda: dve.tensor_reduce(s["max"][:, :], logits_ps, AX.X, ALU.max),
                lambda: dve.tensor_tensor(r["shifted"][:, :, :], logits_ps, per_expert(s["max"]), ALU.subtract),
                lambda: dve.tensor_reduce(s["sum"][:, :], r["exp"][:, :, :], AX.X, ALU.add),
                lambda: dve.reciprocal(s["rsum"][:, :], s["sum"][:, :]),
                lambda: dve.tensor_tensor(r["prob"][:, :, :], r["exp"][:, :, :], per_expert(s["rsum"]), ALU.mult),
                largest("prob", "top1"), compare("prob", "top1", "eq1"), ranked("eq1", "key1"),
                largest("key1", "first1"), compare("key1", "first1", "mask1"),
                lambda: dve.scalar_tensor_tensor(r["rest"][:, :, :], r["mask1"][:, :, :], -2.0, r["prob"][:, :, :],
                                                 ALU.mult, ALU.add),
                largest("rest", "top2"),
                both_of(compare("rest", "top2", "eq2"),
                        lambda: dve.scalar_tensor_tensor(s["den"][:, :], s["top1"][:, :], 1e-20, s["top2"][:, :],
                                                         ALU.add, ALU.add)),
                both_of(ranked("eq2", "key2"), lambda: dve.reciprocal(s["rden"][:, :], s["den"][:, :])),
                largest("key2", "first2"), compare("key2", "first2", "mask2"),
                lambda: dve.tensor_tensor(r["both"][:, :, :], r["mask1"][:, :, :], r["mask2"][:, :, :], ALU.add),
                lambda: dve.tensor_tensor(r["chosen"][:, :, :], r["both"][:, :, :], r["prob"][:, :, :], ALU.mult),
                both_of(*(lambda to=to: dve.tensor_tensor(to, r["chosen"][:, :, :], per_expert(s["rden"]), ALU.mult)
                          for to in (r["combine"][:, :, :], halves_sb[:, :, 0:EXPERTS]))),
                lambda: dve.tensor_tensor(halves_sb[:, :, EXPERTS:], r["combine"][:, :, :],
                                          halves_sb[:, :, 0:EXPERTS].bitcast(F32), ALU.subtract),
            ]
            assert len(route_steps) == ROUTE_STEPS

            def routing(b, steps):
                for n in steps:
                    if n == 0:
                        dve.wait_ge(logits_done, b + 1)
                    elif n == SHIFT_STEP:
                        dve.wait_ge(exp_done, b + 1)
                    else:
                        dve.wait_ge(route, b * ROUTE_STEPS + n)
                    if n == ROUTE_STEPS - 2:
                        at_least(dve, weights_turned, b)
                    route_steps[n]().then_inc(route, 1)

            def product_unit(b, q, u):
                n = b * UNITS + u
                dve.wait_ge(up_done, n + 1)
                dve.wait_ge(weighted_done, n + 1)
                at_least(dve, act_lo_done, n + 1 - last_use(u))
                dve.tensor_tensor(act_f[u % 3][:, :], weighted[(q + u) % 2][:, :],
                                  up_ps[u % 3][:, :], ALU.mult).then_inc(act_done, 1)

            def lo_unit(b, u):
                dve.wait_ge(act_hi_done, b * UNITS + u + 1)
                dve.tensor_tensor(act_lo[u % SLOTS][:, :], act_f[u % 3][:, :],
                                  act_hi[u % SLOTS][:, :].bitcast(F32), ALU.subtract).then_inc(act_lo_done, 1)

            def copy_spread(b, q, u):
                n = b * UNITS + u
                dve.wait_ge(spread_turned, n + 1)
                at_least(dve, weighted_done, n - 1)
                dve.tensor_copy(spread[(q + u) % 2][:, :], spread_ps[:, :]).then_inc(spread_done, 1)

            def add_back(b):
                dve.wait_ge(y_turned, b + 1)
                dve.tensor_tensor(x_all[:, b, :, :], x_all[:, b, :, :],
                                  work_ps[:, :].rearrange("p (c d) -> p c d", c=CH), ALU.add).then_inc(added, 1)

            def sequence(b, q, first, next1, next2):
                for u in range(UNITS):
                    if u == AT_EXP + 1:
                        copy_spread(b, q, u + 1)
                    split = back(b, u - SPLIT_LAG, first)
                    if split:
                        lo_unit(*split)
                    if next1:
                        if u == AT_TURN + 2:
                            norm.vector_lo(dve, b + 1, 1 - q)
                        if u in ROUTE_AT:
                            routing(b + 1, ROUTE_AT[u])
                    if not first and u == AT_BACK + 1:
                        add_back(b - 1)
                    if next2 and u == AT_STATISTICS + 1:
                        norm.vector_moments(dve, b + 2)
                    if next2 and u == AT_ROWS:
                        norm.vector_rows(dve, b + 2)
                    if next2 and u == AT_STATISTICS:
                        norm.vector_statistics(dve, b + 2)
                    product_unit(b, q, u)

            for e in range(EXPERTS):
                dve.memset(rank[:, e:e + 1], float(EXPERTS - e))
            norm.vector_statistics(dve, 0)
            norm.vector_moments(dve, 0)
            norm.vector_rows(dve, 0)
            norm.vector_lo(dve, 0, 0)
            routing(0, range(ROUTE_STEPS))
            norm.vector_statistics(dve, 1)
            norm.vector_moments(dve, 1)
            norm.vector_rows(dve, 1)
            run(sequence, dve)
            for u in range(UNITS - SPLIT_LAG, UNITS):
                lo_unit(SEQS - 1, u)
            add_back(SEQS - 1)

        @block.gpsimd
        def _(pool):
            def weigh_unit(b, q, u):
                n = b * UNITS + u
                pool.wait_ge(silu_done, n + 1)
                pool.wait_ge(spread_done, n + 1)
                at_least(pool, act_done, n - 1)
                pool.tensor_tensor(weighted[(q + u) % 2][:, :], silu[(q + u) % 2][:, :], spread[(q + u) % 2][:, :],
                                   ALU.mult).then_inc(weighted_done, 1)

            norm.gpsimd_setup(pool)
            norm.gpsimd_rstd(pool, 0)
            pool.memset(selector[:, :, :].bitcast(F32), 0.0)
            for i in range(2):
                last = pool.memset(weight_rows[i][:, :].bitcast(F32), 0.0)
            last.then_inc(consts_set, 1)
            norm.gpsimd_rstd(pool, 1)

            def sequence(b, q, first, next1, next2):
                for u in range(UNITS):
                    weigh_unit(b, q, u)
                    if next2 and u == AT_STATISTICS + 2:
                        norm.gpsimd_rstd(pool, b + 2)

            run(sequence, pool)


def linear_phase(nc, sem, x_all, ident, wq, wk, wv, wo, a, scalars, tag):
    with ExitStack() as ctx:
        space = Space(nc, ctx, tag)
        sb, ps = space.sb, space.ps
        work_ps = ps("work", [P, SEQ])
        q_ps = [ps(f"q{i}", [P, SEQ]) for i in range(2)]
        k_ps = [ps(f"k{i}", [P, SEQ]) for i in range(2)]
        v_ps = [ps(f"v{i}", [P, SEQ]) for i in range(2)]
        out_ps = ps("out", [P, CH, D])
        norm = Norm(nc, space, sem, x_all, ident, work_ps, in_time_order=True, scalar_rows=True)
        bv, bo = sb("bv", [P, 1]), sb("bo", [P, D])
        q = [[sb(f"q{f}_{i}", [P, SEQ]) for i in range(2)] for f in range(2)]
        k = [[sb(f"k{f}_{i}", [P, SEQ]) for i in range(2)] for f in range(2)]
        v = [sb(f"v_sb{i}", [P, SEQ]) for i in range(2)]
        kv = [sb(f"kv{f}", [P, SEQ]) for f in range(2)]
        kv_sum = [sb(f"kv_sum{f}", [P, SEQ]) for f in range(2)]
        k_sum = [sb(f"k_sum{f}", [P, SEQ]) for f in range(2)]
        num = [sb(f"num{f}", [P, SEQ]) for f in range(2)]
        den = [sb(f"den{f}", [P, SEQ]) for f in range(2)]
        num_all, den_all, rden, o = (sb(n, [P, SEQ]) for n in ("num", "den", "rden", "o"))
        ones = sb("ones", [P, SEQ])
        o_hi, o_lo = sb("o_hi", [P, SEQ], F32R), sb("o_lo", [P, SEQ], F32R)
        spare = sb("pool_spare", [P, 1])

        names = ("consts_loaded", "ones_set", "k_projected", "v_projected", "q_projected", "k_done", "v_done", "q_done", "kv0_done", "kv1_done", "k_sum_done",
                 "kv_sum_done", "num_parts", "num_done", "den_parts", "den_done", "rden_done", "o_done",
                 "o_hi_done", "o_lo_done", "y_done", "bo_added", "x_done")
        (consts_loaded, ones_set, k_projected, v_projected, q_projected, k_done, v_done, q_done, kv0_done, kv1_done, k_sum_done, kv_sum_done, num_parts,
         num_done, den_parts, den_done, rden_done, o_done, o_hi_done, o_lo_done, y_done, bo_added, x_done) = (
            sem(f"{tag}_{n}") for n in names)

        def run(body, engine):
            body(0, 0, True, True, True)
            body(1, 1, False, True, True)
            with engine.Fori(1, SEQS // 2 - 1) as i:
                body(2 * i, 0, False, True, True)
                body(2 * i + 1, 1, False, True, True)
            body(SEQS - 2, 0, False, True, False)
            body(SEQS - 1, 1, False, False, False)

        block = ctx.enter_context(nc.Block())

        @block.sync
        def _(sp):
            sp.dma_start(bv[:, :], a["b_bv"]).then_inc(consts_loaded, 16)
            sp.dma_start(bo[:, :], a["b_bo"].partition_broadcast(P)).then_inc(consts_loaded, 16)

        @block.tensor
        def _(pe):
            def project(b, i):
                at_least(pe, v_done, b - 1)
                at_least(pe, q_done, b - 1)
                pe.wait_ge(norm.lo_done, b + 1)
                three_products(pe, k_ps[i][:, :], halves(wk), norm.halves(i)).then_inc(k_projected, 1)
                three_products(pe, v_ps[i][:, :], halves(wv), norm.halves(i)).then_inc(v_projected, 1)
                three_products(pe, q_ps[i][:, :], halves(wq), norm.halves(i)).then_inc(q_projected, 1)

            def project_out(b):
                at_least(pe, x_done, b)
                pe.wait_ge(o_lo_done, b + 1)
                for c in range(CH):
                    o_c = tuple(t[:, :].rearrange("r (p c) -> r c p", c=CH)[:, c, :] for t in (o_hi, o_lo))
                    last = three_products(pe, out_ps[:, c, :], o_c, halves(wo))
                last.then_inc(y_done, 1)

            def body(b, i, first, next1, next2):
                if next1:
                    project(b + 1, 1 - i)
                if not first:
                    project_out(b - 1)
                if next2:
                    norm.tensor_transposes(pe, b + 2)

            norm.tensor_transposes(pe, 0)
            project(0, 0)
            norm.tensor_transposes(pe, 1)
            run(body, pe)
            project_out(SEQS - 1)

        @block.scalar
        def _(act):
            def features(b, i):
                at_least(act, o_done, b - 1)
                act.wait_ge(k_projected, b + 1)
                act.activation(k[0][i][:, :], k_ps[i][:, :], ACT.Sigmoid, bias=scalars[:, 4:5], scale=scalars[:, 0:1])
                act.activation(k[1][i][:, :], k_ps[i][:, :], ACT.Sigmoid, bias=scalars[:, 5:6], scale=scalars[:, 1:2])\
                    .then_inc(k_done, 1)
                act.wait_ge(v_projected, b + 1)
                act.activation(v[i][:, :], v_ps[i][:, :], ACT.Identity, bias=bv[:, :]).then_inc(v_done, 1)
                act.wait_ge(q_projected, b + 1)
                act.activation(q[0][i][:, :], q_ps[i][:, :], ACT.Sigmoid, bias=scalars[:, 2:3], scale=scalars[:, 0:1])
                act.activation(q[1][i][:, :], q_ps[i][:, :], ACT.Sigmoid, bias=scalars[:, 3:4], scale=scalars[:, 1:2])\
                    .then_inc(q_done, 1)

            def body(b, i, first, next1, next2):
                if next1:
                    features(b + 1, 1 - i)
                if next2:
                    norm.scalar_rows(act, b + 2)
                    norm.scalar_hi(act, b + 2, i)
                act.wait_ge(o_done, b + 1)
                at_least(act, y_done, b)
                act.copy(o_hi[:, :], o[:, :]).then_inc(o_hi_done, 1)

            act.wait_ge(consts_loaded, 32)
            norm.scalar_rows(act, 0)
            norm.scalar_hi(act, 0, 0)
            features(0, 0)
            norm.scalar_rows(act, 1)
            norm.scalar_hi(act, 1, 1)
            run(body, act)

        @block.vector
        def _(dve):
            def split_o(b):
                dve.wait_ge(o_hi_done, b + 1)
                dve.tensor_tensor(o_lo[:, :], o[:, :], o_hi[:, :].bitcast(F32), ALU.subtract).then_inc(o_lo_done, 1)

            def add_out(b):
                dve.wait_ge(bo_added, b + 1)
                dve.wait_ge(y_done, b + 1)
                dve.tensor_tensor(x_all[:, b, :, :], x_all[:, b, :, :], out_ps[:, :, :], ALU.add)\
                    .then_inc(x_done, 1)

            def body(b, i, first, next1, next2):
                dve.wait_ge(k_done, b + 1)
                at_least(dve, den_done, b)
                for f in range(2):
                    last = dve.tensor_tensor_scan(k_sum[f][:, :], ones[:, :], k[f][i][:, :], 0.0, ALU.mult, ALU.add)
                last.then_inc(k_sum_done, 1)
                dve.wait_ge(v_done, b + 1)
                dve.tensor_tensor(kv[1][:, :], v[i][:, :], k[1][i][:, :], ALU.mult).then_inc(kv1_done, 1)
                if not first:
                    split_o(b - 1)
                dve.wait_ge(kv1_done, b + 1)
                dve.wait_ge(kv0_done, b + 1)
                for f in range(2):
                    last = dve.tensor_tensor_scan(kv_sum[f][:, :], ones[:, :], kv[f][:, :], 0.0, ALU.mult, ALU.add)
                last.then_inc(kv_sum_done, 1)
                if next2:
                    norm.vector_statistics(dve, b + 2)
                    norm.vector_moments(dve, b + 2)
                dve.wait_ge(q_done, b + 1)
                at_least(dve, num_done, b)
                dve.wait_ge(kv_sum_done, b + 1)
                for f in range(2):
                    last = dve.tensor_tensor(num[f][:, :], q[f][i][:, :], kv_sum[f][:, :], ALU.mult)
                last.then_inc(num_parts, 1)
                dve.wait_ge(den_done, b + 1)
                at_least(dve, o_done, b)
                dve.reciprocal(rden[:, :], den_all[:, :]).then_inc(rden_done, 1)
                if not first:
                    add_out(b - 1)
                if next2:
                    norm.vector_lo(dve, b + 2, i)

            dve.memset(ones[:, :], 1.0).then_inc(ones_set, 1)
            dve.wait_ge(ones_set, 1)
            dve.wait_ge(consts_loaded, 32)
            for b in range(2):
                norm.vector_statistics(dve, b)
                norm.vector_moments(dve, b)
                norm.vector_lo(dve, b, b)
            run(body, dve)
            split_o(SEQS - 1)
            add_out(SEQS - 1)

        @block.gpsimd
        def _(pool):
            def add_bias(b):
                pool.wait_ge(norm.rows_done, b + 1)
                pool.tensor_tensor(spare[:, :], norm.eps[:, 0:1], norm.eps[:, 0:1], ALU.add)
                pool.tensor_tensor(x_all[:, b, :, :], x_all[:, b, :, :],
                                   bo[:, :].unsqueeze(1).to_broadcast([P, CH, D]), ALU.add).then_inc(bo_added, 1)

            def first_product(b, i):
                pool.wait_ge(v_done, b + 1)
                at_least(pool, kv_sum_done, b)
                pool.tensor_tensor(kv[0][:, :], v[i][:, :], k[0][i][:, :], ALU.mult).then_inc(kv0_done, 1)

            def body(b, i, first, next1, next2):
                pool.wait_ge(q_done, b + 1)
                pool.wait_ge(k_sum_done, b + 1)
                for f in range(2):
                    last = pool.tensor_tensor(den[f][:, :], q[f][i][:, :], k_sum[f][:, :], ALU.mult)
                last.then_inc(den_parts, 1)
                pool.wait_ge(den_parts, b + 1)
                at_least(pool, rden_done, b)
                pool.tensor_tensor(den_all[:, :], den[0][:, :], den[1][:, :], ALU.add).then_inc(den_done, 1)
                if next2:
                    norm.gpsimd_rstd(pool, b + 2)
                    norm.gpsimd_shift(pool, b + 2)
                pool.wait_ge(num_parts, b + 1)
                pool.tensor_tensor(num_all[:, :], num[0][:, :], num[1][:, :], ALU.add).then_inc(num_done, 1)
                if next1:
                    first_product(b + 1, 1 - i)
                pool.wait_ge(num_done, b + 1)
                pool.wait_ge(rden_done, b + 1)
                at_least(pool, o_lo_done, b)
                pool.tensor_tensor(o[:, :], num_all[:, :], rden[:, :], ALU.mult).then_inc(o_done, 1)
                add_bias(b)

            norm.gpsimd_setup(pool)
            pool.wait_ge(consts_loaded, 32)
            pool.memset(norm.zero[:, :], 0.0).then_inc(norm.power_set, 1)
            pool.wait_ge(norm.power_set, 2)
            for b in range(2):
                norm.gpsimd_rstd(pool, b)
                norm.gpsimd_shift(pool, b)
            first_product(0, 0)
            run(body, pool)


class LinearWeights:
    NAMES = ("wq", "wk", "wv", "wo")

    def __init__(self, nc, sem, ctx, a):
        self.nc, self.a = nc, a
        self.out = {n: tuple(ctx.enter_context(nc.sbuf_tensor(f"b_{n}_{h}", [P, D], F32R)) for h in ("hi", "lo"))
                    for n in self.NAMES}
        self.scalars = ctx.enter_context(nc.sbuf_tensor("b_scalars", [P, 8], F32))
        self.loaded, self.diff_done, self.hi_done, self.beta_done, self.minus_done = (
            sem(f"b_weights_{n}") for n in ("loaded", "diff", "hi", "beta", "minus"))

    def allocate_raw(self, local):
        def sb(name, shape):
            return local.enter_context(self.nc.sbuf_tensor(f"b_{name}", shape, F32))

        self.raw = {n: sb(f"{n}_raw", [P, D]) for n in ("wq0", "wq1", "wk0", "wk1", "wv", "wo")}
        self.diff = {n: sb(f"{n}_diff", [P, D]) for n in ("wq", "wk")}
        self.bias = {n: sb(f"{n}_raw", [P, 2]) for n in ("bq", "bk")}
        self.bias_diff = sb("bias_diff", [P, 2])
        self.beta = sb("beta", [P, 1])

    def load(self, sp):
        for n, t in self.raw.items():
            sp.dma_start(t[:, :], self.a[f"b_{n}"]).then_inc(self.loaded, 16)
        for n, t in self.bias.items():
            sp.dma_start(t[:, :], self.a[f"b_{n}"]).then_inc(self.loaded, 16)
        sp.dma_start(self.beta[:, :], self.a["b_beta"].partition_broadcast(P)).then_inc(self.loaded, 16)

    def whole(self, n):
        return (self.diff[n] if n in self.diff else self.raw[n])[:, :]

    def scalar(self, act):
        act.wait_ge(self.loaded, 9 * 16)
        act.activation(self.scalars[:, 0:1], self.beta[:, :], ACT.Exp).then_inc(self.beta_done, 1)
        act.wait_ge(self.diff_done, 1)
        for n in self.NAMES:
            last = act.copy(self.out[n][0][:, :], self.whole(n))
        last.then_inc(self.hi_done, 1)

    def vector(self, dve):
        scalars = self.scalars
        dve.wait_ge(self.loaded, 9 * 16)
        for n in self.diff:
            dve.tensor_tensor(self.diff[n][:, :], self.raw[f"{n}0"][:, :], self.raw[f"{n}1"][:, :], ALU.subtract)
        for j, n in enumerate(self.bias):
            last = dve.tensor_tensor(self.bias_diff[:, j:j + 1], self.bias[n][:, 0:1], self.bias[n][:, 1:2],
                                     ALU.subtract)
        last.then_inc(self.diff_done, 1)
        dve.wait_ge(self.diff_done, 1)
        dve.wait_ge(self.beta_done, 1)
        dve.tensor_scalar(scalars[:, 1:2], scalars[:, 0:1], -1.0, None, ALU.mult).then_inc(self.minus_done, 1)
        dve.wait_ge(self.minus_done, 1)
        for j in range(2):
            for sign in range(2):
                dve.tensor_tensor(scalars[:, 2 + 2 * j + sign:3 + 2 * j + sign], self.bias_diff[:, j:j + 1],
                                  scalars[:, sign:sign + 1], ALU.mult)
        dve.wait_ge(self.hi_done, 1)
        for n in self.NAMES:
            dve.tensor_tensor(self.out[n][1][:, :], self.whole(n), self.out[n][0][:, :].bitcast(F32), ALU.subtract)


def run_phases(nc, sem, ctx, x_all, ident, a, out):
    x_loaded = (sem("x_first_loaded"), sem("x_rest_loaded"))
    attention, ffn = ("a_wq", "a_wk", "a_wv", "a_wo"), ("gate", "up", "down")
    with ExitStack() as early:
        w, linear, stacks = setup(nc, sem, ctx, early, x_all, ident, a, ffn + attention, True, x_loaded)
        attention_phase(nc, sem, x_all, ident, *(w[n] for n in attention), a, stacks, x_loaded, "a")
    experts = (w["gate"], w["up"], w["down"], a["selector"])
    ffn_phase(nc, sem, x_all, ident, *experts, "f1")
    linear_phase(nc, sem, x_all, ident, *(linear.out[n] for n in linear.NAMES), a, linear.scalars, "b")
    ffn_phase(nc, sem, x_all, ident, *experts, "f2", out)


def setup(nc, sem, ctx, early, x_all, ident, a, split, linear, x_loaded):
    out = {}
    with ExitStack() as local:
        for name in split:
            shape = [int(n) for n in a[name].shape]
            out[name] = tuple(ctx.enter_context(nc.sbuf_tensor(f"{name}_{h}", shape, F32R)) for h in ("hi", "lo"))
        linear_weights = LinearWeights(nc, sem, ctx, a) if linear else None
        stacks = attention_stacks(nc, early) if early else None
        raws = {name: local.enter_context(nc.sbuf_tensor(f"{name}_raw", [int(n) for n in a[name].shape], F32))
                for name in split}
        if linear:
            linear_weights.allocate_raw(local)
        loaded = {name: sem(f"{name}_loaded") for name in split}
        hi_done = sem("weights_hi_done")
        zeroed = sem("identity_zeroed")
        block = local.enter_context(nc.Block())

        def whole(t):
            return t[tuple(slice(None) for _ in t.shape)]

        @block.sync
        def _(sp):
            for name in split:
                sp.dma_start(whole(raws[name]), a[name]).then_inc(loaded[name], 16)
            if linear:
                linear_weights.load(sp)
            for b in range(SEQS):
                sp.dma_start(x_all[:, b, :, :], a["x"][b].rearrange("(p c) d -> p c d", c=CH))\
                    .then_inc(x_loaded[0 if b < 2 else 1], 16)

        @block.scalar
        def _(act):
            for name in split:
                act.wait_ge(loaded[name], 16)
                act.copy(whole(out[name][0]), whole(raws[name])).then_inc(hi_done, 1)
            if linear:
                linear_weights.scalar(act)

        @block.vector
        def _(dve):
            for n, name in enumerate(split):
                dve.wait_ge(hi_done, n + 1)
                dve.tensor_tensor(whole(out[name][1]), whole(raws[name]), whole(out[name][0]).bitcast(F32),
                                  ALU.subtract)
            if linear:
                linear_weights.vector(dve)

        @block.gpsimd
        def _(pool):
            pool.memset(ident[:, :], 0.0).then_inc(zeroed, 1)
            pool.wait_ge(zeroed, 1)
            pool.affine_select(out=ident[:, :], in_=ident[:, :], compare_op=ALU.not_equal, fill=1.0, base=0,
                               pattern=[[-1, P]], channel_multiplier=1)
            if stacks:
                for q_stack, k_stack in zip(*stacks):
                    pool.memset(k_stack[:, :, :].bitcast(F32), 1.0)
                    pool.memset(q_stack[:, :, :].bitcast(F32), 0.0)
    return out, linear_weights, stacks


def program(nc, a, out):
    with ExitStack() as ctx:
        def sem(name):
            return ctx.enter_context(nc.semaphore(name))

        x_all = ctx.enter_context(nc.sbuf_tensor("x_all", [P, SEQS, CH, D], F32))
        ident = ctx.enter_context(nc.sbuf_tensor("ident", [P, P], F32))
        run_phases(nc, sem, ctx, x_all, ident, a, out)



def kernel(**inputs):
    import numpy as np
    import concourse.bacc as bacc
    from concourse.bass_utils import run_bass_kernel_spmd

    i = {name: np.asarray(value) for name, value in inputs.items()}
    heads, width = HEADS, D // HEADS

    def depth_major(w):
        return w.reshape(w.shape[:-1] + (2, heads // 2, width)).swapaxes(-1, -2).reshape(w.shape)

    w1 = i["L0_ffn_w1"].reshape(EXPERTS, D, 2, FFN).transpose(1, 0, 3, 2).reshape(D, UNITS, P, 2).swapaxes(2, 3)
    w2 = i["L0_ffn_w2"].reshape(UNITS, P, D).swapaxes(0, 1)
    selector = np.zeros((2, EXPERTS, UNITS * P), np.float32)
    for e in range(EXPERTS):
        selector[:, e, e * FFN:(e + 1) * FFN] = 1
    pair_first, pair_second = np.arange(D) // 2 * 2, np.arange(D) // 2 * 2 + 1
    laid_out = {
        "x": i["L0_attn_a_hidden_states"],
        "a_wq": depth_major(i["L0_attn_a_Wq"]), "a_bq": depth_major(i["L0_attn_a_bq"])[:, None],
        "a_wk": depth_major(i["L0_attn_a_Wk"]), "a_bk": depth_major(i["L0_attn_a_bk"])[:, None],
        "a_wv": i["L0_attn_a_Wv"], "a_bv": i["L0_attn_a_bv"][None],
        "a_wo": i["L0_attn_a_Wo"], "a_bo": i["L0_attn_a_bo"][None],
        "b_wq0": i["L0_attn_b_Wq"].T[:, pair_first], "b_wq1": i["L0_attn_b_Wq"].T[:, pair_second],
        "b_wk0": i["L0_attn_b_Wk"].T[:, pair_first], "b_wk1": i["L0_attn_b_Wk"].T[:, pair_second],
        "b_bq": np.stack([i["L0_attn_b_bq"][pair_first], i["L0_attn_b_bq"][pair_second]], 1),
        "b_bk": np.stack([i["L0_attn_b_bk"][pair_first], i["L0_attn_b_bk"][pair_second]], 1),
        "b_wv": i["L0_attn_b_Wv"].T, "b_bv": i["L0_attn_b_bv"][:, None],
        "b_wo": i["L0_attn_b_Wo"].T, "b_bo": i["L0_attn_b_bo"][None],
        "b_beta": i["L0_attn_b_beta"][None],
        "gate": i["L0_ffn_gate_w"].T,
        "up": w1, "down": w2,
        "selector": selector.reshape(2 * EXPERTS, UNITS, P),
    }
    nc = bacc.Bacc("TRN2", target_bir_lowering=False, num_devices=1)
    arrays, args = {}, {}
    for name, value in laid_out.items():
        value = np.ascontiguousarray(value)
        arrays[f"in_{name}"] = value
        args[name] = nc.dram_tensor(f"in_{name}", value.shape, F32, kind="ExternalInput").ap()
    out = nc.dram_tensor("out", (SEQS, SEQ, D), F32, kind="ExternalOutput").ap()
    program(nc, args, out)
    result = run_bass_kernel_spmd(nc, [arrays], core_ids=[0])
    return result.results[0]["out"]
```
